# Optimizing a Trainium2 kernel written in Bass

```python
import numpy as np
import jax
import jax.numpy as jnp

def _softmax(x, axis=-1):
    return jax.nn.softmax(x, axis=axis)

def _gelu(x):
    return jax.nn.gelu(x, approximate=True)

def _silu(x):
    return jax.nn.silu(x)

def _sigmoid(x):
    return jax.nn.sigmoid(x)

def _layernorm(x, axis=-1, eps=1e-05):
    m = jnp.mean(x, axis=axis, keepdims=True)
    v = jnp.var(x, axis=axis, keepdims=True)
    return (x - m) / jnp.sqrt(v + eps)

def _scatter_add(tgt, idx, src, axis=0):
    return tgt.at[idx].add(src)

def _segment_sum(src, seg, n):
    return jax.ops.segment_sum(src, seg, n)
kernel_name = 'mk_gnn_ffn_d4_gnn_r32_1fc59a'

def setup_inputs(seed: int=0):
    np.random.seed(seed)
    _w = jnp.asarray

    def _rec_inputs():
        import jax
        import jax.numpy as jnp
        _gk = jax.random.key(seed)
        x = -0.000364 + 1 * jax.random.normal(jax.random.fold_in(_gk, 1), (625, 768), jnp.float32)
        src = jax.random.randint(jax.random.fold_in(_gk, 2), (10000,), 0, 625, jnp.int32)
        dst = jnp.minimum((625 * jax.random.uniform(jax.random.fold_in(_gk, 3), (10000,)) ** 2.0).astype(jnp.int32), 19999)
        _o = jnp.argsort(dst, stable=True)
        src = src[_o]
        dst = dst[_o]
        return (x, src, dst)
    x, src, dst = _rec_inputs()

    def _L0_gnn_setup():
        import jax, jax.numpy as jnp
        import numpy as np
        N, E, DIM, HEADS = (625, 10000, 768, 8)
        HD = DIM // HEADS
        EPS = 1e-05

        def layer_norm(x, w, b):
            mu = jnp.mean(x, axis=-1, keepdims=True)
            var = jnp.var(x, axis=-1, keepdims=True)
            return (x - mu) * jax.lax.rsqrt(var + EPS) * w + b

        def gatv2(x, src, dst, Ws, bs, Wd, bd, attn):
            H, D = attn.shape
            fs = (x @ Ws + bs).reshape(-1, H, D)
            fd = (x @ Wd + bd).reshape(-1, H, D)
            e = jax.nn.leaky_relu(fs[src] + fd[dst], 0.2)
            logits = jnp.einsum('ehd,hd->eh', e, attn)
            m = jax.ops.segment_max(logits, dst, num_segments=N)
            ex = jnp.exp(logits - m[dst])
            denom = jax.ops.segment_sum(ex, dst, num_segments=N)
            alpha = ex / denom[dst]
            out = jax.ops.segment_sum(alpha[:, :, None] * fs[src], dst, num_segments=N)
            return jax.nn.elu(out)
        key = jax.random.key(seed)
        ks = jax.random.split(key, 10)
        s = 1.0 / np.sqrt(DIM)
        return {'x': jax.random.normal(ks[0], (N, DIM), jnp.float32), 'src': jax.random.randint(ks[1], (E,), 0, N, jnp.int32), 'dst': jax.random.randint(ks[2], (E,), 0, N, jnp.int32), 'W1s': jax.random.normal(ks[3], (DIM, DIM), jnp.float32) * s, 'b1s': jnp.zeros((DIM,), jnp.float32), 'W1d': jax.random.normal(ks[4], (DIM, DIM), jnp.float32) * s, 'b1d': jnp.zeros((DIM,), jnp.float32), 'attn1': jax.random.normal(ks[5], (HEADS, HD), jnp.float32) * s, 'ln1_w': jnp.ones((DIM,), jnp.float32), 'ln1_b': jnp.zeros((DIM,), jnp.float32), 'Wos': jax.random.normal(ks[6], (DIM, DIM), jnp.float32) * s, 'bos': jnp.zeros((DIM,), jnp.float32), 'Wod': jax.random.normal(ks[7], (DIM, DIM), jnp.float32) * s, 'bod': jnp.zeros((DIM,), jnp.float32), 'attno': jax.random.normal(ks[8], (1, DIM), jnp.float32) * s, 'lno_w': jnp.ones((DIM,), jnp.float32), 'lno_b': jnp.zeros((DIM,), jnp.float32)}
    _L0_gnn_all = _L0_gnn_setup()
    _L0_gnn_in = {k: v for k, v in _L0_gnn_all.items() if k in ('W1s', 'b1s', 'W1d', 'b1d', 'attn1', 'ln1_w', 'ln1_b', 'Wos', 'bos', 'Wod', 'bod', 'attno', 'lno_w', 'lno_b')}
    del _L0_gnn_all

    def _L0_ffn_setup():
        import jax, jax.numpy as jnp
        import numpy as np
        D_MODEL = 768
        KAN_HIDDEN = 64
        NUM_CP = 16
        DEGREE = 3
        RMIN, RMAX = (-4.0, 4.0)

        def bspline_basis(x, num_cp=NUM_CP, degree=DEGREE, rmin=RMIN, rmax=RMAX):
            h = (rmax - rmin) / (num_cp - degree)
            knots = rmin - degree * h + jnp.arange(num_cp + degree + 1, dtype=x.dtype) * h
            xe = x[..., None]
            b = ((xe >= knots[:-1]) & (xe < knots[1:])).astype(x.dtype)
            for d in range(1, degree + 1):
                t0 = knots[:-(d + 1)]
                t1 = knots[d:-1]
                t2 = knots[d + 1:]
                t3 = knots[1:-d]
                b = (xe - t0) / (t1 - t0) * b[..., :-1] + (t2 - xe) / (t2 - t3) * b[..., 1:]
            return b

        def kan_layer(x, w):
            basis = bspline_basis(x)
            return jnp.einsum('ndk,odk->no', basis, w)
        key = jax.random.key(seed)
        kx, k1, k2 = jax.random.split(key, 3)
        x = jax.random.normal(kx, (2, 64, D_MODEL), dtype=jnp.float32)
        w1 = jax.random.normal(k1, (KAN_HIDDEN, D_MODEL, NUM_CP), dtype=jnp.float32) * (1.0 / np.sqrt(D_MODEL * NUM_CP))
        w2 = jax.random.normal(k2, (D_MODEL, KAN_HIDDEN, NUM_CP), dtype=jnp.float32) * (1.0 / np.sqrt(KAN_HIDDEN * NUM_CP))
        return {'x': x, 'w1': w1, 'w2': w2}
    _L0_ffn_all = _L0_ffn_setup()
    _L0_ffn_in = {k: v for k, v in _L0_ffn_all.items() if k in ('w1', 'w2')}
    del _L0_ffn_all

    def _L1_gnn_setup():
        import jax, jax.numpy as jnp
        import numpy as np
        N_NODES = 10000
        N_EDGES = 2500
        IN_DIM, HID, OUT_DIM, HEADS = (768, 512, 768, 4)
        NEG_SLOPE = 0.2

        def _gat_layer(x, src, dst, W, a_src, a_dst, b, heads, d_out, concat):
            N = x.shape[0]
            h = (x @ W).reshape(N, heads, d_out)
            as_n = jnp.einsum('nhd,hd->nh', h, a_src)
            ad_n = jnp.einsum('nhd,hd->nh', h, a_dst)
            e = jax.nn.leaky_relu(as_n[src] + ad_n[dst], NEG_SLOPE)
            e_max = jax.lax.stop_gradient(jax.ops.segment_max(e, dst, num_segments=N))
            ex = jnp.exp(e - e_max[dst])
            denom = jax.ops.segment_sum(ex, dst, num_segments=N)
            alpha = ex / (denom[dst] + 1e-16)
            msg = alpha[:, :, None] * h[src]
            out = jax.ops.segment_sum(msg, dst, num_segments=N)
            out = out.reshape(N, heads * d_out) if concat else out.mean(axis=1)
            return out + b
        key = jax.random.key(seed)
        ks = jax.random.split(key, 10)
        g = 0.05
        return {'x': jax.random.normal(ks[0], (N_NODES, IN_DIM), jnp.float32), 'edge_index': jax.random.randint(ks[1], (2, N_EDGES), 0, N_NODES, jnp.int64), 'W1': jax.random.normal(ks[2], (IN_DIM, HEADS * HID), jnp.float32) * g, 'a1_src': jax.random.normal(ks[3], (HEADS, HID), jnp.float32) * g, 'a1_dst': jax.random.normal(ks[4], (HEADS, HID), jnp.float32) * g, 'b1': jnp.zeros((HEADS * HID,), jnp.float32), 'W2': jax.random.normal(ks[5], (HEADS * HID, OUT_DIM), jnp.float32) * g, 'a2_src': jax.random.normal(ks[6], (1, OUT_DIM), jnp.float32) * g, 'a2_dst': jax.random.normal(ks[7], (1, OUT_DIM), jnp.float32) * g, 'b2': jnp.zeros((OUT_DIM,), jnp.float32)}
    _L1_gnn_all = _L1_gnn_setup()
    _L1_gnn_in = {k: v for k, v in _L1_gnn_all.items() if k in ('W1', 'a1_src', 'a1_dst', 'b1', 'W2', 'a2_src', 'a2_dst', 'b2')}
    del _L1_gnn_all

    def _L1_ffn_setup():
        import jax, jax.numpy as jnp
        import numpy as np
        B, S, D = (2, 64, 768)
        E, K, F = (8, 2, 1536)

        def _swiglu(xf, wg, wu, wd):
            return jax.nn.silu(xf @ wg.T) * (xf @ wu.T) @ wd.T
        key = jax.random.key(seed)
        ks = jax.random.split(key, 9)
        scale = 0.02
        x = jax.random.normal(ks[0], (B, S, D), dtype=jnp.float32)
        w_router = jax.random.normal(ks[1], (E, D), dtype=jnp.float32) * scale
        expert_bias = jnp.zeros((E,), dtype=jnp.float32)
        Wg = jax.random.normal(ks[2], (E, F, D), dtype=jnp.float32) * scale
        Wu = jax.random.normal(ks[3], (E, F, D), dtype=jnp.float32) * scale
        Wd = jax.random.normal(ks[4], (E, D, F), dtype=jnp.float32) * scale
        sg = jax.random.normal(ks[5], (F, D), dtype=jnp.float32) * scale
        su = jax.random.normal(ks[6], (F, D), dtype=jnp.float32) * scale
        sd = jax.random.normal(ks[7], (D, F), dtype=jnp.float32) * scale
        return {'x': x, 'w_router': w_router, 'expert_bias': expert_bias, 'Wg': Wg, 'Wu': Wu, 'Wd': Wd, 'sg': sg, 'su': su, 'sd': sd}
    _L1_ffn_all = _L1_ffn_setup()
    _L1_ffn_in = {k: v for k, v in _L1_ffn_all.items() if k in ('w_router', 'expert_bias', 'Wg', 'Wu', 'Wd', 'sg', 'su', 'sd')}
    del _L1_ffn_all

    def _L2_gnn_setup():
        import jax, jax.numpy as jnp
        import numpy as np
        N_NODES = 10000
        D = 768
        N_EDGES = 5000

        def gcn_conv(x, W, b, src, dst, n_nodes):
            h = x @ W
            deg = jax.ops.segment_sum(jnp.ones_like(dst, dtype=h.dtype), dst, num_segments=n_nodes)
            dinv = jnp.where(deg > 0, jax.lax.rsqrt(deg), 0.0)
            norm = dinv[src] * dinv[dst]
            msgs = h[src] * norm[:, None]
            out = jax.ops.segment_sum(msgs, dst, num_segments=n_nodes)
            return out + b

        def add_self_loops(edge_index, n_nodes):
            loop = jnp.arange(n_nodes, dtype=edge_index.dtype)
            src = jnp.concatenate([edge_index[0], loop])
            dst = jnp.concatenate([edge_index[1], loop])
            return (src, dst)
        key = jax.random.key(seed)
        k1, k2, k3, k4 = jax.random.split(key, 4)
        x = jax.random.normal(k1, (N_NODES, D), dtype=jnp.float32)
        edge_index = jax.random.randint(k2, (2, N_EDGES), 0, N_NODES, dtype=jnp.int32)
        glorot = float(np.sqrt(6.0 / (D + D)))
        W1 = jax.random.uniform(k3, (D, D), jnp.float32, -glorot, glorot)
        W2 = jax.random.uniform(k4, (D, D), jnp.float32, -glorot, glorot)
        b1 = jnp.zeros((D,), jnp.float32)
        b2 = jnp.zeros((D,), jnp.float32)
        return {'x': x, 'W1': W1, 'b1': b1, 'W2': W2, 'b2': b2, 'edge_index': edge_index}
    _L2_gnn_all = _L2_gnn_setup()
    _L2_gnn_in = {k: v for k, v in _L2_gnn_all.items() if k in ('W1', 'b1', 'W2', 'b2')}
    del _L2_gnn_all

    def _L2_ffn_setup():
        import jax, jax.numpy as jnp
        import numpy as np
        key = jax.random.key(seed)
        k1, k2 = jax.random.split(key)
        B, S, D_IN, D_OUT = (4, 256, 768, 768)
        x = jax.random.normal(k1, (B, S, D_IN), dtype=jnp.float32)
        weight = jax.random.normal(k2, (D_OUT, D_IN), dtype=jnp.float32) * (1.0 / jnp.sqrt(D_OUT))
        return {'x': x, 'weight': weight}
    _L2_ffn_all = _L2_ffn_setup()
    _L2_ffn_in = {k: v for k, v in _L2_ffn_all.items() if k in ('weight',)}
    del _L2_ffn_all

    def _L3_gnn_setup():
        import jax, jax.numpy as jnp
        import numpy as np
        N = 625
        DEG = 16
        E = N * DEG
        H = 12
        DIN = 64
        DOUT = 64
        NEG_SLOPE = 0.2
        key = jax.random.key(seed)
        k_h, k_src, k_w, k_al, k_ar, k_wr = jax.random.split(key, 6)
        std = 1.414 * np.sqrt(2.0 / (DIN + DOUT))
        h = jax.random.normal(k_h, (N, H * DIN), dtype=jnp.float32)
        src = jax.random.randint(k_src, (E,), 0, N, dtype=jnp.int64)
        dst = jnp.repeat(jnp.arange(N, dtype=jnp.int64), DEG)
        W = jax.random.normal(k_w, (DOUT, DIN), dtype=jnp.float32) * std
        attn_l = jax.random.normal(k_al, (1, H, DOUT), dtype=jnp.float32) * std
        attn_r = jax.random.normal(k_ar, (1, H, DOUT), dtype=jnp.float32) * std
        W_res = jax.random.normal(k_wr, (DOUT, DIN), dtype=jnp.float32) * std
        return {'h': h, 'src': src, 'dst': dst, 'W': W, 'attn_l': attn_l, 'attn_r': attn_r, 'W_res': W_res}
    _L3_gnn_all = _L3_gnn_setup()
    _L3_gnn_in = {k: v for k, v in _L3_gnn_all.items() if k in ('W', 'attn_l', 'attn_r', 'W_res')}
    del _L3_gnn_all

    def _L3_ffn_setup():
        import jax, jax.numpy as jnp
        import numpy as np
        B, S, D, F, E = (2, 1024, 768, 96, 8)
        key = jax.random.key(seed)
        k0, k1, k2, k3, k4, k5 = jax.random.split(key, 6)
        scale = 0.02
        return {'hidden_states': jax.random.normal(k0, (B, S, D), dtype=jnp.float32), 'Wg': jax.random.normal(k1, (D, E), dtype=jnp.float32) * scale, 'W1': jax.random.normal(k2, (E, D, F), dtype=jnp.float32) * scale, 'b1': jnp.zeros((E, F), dtype=jnp.float32), 'W2': jax.random.normal(k3, (E, F, D), dtype=jnp.float32) * scale, 'b2': jnp.zeros((E, D), dtype=jnp.float32)}
    _L3_ffn_all = _L3_ffn_setup()
    _L3_ffn_in = {k: v for k, v in _L3_ffn_all.items() if k in ('Wg', 'W1', 'b1', 'W2', 'b2')}
    del _L3_ffn_all
    return {'x': x, 'src': src, 'dst': dst, 'L0_gnn_W1s': _L0_gnn_in['W1s'], 'L0_gnn_b1s': _L0_gnn_in['b1s'], 'L0_gnn_W1d': _L0_gnn_in['W1d'], 'L0_gnn_b1d': _L0_gnn_in['b1d'], 'L0_gnn_attn1': _L0_gnn_in['attn1'], 'L0_gnn_ln1_w': _L0_gnn_in['ln1_w'], 'L0_gnn_ln1_b': _L0_gnn_in['ln1_b'], 'L0_gnn_Wos': _L0_gnn_in['Wos'], 'L0_gnn_bos': _L0_gnn_in['bos'], 'L0_gnn_Wod': _L0_gnn_in['Wod'], 'L0_gnn_bod': _L0_gnn_in['bod'], 'L0_gnn_attno': _L0_gnn_in['attno'], 'L0_gnn_lno_w': _L0_gnn_in['lno_w'], 'L0_gnn_lno_b': _L0_gnn_in['lno_b'], 'L0_ffn_w1': _L0_ffn_in['w1'], 'L0_ffn_w2': _L0_ffn_in['w2'], 'L1_gnn_W1': _L1_gnn_in['W1'], 'L1_gnn_a1_src': _L1_gnn_in['a1_src'], 'L1_gnn_a1_dst': _L1_gnn_in['a1_dst'], 'L1_gnn_b1': _L1_gnn_in['b1'], 'L1_gnn_W2': _L1_gnn_in['W2'], 'L1_gnn_a2_src': _L1_gnn_in['a2_src'], 'L1_gnn_a2_dst': _L1_gnn_in['a2_dst'], 'L1_gnn_b2': _L1_gnn_in['b2'], 'L1_ffn_w_router': _L1_ffn_in['w_router'], 'L1_ffn_expert_bias': _L1_ffn_in['expert_bias'], 'L1_ffn_Wg': _L1_ffn_in['Wg'], 'L1_ffn_Wu': _L1_ffn_in['Wu'], 'L1_ffn_Wd': _L1_ffn_in['Wd'], 'L1_ffn_sg': _L1_ffn_in['sg'], 'L1_ffn_su': _L1_ffn_in['su'], 'L1_ffn_sd': _L1_ffn_in['sd'], 'L2_gnn_W1': _L2_gnn_in['W1'], 'L2_gnn_b1': _L2_gnn_in['b1'], 'L2_gnn_W2': _L2_gnn_in['W2'], 'L2_gnn_b2': _L2_gnn_in['b2'], 'L2_ffn_weight': _L2_ffn_in['weight'], 'L3_gnn_W': _L3_gnn_in['W'], 'L3_gnn_attn_l': _L3_gnn_in['attn_l'], 'L3_gnn_attn_r': _L3_gnn_in['attn_r'], 'L3_gnn_W_res': _L3_gnn_in['W_res'], 'L3_ffn_Wg': _L3_ffn_in['Wg'], 'L3_ffn_W1': _L3_ffn_in['W1'], 'L3_ffn_b1': _L3_ffn_in['b1'], 'L3_ffn_W2': _L3_ffn_in['W2'], 'L3_ffn_b2': _L3_ffn_in['b2']}

def reference(x, src, dst, L0_gnn_W1s, L0_gnn_b1s, L0_gnn_W1d, L0_gnn_b1d, L0_gnn_attn1, L0_gnn_ln1_w, L0_gnn_ln1_b, L0_gnn_Wos, L0_gnn_bos, L0_gnn_Wod, L0_gnn_bod, L0_gnn_attno, L0_gnn_lno_w, L0_gnn_lno_b, L0_ffn_w1, L0_ffn_w2, L1_gnn_W1, L1_gnn_a1_src, L1_gnn_a1_dst, L1_gnn_b1, L1_gnn_W2, L1_gnn_a2_src, L1_gnn_a2_dst, L1_gnn_b2, L1_ffn_w_router, L1_ffn_expert_bias, L1_ffn_Wg, L1_ffn_Wu, L1_ffn_Wd, L1_ffn_sg, L1_ffn_su, L1_ffn_sd, L2_gnn_W1, L2_gnn_b1, L2_gnn_W2, L2_gnn_b2, L2_ffn_weight, L3_gnn_W, L3_gnn_attn_l, L3_gnn_attn_r, L3_gnn_W_res, L3_ffn_Wg, L3_ffn_W1, L3_ffn_b1, L3_ffn_W2, L3_ffn_b2):
    import jax
    import jax.numpy as jnp

    def _L0_gnn_ref(x, src, dst, W1s, b1s, W1d, b1d, attn1, ln1_w, ln1_b, Wos, bos, Wod, bod, attno, lno_w, lno_b):
        import jax, jax.numpy as jnp
        import numpy as np
        N, E, DIM, HEADS = (625, 10000, 768, 8)
        HD = DIM // HEADS
        EPS = 1e-05

        def layer_norm(x, w, b):
            mu = jnp.mean(x, axis=-1, keepdims=True)
            var = jnp.var(x, axis=-1, keepdims=True)
            return (x - mu) * jax.lax.rsqrt(var + EPS) * w + b

        def gatv2(x, src, dst, Ws, bs, Wd, bd, attn):
            H, D = attn.shape
            fs = (x @ Ws + bs).reshape(-1, H, D)
            fd = (x @ Wd + bd).reshape(-1, H, D)
            e = jax.nn.leaky_relu(fs[src] + fd[dst], 0.2)
            logits = jnp.einsum('ehd,hd->eh', e, attn)
            m = jax.ops.segment_max(logits, dst, num_segments=N)
            ex = jnp.exp(logits - m[dst])
            denom = jax.ops.segment_sum(ex, dst, num_segments=N)
            alpha = ex / denom[dst]
            out = jax.ops.segment_sum(alpha[:, :, None] * fs[src], dst, num_segments=N)
            return jax.nn.elu(out)
        h = gatv2(x, src, dst, W1s, b1s, W1d, b1d, attn1).reshape(N, DIM)
        h = layer_norm(h + x, ln1_w, ln1_b)
        out = gatv2(h, src, dst, Wos, bos, Wod, bod, attno).reshape(N, DIM)
        return layer_norm(out, lno_w, lno_b)

    def _L0_ffn_ref(x, w1, w2):
        import jax, jax.numpy as jnp
        import numpy as np
        D_MODEL = 768
        KAN_HIDDEN = 64
        NUM_CP = 16
        DEGREE = 3
        RMIN, RMAX = (-4.0, 4.0)

        def bspline_basis(x, num_cp=NUM_CP, degree=DEGREE, rmin=RMIN, rmax=RMAX):
            h = (rmax - rmin) / (num_cp - degree)
            knots = rmin - degree * h + jnp.arange(num_cp + degree + 1, dtype=x.dtype) * h
            xe = x[..., None]
            b = ((xe >= knots[:-1]) & (xe < knots[1:])).astype(x.dtype)
            for d in range(1, degree + 1):
                t0 = knots[:-(d + 1)]
                t1 = knots[d:-1]
                t2 = knots[d + 1:]
                t3 = knots[1:-d]
                b = (xe - t0) / (t1 - t0) * b[..., :-1] + (t2 - xe) / (t2 - t3) * b[..., 1:]
            return b

        def kan_layer(x, w):
            basis = bspline_basis(x)
            return jnp.einsum('ndk,odk->no', basis, w)
        B, T, D = x.shape
        input_dtype = x.dtype
        h = x.reshape(B * T, D).astype(jnp.float32)
        h = kan_layer(h, w1)
        h = kan_layer(h, w2)
        h = h.astype(input_dtype)
        return h.reshape(B, T, -1)

    def _L1_gnn_ref(x, edge_index, W1, a1_src, a1_dst, b1, W2, a2_src, a2_dst, b2):
        import jax, jax.numpy as jnp
        import numpy as np
        N_NODES = 10000
        N_EDGES = 2500
        IN_DIM, HID, OUT_DIM, HEADS = (768, 512, 768, 4)
        NEG_SLOPE = 0.2

        def _gat_layer(x, src, dst, W, a_src, a_dst, b, heads, d_out, concat):
            N = x.shape[0]
            h = (x @ W).reshape(N, heads, d_out)
            as_n = jnp.einsum('nhd,hd->nh', h, a_src)
            ad_n = jnp.einsum('nhd,hd->nh', h, a_dst)
            e = jax.nn.leaky_relu(as_n[src] + ad_n[dst], NEG_SLOPE)
            e_max = jax.lax.stop_gradient(jax.ops.segment_max(e, dst, num_segments=N))
            ex = jnp.exp(e - e_max[dst])
            denom = jax.ops.segment_sum(ex, dst, num_segments=N)
            alpha = ex / (denom[dst] + 1e-16)
            msg = alpha[:, :, None] * h[src]
            out = jax.ops.segment_sum(msg, dst, num_segments=N)
            out = out.reshape(N, heads * d_out) if concat else out.mean(axis=1)
            return out + b
        N = x.shape[0]
        loops = jnp.arange(N, dtype=edge_index.dtype)
        src = jnp.concatenate([edge_index[0], loops])
        dst = jnp.concatenate([edge_index[1], loops])
        h = _gat_layer(x, src, dst, W1, a1_src, a1_dst, b1, HEADS, HID, True)
        h = jax.nn.elu(h)
        out = _gat_layer(h, src, dst, W2, a2_src, a2_dst, b2, 1, OUT_DIM, False)
        return out

    def _L1_ffn_ref(x, w_router, expert_bias, Wg, Wu, Wd, sg, su, sd):
        import jax, jax.numpy as jnp
        import numpy as np
        B, S, D = (2, 64, 768)
        E, K, F = (8, 2, 1536)

        def _swiglu(xf, wg, wu, wd):
            return jax.nn.silu(xf @ wg.T) * (xf @ wu.T) @ wd.T
        b, s, d = x.shape
        xf = x.reshape(-1, d)
        T = xf.shape[0]
        e = w_router.shape[0]
        logits = xf @ w_router.T
        scores = jax.nn.softmax(logits, axis=-1)
        selection = scores + expert_bias[None, :]
        _, top_idx = jax.lax.top_k(selection, K)
        top_s = jnp.take_along_axis(scores, top_idx, axis=-1)
        top_s = top_s / (jnp.sum(top_s, axis=-1, keepdims=True) + 1e-09)
        comb = jnp.zeros((T, e), dtype=x.dtype).at[jnp.arange(T)[:, None], top_idx].add(top_s)

        def body(acc, p):
            wg, wu, wd, c = p
            return (acc + c[:, None] * _swiglu(xf, wg, wu, wd), None)
        routed, _ = jax.lax.scan(body, jnp.zeros_like(xf), (Wg, Wu, Wd, comb.T))
        out = routed + _swiglu(xf, sg, su, sd)
        return out.reshape(b, s, d)

    def _L2_gnn_ref(x, W1, b1, W2, b2, edge_index):
        import jax, jax.numpy as jnp
        import numpy as np
        N_NODES = 10000
        D = 768
        N_EDGES = 5000

        def gcn_conv(x, W, b, src, dst, n_nodes):
            h = x @ W
            deg = jax.ops.segment_sum(jnp.ones_like(dst, dtype=h.dtype), dst, num_segments=n_nodes)
            dinv = jnp.where(deg > 0, jax.lax.rsqrt(deg), 0.0)
            norm = dinv[src] * dinv[dst]
            msgs = h[src] * norm[:, None]
            out = jax.ops.segment_sum(msgs, dst, num_segments=n_nodes)
            return out + b

        def add_self_loops(edge_index, n_nodes):
            loop = jnp.arange(n_nodes, dtype=edge_index.dtype)
            src = jnp.concatenate([edge_index[0], loop])
            dst = jnp.concatenate([edge_index[1], loop])
            return (src, dst)
        n = x.shape[0]
        src, dst = add_self_loops(edge_index, n)
        h = gcn_conv(x, W1, b1, src, dst, n)
        h = jax.nn.relu(h)
        out = gcn_conv(h, W2, b2, src, dst, n)
        return out

    def _L2_ffn_ref(x, weight):
        import jax, jax.numpy as jnp
        import numpy as np
        w_bin = jnp.sign(weight)
        return jnp.einsum('bsi,oi->bso', x, w_bin)

    def _L3_gnn_ref(h, src, dst, W, attn_l, attn_r, W_res):
        import jax, jax.numpy as jnp
        import numpy as np
        N = 625
        DEG = 16
        E = N * DEG
        H = 12
        DIN = 64
        DOUT = 64
        NEG_SLOPE = 0.2
        n = h.shape[0]
        hv = h.reshape(n, H, DIN)
        ft = jnp.einsum('nhd,od->nho', hv, W)
        a1 = jnp.sum(ft * attn_l, axis=-1)
        a2 = jnp.sum(ft * attn_r, axis=-1)
        e = jax.nn.leaky_relu(a1[src] + a2[dst], negative_slope=NEG_SLOPE)
        m = jax.ops.segment_max(e, dst, num_segments=n)
        m = jnp.where(jnp.isfinite(m), m, 0.0)
        w = jnp.exp(e - m[dst])
        denom = jax.ops.segment_sum(w, dst, num_segments=n)
        alpha = w / jnp.maximum(denom[dst], 1e-16)
        msg = alpha[:, :, None] * ft[src]
        agg = jax.ops.segment_sum(msg, dst, num_segments=n)
        res = jnp.einsum('nhd,od->nho', hv, W_res)
        out = jax.nn.relu((agg + res).reshape(n, H * DOUT))
        return out

    def _L3_ffn_ref(hidden_states, Wg, W1, b1, W2, b2):
        import jax, jax.numpy as jnp
        import numpy as np
        B, S, D, F, E = (2, 1024, 768, 96, 8)
        b, s, d = hidden_states.shape
        e = W1.shape[0]
        x = hidden_states.reshape(-1, d)
        logits = x @ Wg
        probs = jax.nn.softmax(logits, axis=-1)
        gate = jnp.max(probs, axis=-1)
        expert_idx = jnp.argmax(probs, axis=-1)
        h = jax.nn.silu(jnp.einsum('td,edf->etf', x, W1) + b1[:, None, :])
        y = jnp.einsum('etf,efd->etd', h, W2) + b2[:, None, :]
        combine = jax.nn.one_hot(expert_idx, e, dtype=x.dtype) * gate[:, None]
        out = jnp.einsum('te,etd->td', combine, y)
        return out.reshape(b, s, d)
    edge_index = jnp.stack([src, dst])
    x = x + _L0_gnn_ref(_layernorm(x, axis=-1), src, dst, L0_gnn_W1s, L0_gnn_b1s, L0_gnn_W1d, L0_gnn_b1d, L0_gnn_attn1, L0_gnn_ln1_w, L0_gnn_ln1_b, L0_gnn_Wos, L0_gnn_bos, L0_gnn_Wod, L0_gnn_bod, L0_gnn_attno, L0_gnn_lno_w, L0_gnn_lno_b)
    x = x + _L0_ffn_ref(_layernorm(x, axis=-1)[None], L0_ffn_w1, L0_ffn_w2)[0]
    x = x + _L1_gnn_ref(_layernorm(x, axis=-1), edge_index, L1_gnn_W1, L1_gnn_a1_src, L1_gnn_a1_dst, L1_gnn_b1, L1_gnn_W2, L1_gnn_a2_src, L1_gnn_a2_dst, L1_gnn_b2)
    x = x + _L1_ffn_ref(_layernorm(x, axis=-1)[None], L1_ffn_w_router, L1_ffn_expert_bias, L1_ffn_Wg, L1_ffn_Wu, L1_ffn_Wd, L1_ffn_sg, L1_ffn_su, L1_ffn_sd)[0]
    x = x + _L2_gnn_ref(_layernorm(x, axis=-1), L2_gnn_W1, L2_gnn_b1, L2_gnn_W2, L2_gnn_b2, edge_index)
    x = x + _L2_ffn_ref(_layernorm(x, axis=-1)[None], L2_ffn_weight)[0]
    x = x + _L3_gnn_ref(_layernorm(x, axis=-1), src, dst, L3_gnn_W, L3_gnn_attn_l, L3_gnn_attn_r, L3_gnn_W_res)
    x = x + _L3_ffn_ref(_layernorm(x, axis=-1)[None], L3_ffn_Wg, L3_ffn_W1, L3_ffn_b1, L3_ffn_W2, L3_ffn_b2)[0]
    return x

_drawn_inputs = setup_inputs


def setup_inputs(seed=0):
    import zlib

    import numpy as np

    out = dict(_drawn_inputs(seed))
    spreads = {'L0_gnn_b1s': (0.0, 0.1),
     'L0_gnn_b1d': (0.0, 2.0),
     'L0_gnn_ln1_w': (1.0, 0.2),
     'L0_gnn_ln1_b': (0.0, 0.1),
     'L0_gnn_bos': (0.0, 0.1),
     'L0_gnn_bod': (0.0, 0.476),
     'L0_gnn_lno_w': (1.0, 0.2),
     'L0_gnn_lno_b': (0.0, 0.1),
     'L1_gnn_b1': (0.0, 0.1),
     'L1_gnn_b2': (0.0, 0.1),
     'L1_ffn_expert_bias': (0.0, 0.1),
     'L2_gnn_b1': (0.0, 0.1),
     'L2_gnn_b2': (0.0, 0.1),
     'L3_ffn_b1': (0.0, 2.0),
     'L3_ffn_b2': (0.0, 2.0)}
    factors = {'L0_gnn_W1d': 2.794,
     'L3_gnn_attn_l': 3.995,
     'L3_gnn_attn_r': 40.748,
     'L3_ffn_Wg': 8.0,
     'L3_ffn_W1': 8.0,
     'L3_ffn_W2': 8.0}
    for name, (base, spread) in spreads.items():
        noise = np.random.default_rng([zlib.crc32(name.encode()), seed]).standard_normal(out[name].shape)
        drawn = base * np.exp(spread * noise) if base else spread * noise
        out[name] = jnp.asarray(drawn.astype(out[name].dtype))
    for name, factor in factors.items():
        out[name] = (out[name] * factor).astype(out[name].dtype)
    return out
```

```python
from contextlib import ExitStack

import concourse.bass as bass
from concourse import mybir

ALU = mybir.AluOpType
ACT = mybir.ActivationFunctionType
AX = mybir.AxisListType.X
F32 = mybir.dt.float32
BF16 = mybir.dt.bfloat16
I32 = mybir.dt.int32

N = 625
P = 125
T = N // P
D = 768
C = D // 128
HALF = D // 2
E = 10000
ET = E // P
RING = 3
SLAB = C * D
NEG = -1.0e30
EPS = 1e-5
SLOPE = 0.2
NCP = 16
KH = 64
KG = 4
H_L0, H_L1, H_L3 = 8, 4, 12
HID1 = 512
FF, FFC, EXPERTS = 1536, 12, 8
F3 = 96


class Count:

    def __init__(self, sem):
        self.sem, self.n = sem, 0

    def mark(self, ins):
        ins.then_inc(self.sem, 1)
        self.n += 1
        return self.n

    def mark_dma(self, ins):
        ins.then_inc(self.sem, 16)
        self.n += 16
        return self.n


def wait(eng, count, value):
    if value > 0:
        eng.wait_ge(count.sem, value)


def step(eng, count, ins):
    eng.wait_ge(count.sem, count.mark(ins))


class Kit:

    def __init__(self, nc, ctx, a):
        self.nc, self.a = nc, a

        def sb(name, shape, dt=F32):
            return ctx.enter_context(nc.sbuf_tensor(name, shape, dt))

        def count(name):
            return Count(ctx.enter_context(nc.semaphore(name)))

        self.x = sb("x", [P, T, D])
        self.xn = sb("xn", [P, T, D])
        self.xT = sb("xT", [128, C, N])
        self.ring = sb("ring", [128, RING, SLAB])
        self.cT = sb("cT", [P, T, N])
        self.neg = sb("neg", [P, T, N])
        self.deg = sb("deg", [P, T])
        self.key = sb("key", [P, ET], I32)
        self.srci = sb("srci", [P, ET], I32)
        self.dsti = sb("dsti", [P, ET], I32)
        self.ident = sb("ident", [128, 128])
        self.ones = sb("ones", [128, 128])
        self.kcol = sb("kcol", [128, NCP])
        self.kcol2 = sb("kcol2", [128, NCP // 2])
        self.two = sb("two", [128, 1])
        self.eps = sb("eps", [128, 1])
        self.arena_words = 20700
        self.arena = sb("arena", [128, self.arena_words])
        self.ps = ctx.enter_context(nc.psum_tensor("ps", [128, 4, 1024], F32))

        self.filled = count("psum_filled")
        self.emptied = count("psum_emptied")
        self.var_ready = count("var_ready")
        self.std_ready = count("std_ready")
        self.dve_step = count("dve_step")
        self.act_step = count("act_step")
        self.pool_step = count("pool_step")
        self.pe_step = count("pe_step")
        self.act_ready = count("act_ready")
        self.dve_ready = count("dve_ready")
        self.dve_for_pe = count("dve_for_pe")
        self.act_for_pe = count("act_for_pe")
        self.params_in = count("params_in")
        self.stored = count("stored")
        self.slab_in = [count(f"slab_in{i}") for i in range(RING)]
        self.slab_free = count("slab_free")
        self.gathered = [count(f"gathered{i}") for i in range(4)]
        self.scattered = count("scattered")
        self.logits_ready = count("logits_ready")
        self.dense_in = [count(f"dense_in{i}") for i in range(2)]

        self.slabs, self.issued, self.used = [], 0, 0
        self.fs_d = nc.dram_tensor("fs_rows", (N, D), F32, kind="Internal").ap()
        self.fd_d = nc.dram_tensor("fd_rows", (N, D), F32, kind="Internal").ap()
        self.dense = {8: nc.dram_tensor("dense_logits8", (N * N, 8), F32, kind="Internal").ap(),
                      1: nc.dram_tensor("dense_logits1", (N * N, 1), F32, kind="Internal").ap()}

    def reset(self, keep=0):
        self.at = keep

    def carve(self, parts, *shape):
        n = 1
        for s in shape:
            n *= s
        v = self.arena[0:parts, self.at:self.at + n]
        self.at += n
        assert self.at <= self.arena_words, self.at
        if len(shape) == 2:
            v = v.rearrange("p (a b) -> p a b", a=shape[0])
        elif len(shape) == 3:
            v = v.rearrange("p (a b c) -> p a b c", a=shape[0], b=shape[1])
        return v

    def feed(self, sp, uses):
        self.will_use = self.used_before + uses
        while self.issued < min(len(self.slabs), self.will_use + RING - 1):
            i = self.issued
            src, parts, words = self.slabs[i]
            if i >= RING:
                sp.wait_ge(self.slab_free.sem, i - RING + 1)
            dst = self.ring[0:parts, i % RING, 0:words]
            self.slab_in[i % RING].mark_dma(sp.dma_start(dst, src))
            self.issued += 1
        self.used_before += uses

    def slab(self, eng, n=0):
        i = self.used + n
        eng.wait_ge(self.slab_in[i % RING].sem, 16 * (i // RING + 1))
        return self.ring[:, i % RING, :]

    def release(self, ins):
        self.slab_free.mark(ins)
        self.used += 1


def plan_slabs(k):
    a = k.a

    def add(ap, parts=128):
        k.slabs.append((ap, parts, ap.shape[1]))

    for w in ("L0_gnn_W1s", "L0_gnn_W1d", "L0_gnn_Wos", "L0_gnn_Wod"):
        add(a[w])
    for h in range(2):
        add(a["L0_ffn_w1"][:, h * 48 * KH:(h + 1) * 48 * KH])
    for h in range(2):
        add(a["L0_ffn_w2"][:, h * 4 * D:(h + 1) * 4 * D])
    for h in range(H_L1):
        add(a["L1_gnn_W1"][:, h * C * HID1:(h + 1) * C * HID1])
    for c0, c1 in ((0, 6), (6, 12), (12, 16)):
        add(a["L1_gnn_W2"][:, c0 * D:c1 * D])
    for e in range(EXPERTS + 1):
        for half in range(2):
            for w in (("L1_ffn_sg", "L1_ffn_su", "L1_ffn_sd") if e == EXPERTS else ("L1_ffn_Wg", "L1_ffn_Wu", "L1_ffn_Wd")):
                add(a[w][:, half * SLAB:(half + 1) * SLAB] if e == EXPERTS else a[w][e][:, half * SLAB:(half + 1) * SLAB])
    for w in ("L2_gnn_W1", "L2_gnn_W2", "L2_ffn_weight", "L3_ffn_W1"):
        add(a[w])
    for h in range(2):
        add(a["L3_ffn_W2"][:, h * 4 * D:(h + 1) * 4 * D], F3)
    k.used_before = 0


def halves(ap):
    return ap.rearrange("p (b f) -> p b f", b=2)[:, :, 0:HALF]


def wide(ap):
    return ap.rearrange("p (b f) -> p b f", b=2)


def tiles(ap):
    return ap.rearrange("p (t c) -> p t c", c=128)[:, 0:T, 0:P]


def graph_stage(k):
    nc, a = k.nc, k.a
    k.reset()
    iota = k.carve(P, N)
    fill = k.carve(P, 5000)
    srcf = k.carve(P, ET)
    dstf = k.carve(P, ET)
    keyf = k.carve(P, ET)
    hot = k.carve(P, 2 * 3 * N // 2 + 3).bitcast(BF16)
    hot = hot[:, 0:6 * N].rearrange("p (s w n) -> p s w n", s=3, w=2)
    filled0, emptied0 = k.filled.n, k.emptied.n
    ready0, pe0, st0, pool0 = k.dve_for_pe.n, k.pe_step.n, k.stored.n, k.pool_step.n
    dve0 = k.dve_ready.n
    counts_in = []
    with nc.Block() as block:
        @block.sync
        def _(sp):
            k.params_in.mark_dma(sp.dma_start(k.srci[:, :], a["src"].rearrange("(p t) -> p t", t=ET)))
            k.params_in.mark_dma(sp.dma_start(k.dsti[:, :], a["dst"].rearrange("(p t) -> p t", t=ET)))
            k.params_in.mark_dma(sp.dma_start(k.x[:, :, :], a["x"].rearrange("(t p) d -> p t d", p=P)))
            k.feed(sp, 0)
            sp.wait_ge(k.dve_ready.sem, dve0 + 1)
            table = k.dense[8].rearrange("(k p c) h -> k p (c h)", p=P, k=25)
            for i in range(25):
                k.stored.mark_dma(sp.dma_start(table[i], fill[:, 0:1000]))
            k.stored.mark_dma(sp.dma_start(k.dense[1].rearrange("(p c) h -> p (c h)", p=P), fill[:, 0:N * T]))
            sp.wait_ge(k.params_in.sem, k.params_in.n)
            sp.wait_ge(k.stored.sem, k.stored.n)

        @block.gpsimd
        def _(pool):
            step(pool, k.pool_step, pool.iota(iota[:, :], [[1, N]], base=0, channel_multiplier=0,
                                       allow_small_or_imprecise_dtypes=True))
            step(pool, k.pool_step, pool.memset(k.ident[:, :], 0.0))
            step(pool, k.pool_step, pool.affine_select(out=k.ident[:, :], in_=k.ident[:, :], compare_op=ALU.not_equal,
                                                fill=1.0, base=0, pattern=[[-1, 128]], channel_multiplier=1))
            step(pool, k.pool_step, pool.memset(k.ones[:, :], 1.0))
            step(pool, k.pool_step, pool.iota(k.kcol[:, :], [[-1, NCP]], base=-2, channel_multiplier=0,
                                       allow_small_or_imprecise_dtypes=True))
            step(pool, k.pool_step, pool.iota(k.kcol2[0:64, :], [[-2, NCP // 2]], base=-2, channel_multiplier=0,
                                       allow_small_or_imprecise_dtypes=True))
            step(pool, k.pool_step, pool.iota(k.kcol2[64:128, :], [[-2, NCP // 2]], base=-3, channel_multiplier=0,
                                       allow_small_or_imprecise_dtypes=True))

        @block.vector
        def _(dve):
            k.dve_ready.mark(dve.memset(fill, NEG))
            k.dve_step.mark(dve.memset(k.two[:, :], 2.0))
            k.dve_step.mark(dve.memset(k.eps[:, :], EPS))
            dve.wait_ge(k.params_in.sem, 48)
            k.dve_step.mark(dve.tensor_copy(srcf, k.srci[:, :]))
            step(dve, k.dve_step, dve.tensor_copy(dstf, k.dsti[:, :]))
            step(dve, k.dve_step, dve.scalar_tensor_tensor(keyf, dstf, float(N), srcf, ALU.mult, ALU.add))
            k.dve_step.mark(dve.tensor_copy(k.key[:, :], keyf))
            dve.wait_ge(k.pool_step.sem, pool0 + 1)
            for t in range(ET):
                if t >= 3:
                    dve.wait_ge(k.pe_step.sem, pe0 + t - 2)
                k.dve_for_pe.mark(dve.tensor_scalar(hot[:, t % 3, 0, :], iota, srcf[:, t:t + 1], None, ALU.is_equal))
                k.dve_for_pe.mark(dve.tensor_scalar(hot[:, t % 3, 1, :], iota, dstf[:, t:t + 1], None, ALU.is_equal))
            dve.wait_ge(k.filled.sem, filled0 + 1)
            for i in range(T):
                bank = k.ps[0:P, i // 2, (i % 2) * 512:(i % 2) * 512 + 512]
                k.dve_step.mark(dve.tensor_copy(k.cT[:, i, 0:500], bank[:, 0:500]))
                b = T + i // 3
                tail = k.ps[0:P, b // 2, (b % 2) * 512 + (i % 3) * P:(b % 2) * 512 + (i % 3 + 1) * P]
                k.dve_step.mark(dve.tensor_copy(k.cT[:, i, 500:625], tail))
            counts_in.append(k.dve_step.n)
            for j in range(T):
                dve.wait_ge(k.filled.sem, filled0 + 2 + j)
                k.dve_step.mark(dve.tensor_scalar(k.neg[:, j, :].rearrange("p (i s) -> p i s", i=T), tiles(k.ps[0:P, j % 4, :]),
                                                  0.0, NEG, ALU.is_equal, ALU.mult))
                k.emptied.mark(dve.tensor_reduce(k.deg[:, j:j + 1], tiles(k.ps[0:P, j % 4, :]), mybir.AxisListType.XY, ALU.add))

        @block.tensor
        def _(pe):
            for t in range(ET):
                pe.wait_ge(k.dve_for_pe.sem, ready0 + 2 * t + 2)
                for i in range(T):
                    w = hot[:, t % 3, 0, i * P:(i + 1) * P]
                    bank = k.ps[0:P, i // 2, (i % 2) * 512:(i % 2) * 512 + 512]
                    b = T + i // 3
                    tail = k.ps[0:P, b // 2, (b % 2) * 512 + (i % 3) * P:(b % 2) * 512 + (i % 3 + 1) * P]
                    pe.matmul(bank[:, 0:500], w, hot[:, t % 3, 1, 0:500], start=t == 0, stop=t == ET - 1, skip_group_check=True)
                    last = pe.matmul(tail, w, hot[:, t % 3, 1, 500:625], start=t == 0 and i % 3 == 0, stop=t == ET - 1, skip_group_check=True)
                if t < ET - 1:
                    k.pe_step.mark(last)
                else:
                    k.filled.mark(last)
            pe.wait_ge(k.pool_step.sem, pool0 + 3)
            pe.wait_ge(k.dve_step.sem, counts_in[0])
            for j in range(T):
                if j >= 4:
                    pe.wait_ge(k.emptied.sem, emptied0 + j - 3)
                for i in range(T):
                    last = pe.transpose(k.ps[0:P, j % 4, i * 128:i * 128 + P], k.cT[:, i, j * P:(j + 1) * P], k.ident[0:P, 0:P])
                k.filled.mark(last)


def row_norm(k, dve, st, src, j=0):
    k.dve_step.mark(dve.bn_stats(st[:, 0:6], src[:, 0:HALF]))
    step(dve, k.dve_step, dve.bn_stats(st[:, 6:12], src[:, HALF:D]))
    k.var_ready.mark(dve.bn_aggr(st[:, 12:14], st[:, 0:12]))


def deviation(k, act, st, nth):
    act.wait_ge(k.var_ready.sem, nth)
    k.std_ready.mark(act.activation(st[:, 14:15], st[:, 13:14], ACT.Sqrt, bias=k.eps[0:P, :]))


def norm_stage(k, normalise=True):
    nc = k.nc
    st = k.arena[0:P, k.arena_words - 80:].rearrange("p (t s) -> p t s", t=T)
    f0, e0, d0, v0, rs0 = k.filled.n, k.emptied.n, k.dve_for_pe.n, k.var_ready.n, k.std_ready.n
    with nc.Block() as block:
        @block.sync
        def _(sp):
            k.feed(sp, 0)

        @block.vector
        def _(dve):
            if normalise:
                for t in range(T):
                    row_norm(k, dve, st[:, t, :], k.x[:, t, :])
                for t in range(T):
                    dve.wait_ge(k.std_ready.sem, rs0 + t + 1)
                    step(dve, k.dve_step, dve.reciprocal(st[:, t, 14:15], st[:, t, 14:15]))
                    k.dve_for_pe.mark(dve.tensor_scalar(k.xn[:, t, :], k.x[:, t, :], st[:, t, 12:13], st[:, t, 14:15],
                                                        ALU.subtract, ALU.mult))

        @block.tensor
        def _(pe):
            if normalise:
                pe.wait_ge(k.dve_for_pe.sem, d0 + T)
            for c in range(C):
                if c >= 4:
                    pe.wait_ge(k.emptied.sem, e0 + c - 3)
                for t in range(T):
                    last = pe.transpose(k.ps[:, c % 4, t * 128:t * 128 + P], k.xn[:, t, c * 128:(c + 1) * 128], k.ident[0:P, 0:P])
                k.filled.mark(last)

        @block.scalar
        def _(act):
            if normalise:
                for t in range(T):
                    deviation(k, act, st[:, t, :], v0 + t + 1)
            for c in range(C):
                act.wait_ge(k.filled.sem, f0 + c + 1)
                k.emptied.mark(act.activation(k.xT[:, c, :].rearrange("p (t n) -> p t n", t=T), tiles(k.ps[:, c % 4, :]), ACT.Copy))


def node_major(pe, out, lhs, w, chunks, cols=D, start=True, stop=True):
    for c in chunks:
        for b in range(2):
            last = pe.matmul(out[0:P, b * 512:b * 512 + cols // 2], lhs(c), w(c)[:, b * cols // 2:(b + 1) * cols // 2],
                             start=start and c == chunks[0], stop=stop and c == chunks[-1])
    return last


def feature_major(pe, out, parts, lhs, rhs, chunks):
    for c in chunks:
        for lo, hi in ((0, 512), (512, N)):
            last = pe.matmul(out[0:parts, lo:hi], lhs(c), rhs(c)[:, lo:hi], start=c == chunks[0], stop=c == chunks[-1])
    return last


def gat2_project_stage(k, heads, bs, bd, faug):
    nc, a = k.nc, k.a
    hw = D // heads
    bias = k.carve(P, 2, D)
    fd = k.carve(P, T, D)
    f0, e0, p0 = k.filled.n, k.emptied.n, k.params_in.n
    with nc.Block() as block:
        @block.sync
        def _(sp):
            for n, b in enumerate((bs, bd)):
                k.params_in.mark_dma(sp.dma_start(bias[:, n, :], a[b][0:P, :]))
            k.feed(sp, 2)
            fs_rows = k.fs_d.rearrange("(t p) (h f) -> t p h f", p=P, h=heads)
            fd_rows = k.fd_d.rearrange("(t p) d -> t p d", p=P)
            for t in range(T):
                sp.wait_ge(k.emptied.sem, e0 + t + 1)
                k.stored.mark_dma(sp.dma_start(fs_rows[t], faug[:, t, :, 0:hw]))
            for t in range(T):
                sp.wait_ge(k.emptied.sem, e0 + T + t + 1)
                k.stored.mark_dma(sp.dma_start(fd_rows[t], fd[:, t, :]))
            sp.wait_ge(k.stored.sem, k.stored.n)

        @block.tensor
        def _(pe):
            for n in range(2):
                w = k.slab(pe).rearrange("p (c d) -> p c d", c=C)
                for t in range(T):
                    j = n * T + t
                    wait(pe, k.emptied, e0 + j - 3 if j >= 4 else 0)
                    last = node_major(pe, k.ps[:, j % 4, :], lambda c: k.xT[:, c, t * P:(t + 1) * P], lambda c: w[:, c, :], range(C))
                    k.filled.mark(last)
                nop = k.filled.n
                pe.wait_ge(k.filled.sem, nop)
                pe.sem_inc(k.slab_free.sem, 1)
                k.slab_free.n += 1
                k.used += 1

        @block.vector
        def _(dve):
            k.dve_step.mark(dve.memset(faug[:, :, :, hw:hw + 1], 1.0))
            dve.wait_ge(k.params_in.sem, p0 + 32)
            for j in range(2 * T):
                dve.wait_ge(k.filled.sem, f0 + j + 1)
                src = halves(k.ps[0:P, j % 4, :])
                b = bias[:, j // T, :].rearrange("p (b f) -> p b f", b=2)
                if j < T:
                    out = faug[:, j, :, 0:hw]
                    if heads > 1:
                        src = src.rearrange("p b (h f) -> p b h f", f=hw)
                        b = b.rearrange("p b (h f) -> p b h f", f=hw)
                        out = out.rearrange("p (b h) f -> p b h f", b=2)
                    else:
                        out = faug[:, j, 0, 0:D].rearrange("p (b f) -> p b f", b=2)
                else:
                    out = fd[:, j - T, :].rearrange("p (b f) -> p b f", b=2)
                k.emptied.mark(dve.tensor_tensor(out, src, b, ALU.add))


def gat2_edge_stage(k, heads, attn):
    nc, a = k.nc, k.a
    SL, LAG = 4, 3
    ga = k.carve(P, SL, D)
    gb = k.carve(P, SL, D)
    attn_b = k.carve(P, D)
    logit = k.carve(P, ET, heads)
    p0, s0, a0, l0, sc0 = k.params_in.n, k.dve_ready.n, k.act_ready.n, k.logits_ready.n, k.scattered.n
    g0 = [g.n for g in k.gathered]
    with nc.Block() as block:
        @block.sync
        def _(sp):
            k.params_in.mark_dma(sp.dma_start(attn_b, a[attn][0:P, :]))
            k.feed(sp, 0)

        @block.gpsimd
        def _(pool):
            for t in range(ET + LAG):
                if t < ET:
                    if t >= SL:
                        pool.wait_ge(k.logits_ready.sem, l0 + t - SL + 1)
                    for buf, rows, idx in ((ga, k.fs_d, k.srci), (gb, k.fd_d, k.dsti)):
                        k.gathered[t % SL].mark_dma(pool.indirect_dma_start(
                            buf[:, t % SL, :], None, rows, bass.IndirectOffsetOnAxis(ap=idx[:, t:t + 1], axis=0)))
                s = t - LAG
                if s >= 0:
                    pool.wait_ge(k.logits_ready.sem, l0 + s + 1)
                    wait(pool, k.scattered, k.scattered.n)
                    k.scattered.mark_dma(pool.indirect_dma_start(
                        k.dense[heads], bass.IndirectOffsetOnAxis(ap=k.key[:, s:s + 1], axis=0), logit[:, s, :], None))
            pool.wait_ge(k.scattered.sem, k.scattered.n)

        @block.vector
        def _(dve):
            dve.wait_ge(k.params_in.sem, p0 + 16)
            for u in range(ET):
                    dve.wait_ge(k.gathered[u % SL].sem, g0[u % SL] + 32 * (u // SL + 1))
                    step(dve, k.dve_step, dve.tensor_tensor(ga[:, u % SL, :], ga[:, u % SL, :], gb[:, u % SL, :], ALU.add))
                    step(dve, k.dve_step, dve.scalar_tensor_tensor(ga[:, u % SL, :], ga[:, u % SL, :], SLOPE, ga[:, u % SL, :], ALU.mult, ALU.max))
                    step(dve, k.dve_step, dve.tensor_tensor(gb[:, u % SL, :], ga[:, u % SL, :], attn_b, ALU.mult))
                    k.logits_ready.mark(dve.tensor_reduce(logit[:, u, :], gb[:, u % SL, :].rearrange("p (h f) -> p h f", h=heads), AX, ALU.add))


def gat2_dense_stage(k, heads, faug, ln_w, ln_b, last_layer):
    nc, a = k.nc, k.a
    hw = D // heads
    L = k.carve(P, 2, N * heads)
    wt = k.carve(P, 3, T * P)
    m = k.carve(P, 2, heads)
    r = k.carve(P, D)
    e = k.carve(P, D)
    lnw = k.carve(P, D)
    lnb = k.carve(P, D)
    st = k.carve(P, 16)
    rden = k.carve(P, 8)
    p0 = k.params_in.n
    in0 = [s.n for s in k.dense_in]
    neg0, exp0, tr0, wt0, agg0, e0, el0 = (k.dve_ready.n, k.act_for_pe.n, k.filled.n, k.dve_for_pe.n,
                                           k.pe_step.n, k.emptied.n, k.act_ready.n)
    v0, rs0 = k.var_ready.n, k.std_ready.n
    with nc.Block() as block:
        @block.sync
        def _(sp):
            k.params_in.mark_dma(sp.dma_start(lnw, a[ln_w][0:P, :]))
            k.params_in.mark_dma(sp.dma_start(lnb, a[ln_b][0:P, :]))
            k.feed(sp, 0)
            table = k.dense[heads].rearrange("(j p s) h -> j p (s h)", p=P, j=T)
            for j in range(T):
                if j >= 2:
                    sp.wait_ge(k.filled.sem, tr0 + heads * (j - 1))
                k.dense_in[j % 2].mark_dma(sp.dma_start(L[:, j % 2, :], table[j]))

        @block.vector
        def _(dve):
            dve.wait_ge(k.params_in.sem, p0 + 32)

            def row_max(j):
                dve.wait_ge(k.dense_in[j % 2].sem, in0[j % 2] + 16 * (j // 2 + 1))
                if j >= 2:
                    dve.wait_ge(k.act_for_pe.sem, exp0 + heads * (j - 1))
                step(dve, k.dve_step, dve.tensor_reduce(m[:, j % 2, :], L[:, j % 2, :].rearrange("p (s h) -> p h s", h=heads), AX, ALU.max))
                k.dve_ready.mark(dve.tensor_scalar(m[:, j % 2, :], m[:, j % 2, :], -1.0, None, ALU.mult))

            row_max(0)
            for j in range(T):
                for h in range(heads):
                    n = j * heads + h
                    dve.wait_ge(k.filled.sem, tr0 + n + 1)
                    if n >= 3:
                        dve.wait_ge(k.pe_step.sem, agg0 + n - 2)
                    k.dve_for_pe.mark(dve.tensor_tensor(wt[:, n % 3, :].rearrange("p (i d) -> p i d", i=T), tiles(k.ps[0:P, n % 2, :]),
                                                        k.cT[:, :, j * P:(j + 1) * P], ALU.mult))
                    if h == 0 and j + 1 < T:
                        row_max(j + 1)
                dve.wait_ge(k.pe_step.sem, agg0 + (j + 1) * heads)
                out = k.ps[0:P, 2 + j % 2, :]
                if heads == 1:
                    num = wide(out[:, :])[:, :, :]
                    den = out[:, D:D + 1]
                    step(dve, k.dve_step, dve.tensor_scalar(rden[:, 0:1], den, 1e-30, None, ALU.max))
                    step(dve, k.dve_step, dve.reciprocal(rden[:, 0:1], rden[:, 0:1]))
                    step(dve, k.dve_step, dve.tensor_scalar(r, out[:, 0:D], rden[:, 0:1], None, ALU.mult))
                else:
                    v = wide(out)[:, :, 0:4 * (hw + 1)].rearrange("p b (h f) -> p b h f", f=hw + 1)
                    rd = rden[:, :].rearrange("p (b h o) -> p b h o", b=2, o=1)
                    step(dve, k.dve_step, dve.tensor_scalar(rd, v[:, :, :, hw:hw + 1], 1e-30, None, ALU.max))
                    step(dve, k.dve_step, dve.reciprocal(rden, rden))
                    step(dve, k.dve_step, dve.tensor_tensor(r.rearrange("p (b h f) -> p b h f", b=2, f=hw), v[:, :, :, 0:hw],
                                                            rd.broadcast_to([P, 2, 4, hw]), ALU.mult))
                k.emptied.mark(dve.tensor_scalar(e, r, 0.0, None, ALU.min))
                step(dve, k.dve_step, dve.tensor_scalar(r, r, 0.0, -1.0, ALU.max, ALU.add))
                dve.wait_ge(k.act_ready.sem, el0 + j + 1)
                step(dve, k.dve_step, dve.tensor_tensor(r, r, e, ALU.add))
                if not last_layer:
                    step(dve, k.dve_step, dve.tensor_tensor(r, r, k.xn[:, j, :], ALU.add))
                row_norm(k, dve, st, r)
                dve.wait_ge(k.std_ready.sem, rs0 + j + 1)
                step(dve, k.dve_step, dve.reciprocal(st[:, 14:15], st[:, 14:15]))
                step(dve, k.dve_step, dve.tensor_scalar(r, r, st[:, 12:13], st[:, 14:15], ALU.subtract, ALU.mult))
                step(dve, k.dve_step, dve.tensor_tensor(r, r, lnw, ALU.mult))
                if last_layer:
                    step(dve, k.dve_step, dve.tensor_tensor(r, r, lnb, ALU.add))
                    step(dve, k.dve_step, dve.tensor_tensor(k.x[:, j, :], k.x[:, j, :], r, ALU.add))
                else:
                    step(dve, k.dve_step, dve.tensor_tensor(k.xn[:, j, :], r, lnb, ALU.add))

        @block.scalar
        def _(act):
            def exps(j):
                act.wait_ge(k.dve_ready.sem, neg0 + j + 1)
                for h in range(heads):
                    v = L[:, j % 2, :].rearrange("p (s h) -> p h s", h=heads)[:, h, :]
                    k.act_for_pe.mark(act.activation(v, v, ACT.Exp, bias=m[:, j % 2, h:h + 1]))
            exps(0)
            for j in range(T):
                if j + 1 < T:
                    exps(j + 1)
                act.wait_ge(k.emptied.sem, e0 + j + 1)
                k.act_ready.mark(act.activation(e, e, ACT.Exp))
                deviation(k, act, st, v0 + j + 1)

        @block.tensor
        def _(pe):
            def aggregate(n):
                j, h = n // heads, n % heads
                pe.wait_ge(k.dve_for_pe.sem, wt0 + n + 1)
                if h == 0 and j >= 2:
                    pe.wait_ge(k.emptied.sem, e0 + j - 1)
                out = k.ps[0:P, 2 + j % 2, :]
                for i in range(T):
                    w = wt[:, n % 3, i * P:(i + 1) * P]
                    if heads == 1:
                        pe.matmul(out[:, 0:512], w, faug[:, i, 0, 0:512], start=i == 0, stop=i == T - 1)
                        last = pe.matmul(out[:, 512:D + 1], w, faug[:, i, 0, 512:D + 1], start=i == 0, stop=i == T - 1)
                    else:
                        at = h // 4 * 512 + (h % 4) * (hw + 1)
                        last = pe.matmul(out[:, at:at + hw + 1], w, faug[:, i, h, :], start=i == 0, stop=i == T - 1)
                k.pe_step.mark(last)
            for n in range(T * heads):
                j, h = n // heads, n % heads
                pe.wait_ge(k.act_for_pe.sem, exp0 + n + 1)
                if n >= 2:
                    pe.wait_ge(k.dve_for_pe.sem, wt0 + n - 1)
                v = L[:, j % 2, :].rearrange("p (s h) -> p h s", h=heads)
                for i in range(T):
                    last = pe.transpose(k.ps[0:P, n % 2, i * 128:i * 128 + P], v[:, h, i * P:(i + 1) * P], k.ident[0:P, 0:P])
                k.filled.mark(last)
                if n >= 1:
                    aggregate(n - 1)
            aggregate(T * heads - 1)
    for s, n in zip(k.dense_in, in0):
        pass


def gat2(k):
    for heads, bs, bd, attn, w, b, last in ((8, "L0_gnn_b1s", "L0_gnn_b1d", "L0_gnn_attn1", "L0_gnn_ln1_w", "L0_gnn_ln1_b", False),
                                            (1, "L0_gnn_bos", "L0_gnn_bod", "L0_gnn_attno", "L0_gnn_lno_w", "L0_gnn_lno_b", True)):
        norm_stage(k, normalise=not last)
        k.reset()
        faug = k.carve(P, T, heads, D // heads + 1)
        keep = k.at
        gat2_project_stage(k, heads, bs, bd, faug)
        k.reset(keep)
        gat2_edge_stage(k, heads, attn)
        k.reset(keep)
        gat2_dense_stage(k, heads, faug, w, b, last)


RMIN, RMAX, DEGREE = -4.0, 4.0, 3
STEP_H = (RMAX - RMIN) / (NCP - DEGREE)


def spline_stage(k):
    nc, a = k.nc, k.a
    k.reset()
    G = KG * N
    u = k.carve(128, C, N)
    bufs = k.carve(128, 2, 2, G)
    sq = k.carve(128, 2, G)
    groups = [(c, g) for c in range(C) for g in range(NCP // KG)]
    NG = len(groups)
    f0, s0, b0, ba0, act0, po0, e0 = k.filled.n, k.dve_ready.n, k.act_ready.n, k.dve_for_pe.n, k.act_step.n, k.pool_step.n, k.pe_step.n
    with nc.Block() as block:
        @block.sync
        def _(sp):
            k.feed(sp, 2)

        @block.vector
        def _(dve):
            k.dve_ready.mark(dve.tensor_scalar(u, k.xT[:, :, :], 1.0 / STEP_H, -RMIN / STEP_H + DEGREE, ALU.mult, ALU.add))
            for n in range(NG):
                A, B = bufs[:, n % 2, 0, :], bufs[:, n % 2, 1, :]
                dve.wait_ge(k.act_ready.sem, b0 + 2 * n + 1)
                if n >= 2:
                    dve.wait_ge(k.pe_step.sem, e0 + n - 1)
                k.dve_ready.mark(dve.tensor_scalar(B, A, -1.0, 0.0, ALU.add, ALU.max))
                dve.wait_ge(k.act_ready.sem, b0 + 2 * n + 2)
                step(dve, k.dve_step, dve.scalar_tensor_tensor(B, sq[:, 1, :], -4.0, B, ALU.mult, ALU.mult))
                dve.wait_ge(k.pool_step.sem, po0 + n + 1)
                k.dve_for_pe.mark(dve.tensor_tensor(B, A, B, ALU.add))

        @block.scalar
        def _(act):
            act.wait_ge(k.dve_ready.sem, s0 + 1)
            for n, (c, g) in enumerate(groups):
                A, B = bufs[:, n % 2, 0, :], bufs[:, n % 2, 1, :]
                if n >= 2:
                    act.wait_ge(k.dve_for_pe.sem, ba0 + n - 1)
                for i in range(KG):
                    kk = g * KG + i
                    k.act_step.mark(act.activation(A[:, i * N:(i + 1) * N], u[:, c, :], ACT.Abs, bias=k.kcol[:, kk:kk + 1]))
                act.wait_ge(k.act_step.sem, k.act_step.n)
                k.act_ready.mark(act.activation(A, A, ACT.Relu, bias=k.two[:, :], scale=-1.0))
                if n >= 1:
                    act.wait_ge(k.pool_step.sem, po0 + n)
                act.wait_ge(k.act_ready.sem, k.act_ready.n)
                k.act_step.mark(act.activation(sq[:, 0, :], A, ACT.Square))
                act.wait_ge(k.dve_ready.sem, s0 + 2 + n)
                if n >= 1:
                    act.wait_ge(k.dve_for_pe.sem, ba0 + n)
                k.act_ready.mark(act.activation(sq[:, 1, :], B, ACT.Square))

        @block.gpsimd
        def _(pool):
            for n in range(NG):
                A = bufs[:, n % 2, 0, :]
                pool.wait_ge(k.act_step.sem, act0 + (KG + 1) * (n + 1))
                pool.wait_ge(k.dve_ready.sem, s0 + 2 + n)
                k.pool_step.mark(pool.tensor_tensor(A, A, sq[:, 0, :], ALU.mult))

        @block.tensor
        def _(pe):
            for n, (c, g) in enumerate(groups):
                if n % 12 == 0:
                    w = k.slab(pe).rearrange("p (g k o) -> p g k o", k=KG, o=KH)
                pe.wait_ge(k.dve_for_pe.sem, ba0 + n + 1)
                B = bufs[:, n % 2, 1, :]
                for i in range(KG):
                    for lo, hi in ((0, 512), (512, N)):
                        last = pe.matmul(k.ps[0:KH, 0, lo:hi], w[:, n % 12, i, :], B[:, i * N + lo:i * N + hi],
                                         start=n == 0 and i == 0, stop=n == NG - 1 and i == KG - 1)
                k.pe_step.mark(last)
                if n % 12 == 11:
                    pe.wait_ge(k.pe_step.sem, k.pe_step.n)
                    pe.sem_inc(k.slab_free.sem, 1)
                    k.slab_free.n += 1
                    k.used += 1
            k.filled.n += 0
    k.reset()
    u2 = k.carve(128, N)
    A = k.carve(128, 8, N)
    B = k.carve(128, 8, N)
    S = k.carve(128, 8, N)
    f0, e0, ba0, a0 = k.filled.n, k.emptied.n, k.dve_for_pe.n, k.act_ready.n
    dr0 = k.dve_ready.n
    with nc.Block() as block:
        @block.sync
        def _(sp):
            k.feed(sp, 2)

        @block.scalar
        def _(act):
            act.wait_ge(k.dve_ready.sem, dr0 + 2)
            for i in range(8):
                k.act_step.mark(act.activation(A[:, i, :], u2, ACT.Abs, bias=k.kcol2[:, i:i + 1]))
            act.wait_ge(k.act_step.sem, k.act_step.n)
            k.act_ready.mark(act.activation(A, A, ACT.Relu, bias=k.two[:, :], scale=-1.0))
            act.wait_ge(k.act_ready.sem, k.act_ready.n)
            k.act_ready.mark(act.activation(S, A, ACT.Square))

        @block.vector
        def _(dve):
            for half in range(2):
                k.dve_ready.mark(dve.tensor_scalar(u2[half * 64:half * 64 + 64, :], k.ps[0:KH, 0, 0:N], 1.0 / (6.0 * STEP_H),
                                                   -RMIN / STEP_H + DEGREE, ALU.mult, ALU.add))
            dve.wait_ge(k.act_ready.sem, a0 + 1)
            step(dve, k.dve_step, dve.tensor_scalar(B, A, -1.0, 0.0, ALU.add, ALU.max))
            dve.wait_ge(k.act_ready.sem, a0 + 2)
            step(dve, k.dve_step, dve.tensor_tensor(A, S, A, ALU.mult))
            step(dve, k.dve_step, dve.tensor_tensor(S, B, B, ALU.mult))
            step(dve, k.dve_step, dve.scalar_tensor_tensor(B, S, -4.0, B, ALU.mult, ALU.mult))
            k.dve_for_pe.mark(dve.tensor_tensor(B, A, B, ALU.add))
            for t in range(T):
                dve.wait_ge(k.filled.sem, f0 + t + 1)
                xt = k.x[:, t, :].rearrange("p (b f) -> p b f", b=2)
                k.emptied.mark(dve.scalar_tensor_tensor(xt, halves(k.ps[0:P, t % 4, :]), 1.0 / 6.0, xt, ALU.mult, ALU.add))

        @block.tensor
        def _(pe):
            pe.wait_ge(k.dve_for_pe.sem, ba0 + 1)
            w = [k.slab(pe, s).rearrange("p (c d) -> p c d", c=C) for s in range(2)]
            for t in range(T):
                wait(pe, k.emptied, e0 + t - 3 if t >= 4 else 0)
                last = node_major(pe, k.ps[:, t % 4, :], lambda c: B[:, c, t * P:(t + 1) * P], lambda c: w[c // 4][:, c % 4, :], range(8))
                k.filled.mark(last)
            pe.wait_ge(k.filled.sem, k.filled.n)
            pe.sem_inc(k.slab_free.sem, 2)
            k.slab_free.n += 2
            k.used += 2


def pair_weights(k, as_col, ad_col, wt, tmp, loops):
    nc = k.nc
    diag, junk, cols = tmp["diag"], tmp["junk"], tmp["cols"]
    mx, pc, qc, as2 = cols[:, 0, :], cols[:, 1, :], cols[:, 2, :], cols[:, 3, :]
    ident = k.ident[0:P, 0:P].rearrange("p (o c) -> p o c", o=1).broadcast_to([P, T, P])
    d0, f0, a0, r0 = k.dve_for_pe.n, k.filled.n, k.act_ready.n, k.dve_ready.n
    used = []
    with nc.Block() as block:
        @block.sync
        def _(sp):
            k.feed(sp, 0)

        @block.vector
        def _(dve):
            def spread(n, col):
                c = col.rearrange("p (t o) -> p t o", o=1).broadcast_to([P, T, P])
                k.dve_for_pe.mark(dve.tensor_tensor(diag[:, n, :].rearrange("p (t c) -> p t c", t=T), ident, c, ALU.mult))
            spread(0, as_col)
            dve.wait_ge(k.filled.sem, f0 + 1)
            for j in range(T):
                step(dve, k.dve_step, dve.tensor_tensor(junk, tiles(k.ps[0:P, 0, :]), k.neg[:, j, :].rearrange("p (t s) -> p t s", t=T), ALU.add))
                step(dve, k.dve_step, dve.tensor_reduce(mx[:, j:j + 1], junk, mybir.AxisListType.XY, ALU.max))
            if loops:
                step(dve, k.dve_step, dve.tensor_tensor(mx, mx, as_col, ALU.max))
            step(dve, k.dve_step, dve.tensor_tensor(mx, mx, ad_col, ALU.add))
            step(dve, k.dve_step, dve.scalar_tensor_tensor(mx, mx, SLOPE, mx, ALU.mult, ALU.max))
            k.dve_step.mark(dve.tensor_tensor(pc, ad_col, mx, ALU.subtract))
            k.dve_step.mark(dve.tensor_scalar(as2, as_col, SLOPE, None, ALU.mult))
            step(dve, k.dve_step, dve.scalar_tensor_tensor(qc, ad_col, SLOPE, mx, ALU.mult, ALU.subtract))
            spread(1, pc)
            spread(2, qc)
            dve.wait_ge(k.filled.sem, f0 + 2)
            for i in range(T):
                dve.wait_ge(k.act_ready.sem, a0 + 2 * i + 1)
                v = tmp["t"][:, i % 2, :].rearrange("p (t c) -> p t c", t=T)
                k.dve_ready.mark(dve.scalar_tensor_tensor(v, tiles(k.ps[0:P, 1, :]), as_col[:, i:i + 1], v, ALU.add, ALU.max))
                if i >= 1:
                    dve.wait_ge(k.act_ready.sem, a0 + 2 * i)
                    used.append(k.dve_step.mark(dve.scalar_tensor_tensor(wt[:, i - 1, :], tmp["t"][:, (i - 1) % 2, :], 1.0,
                                                                         k.cT[:, i - 1, :], ALU.min, ALU.mult)))
            dve.wait_ge(k.act_ready.sem, a0 + 2 * T)
            k.dve_step.mark(dve.scalar_tensor_tensor(wt[:, T - 1, :], tmp["t"][:, (T - 1) % 2, :], 1.0, k.cT[:, T - 1, :], ALU.min, ALU.mult))

        @block.scalar
        def _(act):
            act.wait_ge(k.filled.sem, f0 + 2)
            for i in range(T):
                if i >= 2:
                    act.wait_ge(k.dve_step.sem, used[i - 2])
                v = tmp["t"][:, i % 2, :]
                k.act_ready.mark(act.activation(v.rearrange("p (t c) -> p t c", t=T), tiles(k.ps[0:P, 2, :]), ACT.Identity, bias=as2[:, i:i + 1]))
                act.wait_ge(k.dve_ready.sem, r0 + i + 1)
                k.act_ready.mark(act.activation(v, v, ACT.Exp))

        @block.tensor
        def _(pe):
            def rows(n, slot):
                for t in range(T):
                    last = pe.matmul(k.ps[:, slot, t * 128:t * 128 + P], k.ones[0:P, :], diag[:, n, t * P:(t + 1) * P], start=True, stop=True)
                return last
            pe.wait_ge(k.dve_for_pe.sem, d0 + 1)
            k.filled.mark(rows(0, 0))
            pe.wait_ge(k.dve_for_pe.sem, d0 + 3)
            rows(1, 1)
            k.filled.mark(rows(2, 2))


def pair_tmp(k):
    flat = k.xn[:, :, :].rearrange("p t d -> p (t d)")
    tmp = {"diag": flat[:, 0:3 * N].rearrange("p (n c) -> p n c", n=3),
           "junk": flat[:, 3 * N:4 * N].rearrange("p (t c) -> p t c", t=T),
           "t": flat[:, 4 * N:6 * N].rearrange("p (n c) -> p n c", n=2),
           "cols": flat[:, 6 * N:6 * N + 4 * T].rearrange("p (n c) -> p n c", n=4)}
    return tmp


def release_slabs(k, pe, count, n):
    pe.wait_ge(count.sem, count.n)
    pe.sem_inc(k.slab_free.sem, n)
    k.slab_free.n += n
    k.used += n


def gat1_head_stage(k, h, hh, cols, src, dst, width):
    nc, a = k.nc, k.a
    av = k.carve(P, 2, width)
    junk = k.carve(P, width)
    f0, e0, p0 = k.filled.n, k.emptied.n, k.params_in.n
    second = width == D
    chunks = 16 if second else C
    with nc.Block() as block:
        @block.sync
        def _(sp):
            for n, v in enumerate((src, dst)):
                rows = a[v][0:P, 0:D] if second else a[v][0:P, h * width:(h + 1) * width]
                k.params_in.mark_dma(sp.dma_start(av[:, n, :], rows))
            k.feed(sp, 3 if second else 1)

        @block.tensor
        def _(pe):
            if second:
                w = [k.slab(pe, s).rearrange("p (c d) -> p c d", c=C) for s in range(3)]
            else:
                w = k.slab(pe)[:, 0:C * HID1].rearrange("p (c d) -> p c d", c=C)
            for t in range(T):
                wait(pe, k.emptied, e0 + t - 3 if t >= 4 else 0)
                if second:
                    last = node_major(pe, k.ps[:, t % 4, :], lambda c: k.h2T[:, c, t * P:(t + 1) * P], lambda c: w[c // 6][:, c % 6, :], range(chunks))
                else:
                    for c in range(C):
                        last = pe.matmul(k.ps[0:P, t % 4, 0:HID1], k.xT[:, c, t * P:(t + 1) * P], w[:, c, :], start=c == 0, stop=c == C - 1)
                k.filled.mark(last)
            release_slabs(k, pe, k.filled, 3 if second else 1)

        @block.scalar
        def _(act):
            for t in range(T):
                act.wait_ge(k.filled.sem, f0 + t + 1)
                if second:
                    k.emptied.mark(act.activation(hh[:, t, 0:D].rearrange("p (b f) -> p b f", b=2), halves(k.ps[0:P, t % 4, :]), ACT.Copy))
                else:
                    k.emptied.mark(act.activation(hh[:, t, 0:HID1], k.ps[0:P, t % 4, 0:HID1], ACT.Copy))

        @block.vector
        def _(dve):
            k.dve_step.mark(dve.memset(hh[:, :, width:width + 1], 1.0))
            dve.wait_ge(k.params_in.sem, p0 + 32)
            for t in range(T):
                dve.wait_ge(k.emptied.sem, e0 + t + 1)
                for n in range(2):
                    dve.wait_ge(k.dve_step.sem, k.dve_step.n)
                    k.dve_step.mark(dve.tensor_tensor_reduce(junk, hh[:, t, 0:width], av[:, n, :], 1.0, 0.0, ALU.mult, ALU.add,
                                                             cols[:, n, t:t + 1]))


def gat1_gather_stage(k, h, hh, wt):
    nc, a = k.nc, k.a
    rden = k.carve(128, N)
    r = k.carve(128, 2, N)
    e = k.carve(128, 2, N)
    bcol = k.carve(128, 4)
    f0, e0, p0, r0, a0, s0 = k.filled.n, k.emptied.n, k.params_in.n, k.dve_ready.n, k.act_ready.n, k.dve_step.n
    FC = HID1 // 128
    with nc.Block() as block:
        @block.sync
        def _(sp):
            k.params_in.mark_dma(sp.dma_start(bcol, a["L1_gnn_b1"][:, h * FC:(h + 1) * FC]))
            k.feed(sp, 0)

        @block.tensor
        def _(pe):
            k.filled.mark(feature_major(pe, k.ps[:, 3, :], 128, lambda i: k.ones[0:P, :], lambda i: wt[:, i, :], range(T)))
            for f in range(FC):
                wait(pe, k.emptied, e0 + f - 2 if f >= 3 else 0)
                k.filled.mark(feature_major(pe, k.ps[:, f % 3, :], 128, lambda i: hh[:, i, f * 128:(f + 1) * 128], lambda i: wt[:, i, :], range(T)))

        @block.vector
        def _(dve):
            dve.wait_ge(k.filled.sem, f0 + 1)
            step(dve, k.dve_step, dve.tensor_scalar(rden, k.ps[:, 3, 0:N], 1e-16, None, ALU.add))
            step(dve, k.dve_step, dve.reciprocal(rden, rden))
            dve.wait_ge(k.params_in.sem, p0 + 16)
            for f in range(FC + 1):
                if f < FC:
                    R = r[:, f % 2, :]
                    dve.wait_ge(k.filled.sem, f0 + 2 + f)
                    k.emptied.mark(dve.tensor_tensor(R, k.ps[:, f % 3, 0:N], rden, ALU.mult))
                    dve.wait_ge(k.emptied.sem, k.emptied.n)
                    step(dve, k.dve_step, dve.tensor_scalar(R, R, bcol[:, f:f + 1], None, ALU.add))
                    k.dve_ready.mark(dve.tensor_scalar(e[:, f % 2, :], R, 0.0, None, ALU.min))
                    step(dve, k.dve_step, dve.tensor_scalar(R, R, 0.0, -1.0, ALU.max, ALU.add))
                if f >= 1:
                    dve.wait_ge(k.act_ready.sem, a0 + f)
                    step(dve, k.dve_step, dve.tensor_tensor(k.h2T[:, h * FC + f - 1, :], r[:, (f - 1) % 2, :], e[:, (f - 1) % 2, :], ALU.add))

        @block.scalar
        def _(act):
            for f in range(FC):
                act.wait_ge(k.dve_ready.sem, r0 + f + 1)
                k.act_ready.mark(act.activation(e[:, f % 2, :], e[:, f % 2, :], ACT.Exp))


def add_scaled_stage(k, lhs, rhs, slabs, finish, width=D):
    nc = k.nc
    f0, e0 = k.filled.n, k.emptied.n
    with nc.Block() as block:
        @block.sync
        def _(sp):
            k.feed(sp, slabs)

        @block.tensor
        def _(pe):
            for t in range(T):
                wait(pe, k.emptied, e0 + t - 3 if t >= 4 else 0)
                for i in range(T):
                    for lo, hi in ((0, min(512, width)), (512, width)):
                        if hi > lo:
                            last = pe.matmul(k.ps[0:P, t % 4, lo:hi], lhs(i, t), rhs(i)[:, lo:hi], start=i == 0, stop=i == T - 1)
                k.filled.mark(last)

        @block.vector
        def _(dve):
            for t in range(T):
                dve.wait_ge(k.filled.sem, f0 + t + 1)
                finish(dve, t, k.ps[0:P, t % 4, :])


def gat1(k):
    nc, a = k.nc, k.a
    norm_stage(k)
    k.reset()
    k.h2T = k.carve(128, 16, N)
    hh = k.carve(P, T, HID1 + 1)
    cols = k.carve(P, 2, T)
    keep = k.at
    loops_stage(k, 1.0)
    for h in range(H_L1):
        k.reset(keep)
        gat1_head_stage(k, h, hh, cols, "L1_gnn_a1_src", "L1_gnn_a1_dst", HID1)
        k.reset(keep)
        wt = k.carve(P, T, N)
        pair_weights(k, cols[:, 0, :], cols[:, 1, :], wt, pair_tmp(k), True)
        gat1_gather_stage(k, h, hh, wt)
    k.reset(16 * N)
    hh = k.carve(P, T, D + 1)
    cols = k.carve(P, 2, T)
    keep = k.at
    gat1_head_stage(k, 0, hh, cols, "L1_gnn_a2_src", "L1_gnn_a2_dst", D)
    k.reset(0)
    wt = k.carve(P, T, N)
    b2 = k.carve(P, D)
    r = k.carve(P, D)
    rden = k.carve(P, 1)
    pair_weights(k, cols[:, 0, :], cols[:, 1, :], wt, pair_tmp(k), True)
    load_stage(k, [(b2, a["L1_gnn_b2"][0:P, :])])

    def finish(dve, t, ps):
        step(dve, k.dve_step, dve.tensor_scalar(rden, ps[:, D:D + 1], 1e-16, None, ALU.add))
        step(dve, k.dve_step, dve.reciprocal(rden, rden))
        k.emptied.mark(dve.scalar_tensor_tensor(r, ps[:, 0:D], rden, b2, ALU.mult, ALU.add))
        dve.wait_ge(k.emptied.sem, k.emptied.n)
        step(dve, k.dve_step, dve.tensor_tensor(k.x[:, t, :], k.x[:, t, :], r, ALU.add))
    add_scaled_stage(k, lambda i, t: wt[:, i, t * P:(t + 1) * P], lambda i: hh[:, i, :], 0, finish, D + 1)


def load_stage(k, loads):
    with k.nc.Block() as block:
        @block.sync
        def _(sp):
            for dst, src in loads:
                k.params_in.mark_dma(sp.dma_start(dst, src))
            sp.wait_ge(k.params_in.sem, k.params_in.n)
            k.feed(sp, 0)


def loops_stage(k, sign):
    with k.nc.Block() as block:
        @block.vector
        def _(dve):
            for t in range(T):
                d = k.cT[:, t, t * P:(t + 1) * P]
                k.dve_step.mark(dve.scalar_tensor_tensor(d, k.ident[0:P, 0:P], sign, d, ALU.mult, ALU.add))
            k.dve_step.mark(dve.tensor_scalar(k.deg[:, :], k.deg[:, :], sign, None, ALU.add))


def route_stage(k, w_name, comb, bias_name, top):
    nc, a = k.nc, k.a
    X8 = EXPERTS
    wr = k.carve(128, C, X8)
    sc = k.carve(P, T, X8)
    sel = k.carve(P, T, X8)
    big = k.carve(P, T, X8, X8)
    bi2 = k.carve(P, T, X8, X8)
    low = k.carve(P, X8, X8)
    mx = k.carve(P, T)
    bias = k.carve(P, X8)
    f0, p0, r0, a0 = k.filled.n, k.params_in.n, k.dve_ready.n, k.act_ready.n
    po0 = k.pool_step.n
    with nc.Block() as block:
        @block.sync
        def _(sp):
            k.params_in.mark_dma(sp.dma_start(wr, a[w_name].rearrange("p (c e) -> p c e", c=C)))
            if bias_name:
                k.params_in.mark_dma(sp.dma_start(bias, a[bias_name][0:P, :]))
            k.feed(sp, 0)

        @block.gpsimd
        def _(pool):
            step(pool, k.pool_step, pool.memset(low, 1.0))
            k.pool_step.mark(pool.affine_select(out=low, in_=low, compare_op=ALU.is_gt, fill=0.0, base=0,
                                                pattern=[[1, X8], [-1, X8]], channel_multiplier=0))

        @block.tensor
        def _(pe):
            pe.wait_ge(k.params_in.sem, p0 + 16 * (2 if bias_name else 1))
            for t in range(T):
                for c in range(C):
                    last = pe.matmul(k.ps[0:P, 0, t * X8:(t + 1) * X8], k.xT[:, c, t * P:(t + 1) * P], wr[:, c, :],
                                     start=c == 0, stop=c == C - 1, skip_group_check=True)
            k.filled.mark(last)

        @block.vector
        def _(dve):
            def cast(v):
                return v.rearrange("p (t o) -> p t o", o=1).broadcast_to([P, T, X8])
            dve.wait_ge(k.params_in.sem, p0 + 16 * (2 if bias_name else 1))
            dve.wait_ge(k.filled.sem, f0 + 1)
            lg = k.ps[0:P, 0, 0:T * X8].rearrange("p (t e) -> p t e", t=T)
            step(dve, k.dve_step, dve.tensor_reduce(mx, lg, AX, ALU.max))
            k.dve_ready.mark(dve.tensor_tensor(sc, lg, cast(mx), ALU.subtract))
            dve.wait_ge(k.act_ready.sem, a0 + 1)
            step(dve, k.dve_step, dve.tensor_reduce(mx, sc, AX, ALU.add))
            step(dve, k.dve_step, dve.reciprocal(mx, mx))
            step(dve, k.dve_step, dve.tensor_tensor(sc, sc, cast(mx), ALU.mult))
            if bias_name:
                step(dve, k.dve_step, dve.tensor_tensor(sel, sc, bias.rearrange("p (o e) -> p o e", o=1).broadcast_to([P, T, X8]), ALU.add))
            else:
                step(dve, k.dve_step, dve.tensor_copy(sel, sc))
            dve.wait_ge(k.pool_step.sem, po0 + 2)
            for t in range(T):
                me = sel[:, t, :].rearrange("p (e o) -> p e o", o=1).broadcast_to([P, X8, X8])
                other = sel[:, t, :].rearrange("p (o e) -> p o e", o=1).broadcast_to([P, X8, X8])
                k.dve_step.mark(dve.tensor_tensor(big[:, t], other, me, ALU.is_gt))
                step(dve, k.dve_step, dve.tensor_tensor(bi2[:, t], other, me, ALU.is_equal))
                step(dve, k.dve_step, dve.tensor_tensor(bi2[:, t], bi2[:, t], low, ALU.mult))
                step(dve, k.dve_step, dve.tensor_tensor(big[:, t], big[:, t], bi2[:, t], ALU.add))
                step(dve, k.dve_step, dve.tensor_reduce(sel[:, t, :], big[:, t], AX, ALU.add))
            step(dve, k.dve_step, dve.tensor_scalar(sel, sel, float(top), None, ALU.is_lt))
            step(dve, k.dve_step, dve.tensor_tensor(comb, sel, sc, ALU.mult))
            if top > 1:
                step(dve, k.dve_step, dve.tensor_reduce(mx, comb, AX, ALU.add))
                step(dve, k.dve_step, dve.tensor_scalar(mx, mx, 1e-9, None, ALU.add))
                step(dve, k.dve_step, dve.reciprocal(mx, mx))
                step(dve, k.dve_step, dve.tensor_tensor(comb, comb, cast(mx), ALU.mult))

        @block.scalar
        def _(act):
            act.wait_ge(k.dve_ready.sem, r0 + 1)
            k.act_ready.mark(act.activation(sc, sc, ACT.Exp))


def swiglu_stage(k, comb):
    nc = k.nc
    hid = k.carve(128, 2, C, N)
    sg = k.carve(128, 2, N)
    HC = C
    units = [(e, half) for e in range(EXPERTS + 1) for half in range(2)]
    f0, e0, a0, h0, ff0, st0 = k.filled.n, k.emptied.n, k.act_ready.n, k.dve_for_pe.n, k.pe_step.n, k.dve_step.n
    NU = len(units)
    with nc.Block() as block:
        @block.sync
        def _(sp):
            k.feed(sp, 3 * NU)

        @block.tensor
        def _(pe):
            def down(n):
                wd = k.slab(pe).rearrange("p (c d) -> p c d", c=C)
                for t in range(T):
                    if t == 0:
                        pe.wait_ge(k.dve_for_pe.sem, h0 + HC * (n + 1))
                    q = n * T + t
                    if q >= 2:
                        pe.wait_ge(k.dve_step.sem, st0 + q - 1)
                    last = node_major(pe, k.ps[:, 2 + q % 2, :], lambda c: hid[:, n % 2, c, t * P:(t + 1) * P], lambda c: wd[:, c, :], range(C))
                    if t == T - 1:
                        pass
                    k.pe_step.mark(last)
                release_slabs(k, pe, k.pe_step, 1)
            for n in range(NU):
                wg = k.slab(pe, 0).rearrange("p (c d) -> p c d", c=C)
                wu = k.slab(pe, 1).rearrange("p (c d) -> p c d", c=C)
                for f in range(HC):
                    q = n * HC + f
                    if q >= 1:
                        pe.wait_ge(k.act_ready.sem, a0 + q)
                    feature_major(pe, k.ps[:, 0, :], 128, lambda c: wg[:, c, f * 128:(f + 1) * 128], lambda c: k.xT[:, c, :], range(C)).then_inc(k.filled.sem, 1)
                    k.filled.n += 1
                    if q >= 1:
                        pe.wait_ge(k.dve_for_pe.sem, h0 + q)
                    k.filled.mark(feature_major(pe, k.ps[:, 1, :], 128, lambda c: wu[:, c, f * 128:(f + 1) * 128], lambda c: k.xT[:, c, :], range(C)))
                release_slabs(k, pe, k.filled, 2)
                down(n)

        @block.scalar
        def _(act):
            for q in range(NU * HC):
                act.wait_ge(k.filled.sem, f0 + 2 * q + 1)
                if q >= 2:
                    act.wait_ge(k.dve_for_pe.sem, h0 + q - 1)
                k.act_ready.mark(act.activation(sg[:, q % 2, :], k.ps[:, 0, 0:N], ACT.Silu))

        @block.vector
        def _(dve):
            def outputs(n):
                e = units[n][0]
                for t in range(T):
                    dve.wait_ge(k.pe_step.sem, ff0 + n * T + t + 1)
                    xt = k.x[:, t, :].rearrange("p (b f) -> p b f", b=2)
                    c = comb[:, t, e:e + 1] if e < EXPERTS else 1.0
                    if n >= 1:
                        dve.wait_ge(k.dve_step.sem, st0 + (n - 1) * T + t + 1)
                    k.dve_step.mark(dve.scalar_tensor_tensor(xt, halves(k.ps[0:P, 2 + (n * T + t) % 2, :]), c, xt, ALU.mult, ALU.add))
            for n in range(NU):
                for f in range(HC):
                    q = n * HC + f
                    dve.wait_ge(k.act_ready.sem, a0 + q + 1)
                    dve.wait_ge(k.filled.sem, f0 + 2 * q + 2)
                    if n >= 2 and f == 0:
                        dve.wait_ge(k.pe_step.sem, ff0 + (n - 1) * T)
                    k.dve_for_pe.mark(dve.tensor_tensor(hid[:, n % 2, f, :], sg[:, q % 2, :], k.ps[:, 1, 0:N], ALU.mult))
                outputs(n)


def gcn_project_stage(k, hs, dinv):
    nc = k.nc
    f0, e0, rs0 = k.filled.n, k.emptied.n, k.std_ready.n
    with nc.Block() as block:
        @block.sync
        def _(sp):
            k.feed(sp, 1)

        @block.tensor
        def _(pe):
            w = k.slab(pe).rearrange("p (c d) -> p c d", c=C)
            for t in range(T):
                wait(pe, k.emptied, e0 + t - 3 if t >= 4 else 0)
                k.filled.mark(node_major(pe, k.ps[:, t % 4, :], lambda c: k.xT[:, c, t * P:(t + 1) * P], lambda c: w[:, c, :], range(C)))
            release_slabs(k, pe, k.filled, 1)

        @block.scalar
        def _(act):
            k.std_ready.mark(act.activation(dinv, k.deg[:, :], ACT.Sqrt))

        @block.vector
        def _(dve):
            dve.wait_ge(k.std_ready.sem, rs0 + 1)
            step(dve, k.dve_step, dve.reciprocal(dinv, dinv))
            for t in range(T):
                dve.wait_ge(k.filled.sem, f0 + t + 1)
                k.emptied.mark(dve.tensor_scalar(hs[:, t, :].rearrange("p (b f) -> p b f", b=2), halves(k.ps[0:P, t % 4, :]),
                                                 dinv[:, t:t + 1], None, ALU.mult))


def gcn(k):
    a = k.a
    k.reset()
    hs = k.carve(P, T, D)
    dinv = k.carve(P, T)
    bias = k.carve(P, D)
    r = k.carve(P, D)
    for layer, b in ((0, "L2_gnn_b1"), (1, "L2_gnn_b2")):
        norm_stage(k, normalise=layer == 0)
        load_stage(k, [(bias, a[b][0:P, :])])
        gcn_project_stage(k, hs, dinv)

        def finish(dve, t, ps):
            k.emptied.mark(dve.scalar_tensor_tensor(r, ps[:, 0:D], dinv[:, t:t + 1], bias, ALU.mult, ALU.add))
            dve.wait_ge(k.emptied.sem, k.emptied.n)
            if layer == 0:
                step(dve, k.dve_step, dve.tensor_scalar(k.xn[:, t, :], r, 0.0, None, ALU.max))
            else:
                step(dve, k.dve_step, dve.tensor_tensor(k.x[:, t, :], k.x[:, t, :], r, ALU.add))
        add_scaled_stage(k, lambda i, t: k.cT[:, i, t * P:(t + 1) * P], lambda i: hs[:, i, :], 0, finish)


def sign_ffn(k):
    nc = k.nc
    norm_stage(k)
    f0, e0, a0 = k.filled.n, k.emptied.n, k.act_for_pe.n
    with nc.Block() as block:
        @block.sync
        def _(sp):
            k.feed(sp, 1)

        @block.scalar
        def _(act):
            w = k.slab(act)
            for c in range(C):
                k.act_for_pe.mark(act.activation(w[:, c * D:(c + 1) * D], w[:, c * D:(c + 1) * D], ACT.Sign))

        @block.tensor
        def _(pe):
            pe.wait_ge(k.act_for_pe.sem, a0 + C)
            w = k.slab(pe).rearrange("p (c d) -> p c d", c=C)
            for t in range(T):
                wait(pe, k.emptied, e0 + t - 3 if t >= 4 else 0)
                k.filled.mark(node_major(pe, k.ps[:, t % 4, :], lambda c: k.xT[:, c, t * P:(t + 1) * P], lambda c: w[:, c, :], range(C)))
            release_slabs(k, pe, k.filled, 1)

        @block.vector
        def _(dve):
            for t in range(T):
                dve.wait_ge(k.filled.sem, f0 + t + 1)
                xt = k.x[:, t, :].rearrange("p (b f) -> p b f", b=2)
                k.emptied.mark(dve.tensor_tensor(xt, halves(k.ps[0:P, t % 4, :]), xt, ALU.add))


def gat3(k):
    nc, a = k.nc, k.a
    norm_stage(k)
    k.reset()
    HD3 = 64
    ft = k.carve(P, T, H_L3, HD3 + 1)
    res = k.carve(P, T, D)
    asd = k.carve(P, 2, H_L3, T)
    keep = k.at
    bd = k.carve(128, 256)
    av = k.carve(P, 2, D)
    junk = k.carve(P, D)
    f0, e0, p0, s0 = k.filled.n, k.emptied.n, k.params_in.n, k.dve_ready.n
    with nc.Block() as block:
        @block.vector
        def _(dve):
            k.dve_ready.mark(dve.memset(bd, 0.0))
            k.dve_step.mark(dve.memset(ft[:, :, :, HD3:HD3 + 1], 1.0))
            dve.wait_ge(k.params_in.sem, p0 + 16 * 6)
            for t in range(T):
                for c2 in range(3):
                    n = t * 3 + c2
                    dve.wait_ge(k.filled.sem, f0 + n + 1)
                    ps = wide(k.ps[0:P, n % 4, :])[:, :, 0:256].rearrange("p b (w h f) -> p b w h f", w=2, h=2)
                    for b in range(2):
                        k.dve_step.mark(dve.tensor_copy(ft[:, t, 4 * c2 + 2 * b:4 * c2 + 2 * b + 2, 0:HD3], ps[:, b, 0]))
                    k.emptied.mark(dve.tensor_copy(res[:, t, c2 * 256:(c2 + 1) * 256].rearrange("p (b h f) -> p b h f", b=2, f=HD3), ps[:, :, 1]))
                for n in range(2):
                    dve.wait_ge(k.dve_step.sem, k.dve_step.n)
                    step(dve, k.dve_step, dve.tensor_tensor(junk.rearrange("p (h f) -> p h f", f=HD3), ft[:, t, :, 0:HD3],
                                                            av[:, n, :].rearrange("p (h f) -> p h f", f=HD3), ALU.mult))
                    step(dve, k.dve_step, dve.tensor_reduce(asd[:, n, :, t], junk.rearrange("p (h f) -> p h f", f=HD3), AX, ALU.add))

        @block.sync
        def _(sp):
            sp.wait_ge(k.dve_ready.sem, s0 + 1)
            for n, w in enumerate(("L3_gnn_W", "L3_gnn_W_res")):
                for q in range(2):
                    k.params_in.mark_dma(sp.dma_start(bd[64 * q:64 * q + 64, n * 128 + 64 * q:n * 128 + 64 * q + 64], a[w]))
            for n, v in enumerate(("L3_gnn_attn_l", "L3_gnn_attn_r")):
                k.params_in.mark_dma(sp.dma_start(av[:, n, :], a[v][0:P, :]))
            k.feed(sp, 0)

        @block.tensor
        def _(pe):
            pe.wait_ge(k.params_in.sem, p0 + 16 * 6)
            for t in range(T):
                for c2 in range(3):
                    n = t * 3 + c2
                    if n >= 4:
                        pe.wait_ge(k.emptied.sem, e0 + n - 3)
                    for b in range(2):
                        last = pe.matmul(k.ps[0:P, n % 4, b * 512:b * 512 + 256], k.xT[:, 2 * c2 + b, t * P:(t + 1) * P], bd, start=True, stop=True)
                    k.filled.mark(last)
    for h in range(H_L3):
        k.reset(keep)
        wt = k.carve(P, T, N)
        q = k.carve(P, T, HD3)
        rden = k.carve(P, T)
        pair_weights(k, asd[:, 0, h, :], asd[:, 1, h, :], wt, pair_tmp(k), False)
        f0 = k.filled.n
        with nc.Block() as block:
            @block.sync
            def _(sp):
                k.feed(sp, 0)

            @block.tensor
            def _(pe):
                for j in range(T):
                    for i in range(T):
                        last = pe.matmul(k.ps[0:P, 3, j * 65:(j + 1) * 65], wt[:, i, j * P:(j + 1) * P], ft[:, i, h, :], start=i == 0, stop=i == T - 1)
                k.filled.mark(last)

            @block.vector
            def _(dve):
                dve.wait_ge(k.filled.sem, f0 + 1)
                v = k.ps[0:P, 3, 0:T * 65].rearrange("p (t f) -> p t f", f=65)
                rd = rden.rearrange("p (t o) -> p t o", o=1)
                step(dve, k.dve_step, dve.tensor_scalar(rd, v[:, :, 64:65], 1e-16, None, ALU.max))
                step(dve, k.dve_step, dve.reciprocal(rden, rden))
                step(dve, k.dve_step, dve.tensor_tensor(q, v[:, :, 0:64], rd.broadcast_to([P, T, 64]), ALU.mult))
                step(dve, k.dve_step, dve.tensor_tensor(q, q, res[:, :, h * 64:(h + 1) * 64], ALU.add))
                xt = k.x[:, :, h * 64:(h + 1) * 64]
                k.dve_step.mark(dve.scalar_tensor_tensor(xt, q, 0.0, xt, ALU.max, ALU.add))


def ffn3(k, out):
    nc, a = k.nc, k.a
    norm_stage(k)
    k.reset()
    comb = k.carve(P, T, EXPERTS)
    keep = k.at
    route_stage(k, "L3_ffn_Wg", comb, None, 1)
    k.reset(keep)
    combT = k.carve(EXPERTS, N)
    diag = k.carve(P, 2, T * P)
    hid = k.carve(F3, EXPERTS, N)
    b1 = k.carve(F3, EXPERTS)
    b2 = k.carve(EXPERTS, D)
    f0, e0, p0, d0, a0, h0, r0, s0 = (k.filled.n, k.emptied.n, k.params_in.n, k.dve_for_pe.n, k.act_ready.n, k.pe_step.n,
                                      k.dve_ready.n, k.stored.n)
    ident = k.ident[0:P, 0:P].rearrange("p (o c) -> p o c", o=1).broadcast_to([P, T, P])
    with nc.Block() as block:
        @block.sync
        def _(sp):
            k.params_in.mark_dma(sp.dma_start(b1, a["L3_ffn_b1"]))
            k.params_in.mark_dma(sp.dma_start(b2, a["L3_ffn_b2"]))
            k.feed(sp, 3)
            rows = out.rearrange("(t p) d -> t p d", p=P)
            for t in range(T):
                sp.wait_ge(k.emptied.sem, e0 + t + 1)
                k.stored.mark_dma(sp.dma_start(rows[t], k.x[:, t, :]))
            sp.wait_ge(k.stored.sem, k.stored.n)

        marks_h = []

        @block.vector
        def _(dve):
            dve.wait_ge(k.filled.sem, f0 + 1)
            k.dve_step.mark(dve.tensor_copy(combT.rearrange("p (t c) -> p t c", t=T), tiles(k.ps[0:EXPERTS, 3, :])))
            for e in range(EXPERTS + 1):
                if e < EXPERTS:
                    if e >= 2:
                        dve.wait_ge(k.filled.sem, f0 + e)
                    k.dve_for_pe.mark(dve.tensor_tensor(diag[:, e % 2, :].rearrange("p (t c) -> p t c", t=T), ident,
                                                        comb[:, :, e:e + 1].broadcast_to([P, T, P]), ALU.mult))
                if e >= 1:
                    u = e - 1
                    dve.wait_ge(k.act_ready.sem, a0 + u + 1)
                    hv = hid[:, u, :].rearrange("p (t c) -> p t c", t=T)
                    marks_h.append(k.dve_step.mark(dve.tensor_tensor(hv, hv, tiles(k.ps[0:F3, 1, :]), ALU.mult)))
            for t in range(T):
                dve.wait_ge(k.filled.sem, f0 + 2 + EXPERTS + t)
                xt = k.x[:, t, :].rearrange("p (b f) -> p b f", b=2)
                k.emptied.mark(dve.tensor_tensor(xt, halves(k.ps[0:P, (2, 3, 0)[t % 3], :]), xt, ALU.add))
        @block.tensor
        def _(pe):
            for t in range(T):
                last = pe.transpose(k.ps[0:EXPERTS, 3, t * 128:t * 128 + P], comb[:, t, :], k.ident[0:P, 0:P])
            k.filled.mark(last)
            w1 = k.slab(pe).rearrange("p (c e f) -> p c e f", c=C, e=EXPERTS)
            for e in range(EXPERTS):
                if e >= 1:
                    pe.wait_ge(k.dve_step.sem, marks_h[e - 1])
                pe.wait_ge(k.dve_for_pe.sem, d0 + e + 1)
                for t in range(T):
                    pe.matmul(k.ps[0:F3, 1, t * 128:t * 128 + P], k.ones[0:P, 0:F3], diag[:, e % 2, t * P:(t + 1) * P], start=True, stop=True)
                k.filled.mark(feature_major(pe, k.ps[:, 0, :], F3, lambda c: w1[:, c, e, :], lambda c: k.xT[:, c, :], range(C)))
            w2 = [k.slab(pe, 1 + s).rearrange("p (c d) -> p c d", c=C) for s in range(2)]
            pe.wait_ge(k.dve_step.sem, marks_h[EXPERTS - 1])
            pe.wait_ge(k.params_in.sem, p0 + 32)
            for t in range(T):
                if t == 3:
                    pe.wait_ge(k.emptied.sem, e0 + 1)
                if t == 4:
                    pe.wait_ge(k.emptied.sem, e0 + 2)
                slot = (2, 3, 0)[t % 3]
                node_major(pe, k.ps[:, slot, :], lambda c: hid[:, c, t * P:(t + 1) * P], lambda c: w2[c // 4][0:F3, c % 4, :], range(EXPERTS), stop=False)
                k.filled.mark(node_major(pe, k.ps[:, slot, :], lambda c: combT[:, t * P:(t + 1) * P], lambda c: b2, range(1), start=False))
            release_slabs(k, pe, k.filled, 3)

        @block.scalar
        def _(act):
            act.wait_ge(k.params_in.sem, p0 + 32)
            for e in range(EXPERTS):
                act.wait_ge(k.filled.sem, f0 + 2 + e)
                k.act_ready.mark(act.activation(hid[:, e, :], k.ps[0:F3, 0, 0:N], ACT.Silu, bias=b1[:, e:e + 1]))



def network(nc, a, out, upto=99):
    with ExitStack() as ctx:
        k = Kit(nc, ctx, a)
        plan_slabs(k)
        graph_stage(k)
        done = [lambda: gat2(k), lambda: (norm_stage(k), spline_stage(k)), lambda: gat1(k), lambda: moe(k),
                lambda: gcn(k), lambda: (loops_stage(k, -1.0), sign_ffn(k)), lambda: gat3(k)]
        for n, f in enumerate(done):
            if n < upto:
                f()
        if upto >= 8:
            ffn3(k, out)
        else:
            with nc.Block() as block:
                @block.sync
                def _(sp):
                    k.stored.mark_dma(sp.dma_start(out.rearrange("(t p) d -> p t d", p=P), k.x[:, :, :]))
                    sp.wait_ge(k.stored.sem, k.stored.n)
                    for s in k.slab_in:
                        pass
                    for i in range(max(0, k.issued - RING), k.issued):
                        sp.wait_ge(k.slab_in[i % RING].sem, 16 * (i // RING + 1))


def moe(k):
    norm_stage(k)
    k.reset()
    comb = k.carve(P, T, EXPERTS)
    keep = k.at
    route_stage(k, "L1_ffn_w_router", comb, "L1_ffn_expert_bias", 2)
    k.reset(keep)
    swiglu_stage(k, comb)


def layouts(np, x):
    def chunked(w):
        i, o = w.shape
        return np.ascontiguousarray(w.reshape(i // 128, 128, o).transpose(1, 0, 2).reshape(128, -1))

    def rows(v):
        return np.ascontiguousarray(np.broadcast_to(v.reshape(1, -1), (128, v.size)))

    def cols(v):
        return np.ascontiguousarray(v.reshape(-1, 128).T)

    def halved(w):
        h = w.shape[1] // 2
        return np.concatenate([chunked(w[:, :h]), chunked(w[:, h:])], axis=1)

    o = {"x": x["x"], "src": x["src"], "dst": x["dst"]}
    for n in ("L0_gnn_W1s", "L0_gnn_W1d", "L0_gnn_Wos", "L0_gnn_Wod", "L1_gnn_W2", "L2_gnn_W1", "L2_gnn_W2"):
        o[n] = chunked(x[n])
    for n in ("L0_gnn_b1s", "L0_gnn_b1d", "L0_gnn_attn1", "L0_gnn_ln1_w", "L0_gnn_ln1_b", "L0_gnn_bos", "L0_gnn_bod", "L0_gnn_attno",
              "L0_gnn_lno_w", "L0_gnn_lno_b", "L1_gnn_a1_src", "L1_gnn_a1_dst", "L1_gnn_a2_src", "L1_gnn_a2_dst", "L1_gnn_b2",
              "L1_ffn_expert_bias", "L2_gnn_b1", "L2_gnn_b2", "L3_gnn_attn_l", "L3_gnn_attn_r"):
        o[n] = rows(x[n])
    o["L1_gnn_b1"] = cols(x["L1_gnn_b1"])
    o["L0_ffn_w1"] = np.ascontiguousarray(x["L0_ffn_w1"].reshape(64, 6, 128, 16).transpose(2, 1, 3, 0).reshape(128, -1))
    o["L0_ffn_w2"] = np.ascontiguousarray(x["L0_ffn_w2"].reshape(768, 64, 8, 2).transpose(3, 1, 2, 0).reshape(128, -1))
    o["L1_gnn_W1"] = np.concatenate([chunked(x["L1_gnn_W1"][:, h * 512:(h + 1) * 512]) for h in range(4)], axis=1)
    for n in ("L1_ffn_Wg", "L1_ffn_Wu"):
        o[n] = np.stack([halved(w.T) for w in x[n]])
    o["L1_ffn_Wd"] = np.stack([chunked(w.T) for w in x["L1_ffn_Wd"]])
    o["L1_ffn_sg"], o["L1_ffn_su"], o["L1_ffn_sd"] = halved(x["L1_ffn_sg"].T), halved(x["L1_ffn_su"].T), chunked(x["L1_ffn_sd"].T)
    o["L1_ffn_w_router"] = chunked(x["L1_ffn_w_router"].T)
    o["L2_ffn_weight"] = chunked(x["L2_ffn_weight"].T)
    o["L3_gnn_W"], o["L3_gnn_W_res"] = np.ascontiguousarray(x["L3_gnn_W"].T), np.ascontiguousarray(x["L3_gnn_W_res"].T)
    o["L3_ffn_Wg"] = chunked(x["L3_ffn_Wg"])
    o["L3_ffn_W1"] = chunked(x["L3_ffn_W1"].transpose(1, 0, 2).reshape(768, 768))
    o["L3_ffn_b1"] = np.ascontiguousarray(x["L3_ffn_b1"].T)
    o["L3_ffn_W2"] = np.ascontiguousarray(x["L3_ffn_W2"].transpose(1, 0, 2).reshape(96, -1))
    o["L3_ffn_b2"] = x["L3_ffn_b2"]
    return o


UPTO = 99


def kernel(**inputs):
    import numpy as _np
    import concourse.bacc as _bacc
    from concourse import mybir as _mybir
    from concourse.bass_utils import run_bass_kernel_spmd as _run

    nc = _bacc.Bacc("TRN2", target_bir_lowering=False, num_devices=1)
    arrays, aps = {}, {}
    for name, v in layouts(_np, {n: _np.asarray(v) for n, v in inputs.items()}).items():
        v = _np.ascontiguousarray(v)
        arrays[f"in_{name}"] = v
        aps[name] = nc.dram_tensor(f"in_{name}", v.shape, _mybir.dt.from_np(v.dtype), kind="ExternalInput").ap()
    out = nc.dram_tensor("out_0", (N, D), _mybir.dt.float32, kind="ExternalOutput").ap()
    network(nc, aps, out, UPTO)
    r = _run(nc, [arrays], core_ids=[0])
    return r.results[0]["out_0"]
```

```python
from contextlib import ExitStack

import concourse.bass as bass
from concourse import mybir

ALU = mybir.AluOpType
ACT = mybir.ActivationFunctionType
AX = mybir.AxisListType.X
F32 = mybir.dt.float32
BF16 = mybir.dt.bfloat16
I32 = mybir.dt.int32

N = 625
P = 125
T = N // P
D = 768
C = D // 128
HALF = D // 2
E = 10000
ET = E // P
RING = 3
SLAB = C * D
NEG = -1.0e30
EPS = 1e-5
SLOPE = 0.2
NCP = 16
KH = 64
KG = 4
H_L0, H_L1, H_L3 = 8, 4, 12
HID1 = 512
FF, EXPERTS = 1536, 8
SIX = 6
BLOCKS = 5
LIST = 128 * BLOCKS
F3 = 96


class Count:

    def __init__(self, sem):
        self.sem, self.n = sem, 0

    def mark(self, ins):
        ins.then_inc(self.sem, 1)
        self.n += 1
        return self.n

    def mark_dma(self, ins):
        ins.then_inc(self.sem, 16)
        self.n += 16
        return self.n


def wait(eng, count, value):
    if value > 0:
        eng.wait_ge(count.sem, value)


def step(eng, count, ins):
    eng.wait_ge(count.sem, count.mark(ins))


class Kit:

    def __init__(self, nc, ctx, a):
        self.nc, self.a = nc, a

        def sb(name, shape, dt=F32):
            return ctx.enter_context(nc.sbuf_tensor(name, shape, dt))

        def count(name):
            return Count(ctx.enter_context(nc.semaphore(name)))

        self.x = sb("x", [P, T, D])
        self.xn = sb("xn", [P, T, D])
        self.xT = sb("xT", [128, C, N])
        self.ring = sb("ring", [128, RING, SLAB])
        self.cT = sb("cT", [P, T, N])
        self.neg = sb("neg", [P, T, N])
        self.deg = sb("deg", [P, T])
        self.key = sb("key", [P, ET], I32)
        self.srci = sb("srci", [P, ET], I32)
        self.dsti = sb("dsti", [P, ET], I32)
        self.ident = sb("ident", [128, 128])
        self.ones = sb("ones", [128, 128])
        self.kcol = sb("kcol", [128, NCP])
        self.kcol2 = sb("kcol2", [128, NCP // 2])
        self.two = sb("two", [128, 1])
        self.eps = sb("eps", [128, 1])
        self.arena_words = 20600
        self.arena = sb("arena", [128, self.arena_words])
        self.ps = ctx.enter_context(nc.psum_tensor("ps", [128, 4, 1024], F32))

        self.filled = count("psum_filled")
        self.emptied = count("psum_emptied")
        self.var_ready = count("var_ready")
        self.std_ready = count("std_ready")
        self.dve_step = count("dve_step")
        self.act_step = count("act_step")
        self.pool_step = count("pool_step")
        self.pe_step = count("pe_step")
        self.act_ready = count("act_ready")
        self.dve_ready = count("dve_ready")
        self.dve_for_pe = count("dve_for_pe")
        self.act_for_pe = count("act_for_pe")
        self.params_in = count("params_in")
        self.stored = count("stored")
        self.slab_in = [count(f"slab_in{i}") for i in range(RING)]
        self.slab_free = count("slab_free")
        self.gathered = [count(f"gathered{i}") for i in range(4)]
        self.scattered = count("scattered")
        self.logits_ready = count("logits_ready")
        self.dense_in = [count(f"dense_in{i}") for i in range(2)]

        self.pe_down = count("expert_outputs")
        self.rows_turned = count("rows_turned")
        self.y_out = [[count(f"y_out{e}_{b}") for b in range(BLOCKS)] for e in range(2)]
        self.xn_d = nc.dram_tensor("xn_rows", (N, D), F32, kind="Internal").ap()
        self.y_d = nc.dram_tensor("expert_rows", (EXPERTS * LIST, D), F32, kind="Internal").ap()
        self.lists = nc.dram_tensor("expert_lists", (EXPERTS * LIST, 1), F32, kind="Internal").ap()
        self.slot = sb("slot", [P, 2, T], I32)
        self.weight = sb("weight", [P, 2, T])
        self.idx = sb("idx", [128, EXPERTS * BLOCKS], I32)
        self.need = sb("need", [1, EXPERTS], I32)
        self.slabs, self.issued, self.used = [], 0, 0
        self.fs_d = nc.dram_tensor("fs_rows", (N, D), F32, kind="Internal").ap()
        self.fd_d = nc.dram_tensor("fd_rows", (N, D), F32, kind="Internal").ap()
        self.dense = {8: nc.dram_tensor("dense_logits8", (N * N, 8), F32, kind="Internal").ap(),
                      1: nc.dram_tensor("dense_logits1", (N * N, 1), F32, kind="Internal").ap()}

    def reset(self, keep=0):
        self.at = keep

    def carve(self, parts, *shape):
        n = 1
        for s in shape:
            n *= s
        v = self.arena[0:parts, self.at:self.at + n]
        self.at += n
        assert self.at <= self.arena_words, self.at
        if len(shape) == 2:
            v = v.rearrange("p (a b) -> p a b", a=shape[0])
        elif len(shape) == 3:
            v = v.rearrange("p (a b c) -> p a b c", a=shape[0], b=shape[1])
        return v

    def feed(self, sp, uses, freed=None):
        first = self.used_before
        self.will_use = self.used_before + uses
        while self.issued < min(len(self.slabs), self.will_use + RING - 1):
            i = self.issued
            src, parts, words = self.slabs[i]
            if i >= RING and freed and i - RING >= first:
                count, value = freed(i - RING - first)
                sp.wait_ge(count.sem, value)
            elif i >= RING:
                sp.wait_ge(self.slab_free.sem, i - RING + 1)
            dst = self.ring[0:parts, i % RING, 0:words]
            self.slab_in[i % RING].mark_dma(sp.dma_start(dst, src))
            self.issued += 1
        self.used_before += uses

    def slab(self, eng, n=0):
        i = self.used + n
        eng.wait_ge(self.slab_in[i % RING].sem, 16 * (i // RING + 1))
        return self.ring[:, i % RING, :]

    def release(self, ins):
        self.slab_free.mark(ins)
        self.used += 1


def plan_slabs(k):
    a = k.a

    def add(ap, parts=128):
        k.slabs.append((ap, parts, ap.shape[1]))

    for w in ("L0_gnn_W1s", "L0_gnn_W1d", "L0_gnn_Wos", "L0_gnn_Wod"):
        add(a[w])
    for h in range(2):
        add(a["L0_ffn_w1"][:, h * 48 * KH:(h + 1) * 48 * KH])
    for h in range(2):
        add(a["L0_ffn_w2"][:, h * 4 * D:(h + 1) * 4 * D])
    for h in range(H_L1):
        add(a["L1_gnn_W1"][:, h * C * HID1:(h + 1) * C * HID1])
    for c0, c1 in ((0, 6), (6, 12), (12, 16)):
        add(a["L1_gnn_W2"][:, c0 * D:c1 * D])
    for q in range(EXPERTS + 1):
        for n in range(SIX):
            add(a["L1_ffn_shared"][n] if q == 0 else a["L1_ffn_experts"][q - 1, n])
    for w in ("L2_gnn_W1", "L2_gnn_W2", "L2_ffn_weight", "L3_ffn_W1"):
        add(a[w])
    for h in range(2):
        add(a["L3_ffn_W2"][:, h * 4 * D:(h + 1) * 4 * D], F3)
    k.used_before = 0


def halves(ap):
    return ap.rearrange("p (b f) -> p b f", b=2)[:, :, 0:HALF]


def wide(ap):
    return ap.rearrange("p (b f) -> p b f", b=2)


def tiles(ap):
    return ap.rearrange("p (t c) -> p t c", c=128)[:, 0:T, 0:P]


def graph_stage(k):
    nc, a = k.nc, k.a
    k.reset()
    iota = k.carve(P, N)
    fill = k.carve(P, 5000)
    srcf = k.carve(P, ET)
    dstf = k.carve(P, ET)
    keyf = k.carve(P, ET)
    hot = k.carve(P, 2 * 3 * N // 2 + 3).bitcast(BF16)
    hot = hot[:, 0:6 * N].rearrange("p (s w n) -> p s w n", s=3, w=2)
    filled0, emptied0 = k.filled.n, k.emptied.n
    ready0, pe0, st0, pool0 = k.dve_for_pe.n, k.pe_step.n, k.stored.n, k.pool_step.n
    dve0 = k.dve_ready.n
    counts_in = []
    with nc.Block() as block:
        @block.sync
        def _(sp):
            k.params_in.mark_dma(sp.dma_start(k.srci[:, :], a["src"].rearrange("(p t) -> p t", t=ET)))
            k.params_in.mark_dma(sp.dma_start(k.dsti[:, :], a["dst"].rearrange("(p t) -> p t", t=ET)))
            k.params_in.mark_dma(sp.dma_start(k.x[:, :, :], a["x"].rearrange("(t p) d -> p t d", p=P)))
            k.feed(sp, 0)
            sp.wait_ge(k.dve_ready.sem, dve0 + 1)
            table = k.dense[8].rearrange("(k p c) h -> k p (c h)", p=P, k=25)
            for i in range(25):
                k.stored.mark_dma(sp.dma_start(table[i], fill[:, 0:1000]))
            k.stored.mark_dma(sp.dma_start(k.dense[1].rearrange("(p c) h -> p (c h)", p=P), fill[:, 0:N * T]))
            sp.wait_ge(k.params_in.sem, k.params_in.n)
            sp.wait_ge(k.stored.sem, k.stored.n)

        @block.gpsimd
        def _(pool):
            step(pool, k.pool_step, pool.iota(iota[:, :], [[1, N]], base=0, channel_multiplier=0,
                                       allow_small_or_imprecise_dtypes=True))
            step(pool, k.pool_step, pool.memset(k.ident[:, :], 0.0))
            step(pool, k.pool_step, pool.affine_select(out=k.ident[:, :], in_=k.ident[:, :], compare_op=ALU.not_equal,
                                                fill=1.0, base=0, pattern=[[-1, 128]], channel_multiplier=1))
            step(pool, k.pool_step, pool.memset(k.ones[:, :], 1.0))
            step(pool, k.pool_step, pool.iota(k.kcol[:, :], [[-1, NCP]], base=-2, channel_multiplier=0,
                                       allow_small_or_imprecise_dtypes=True))
            step(pool, k.pool_step, pool.iota(k.kcol2[0:64, :], [[-2, NCP // 2]], base=-2, channel_multiplier=0,
                                       allow_small_or_imprecise_dtypes=True))
            step(pool, k.pool_step, pool.iota(k.kcol2[64:128, :], [[-2, NCP // 2]], base=-3, channel_multiplier=0,
                                       allow_small_or_imprecise_dtypes=True))

        @block.vector
        def _(dve):
            k.dve_ready.mark(dve.memset(fill, NEG))
            k.dve_step.mark(dve.memset(k.two[:, :], 2.0))
            k.dve_step.mark(dve.memset(k.eps[:, :], EPS))
            dve.wait_ge(k.params_in.sem, 48)
            k.dve_step.mark(dve.tensor_copy(srcf, k.srci[:, :]))
            step(dve, k.dve_step, dve.tensor_copy(dstf, k.dsti[:, :]))
            step(dve, k.dve_step, dve.scalar_tensor_tensor(keyf, dstf, float(N), srcf, ALU.mult, ALU.add))
            k.dve_step.mark(dve.tensor_copy(k.key[:, :], keyf))
            dve.wait_ge(k.pool_step.sem, pool0 + 1)
            for t in range(ET):
                if t >= 3:
                    dve.wait_ge(k.pe_step.sem, pe0 + t - 2)
                k.dve_for_pe.mark(dve.tensor_scalar(hot[:, t % 3, 0, :], iota, srcf[:, t:t + 1], None, ALU.is_equal))
                k.dve_for_pe.mark(dve.tensor_scalar(hot[:, t % 3, 1, :], iota, dstf[:, t:t + 1], None, ALU.is_equal))
            dve.wait_ge(k.filled.sem, filled0 + 1)
            for i in range(T):
                bank = k.ps[0:P, i // 2, (i % 2) * 512:(i % 2) * 512 + 512]
                k.dve_step.mark(dve.tensor_copy(k.cT[:, i, 0:500], bank[:, 0:500]))
                b = T + i // 3
                tail = k.ps[0:P, b // 2, (b % 2) * 512 + (i % 3) * P:(b % 2) * 512 + (i % 3 + 1) * P]
                k.dve_step.mark(dve.tensor_copy(k.cT[:, i, 500:625], tail))
            counts_in.append(k.dve_step.n)
            for j in range(T):
                dve.wait_ge(k.filled.sem, filled0 + 2 + j)
                k.dve_step.mark(dve.tensor_scalar(k.neg[:, j, :].rearrange("p (i s) -> p i s", i=T), tiles(k.ps[0:P, j % 4, :]),
                                                  0.0, NEG, ALU.is_equal, ALU.mult))
                k.emptied.mark(dve.tensor_reduce(k.deg[:, j:j + 1], tiles(k.ps[0:P, j % 4, :]), mybir.AxisListType.XY, ALU.add))

        @block.tensor
        def _(pe):
            for t in range(ET):
                pe.wait_ge(k.dve_for_pe.sem, ready0 + 2 * t + 2)
                for i in range(T):
                    w = hot[:, t % 3, 0, i * P:(i + 1) * P]
                    bank = k.ps[0:P, i // 2, (i % 2) * 512:(i % 2) * 512 + 512]
                    b = T + i // 3
                    tail = k.ps[0:P, b // 2, (b % 2) * 512 + (i % 3) * P:(b % 2) * 512 + (i % 3 + 1) * P]
                    pe.matmul(bank[:, 0:500], w, hot[:, t % 3, 1, 0:500], start=t == 0, stop=t == ET - 1, skip_group_check=True)
                    last = pe.matmul(tail, w, hot[:, t % 3, 1, 500:625], start=t == 0 and i % 3 == 0, stop=t == ET - 1, skip_group_check=True)
                if t < ET - 1:
                    k.pe_step.mark(last)
                else:
                    k.filled.mark(last)
            pe.wait_ge(k.pool_step.sem, pool0 + 3)
            pe.wait_ge(k.dve_step.sem, counts_in[0])
            for j in range(T):
                if j >= 4:
                    pe.wait_ge(k.emptied.sem, emptied0 + j - 3)
                for i in range(T):
                    last = pe.transpose(k.ps[0:P, j % 4, i * 128:i * 128 + P], k.cT[:, i, j * P:(j + 1) * P], k.ident[0:P, 0:P])
                k.filled.mark(last)


def row_norm(k, dve, st, src, j=0):
    k.dve_step.mark(dve.bn_stats(st[:, 0:6], src[:, 0:HALF]))
    step(dve, k.dve_step, dve.bn_stats(st[:, 6:12], src[:, HALF:D]))
    k.var_ready.mark(dve.bn_aggr(st[:, 12:14], st[:, 0:12]))


def deviation(k, act, st, nth):
    act.wait_ge(k.var_ready.sem, nth)
    k.std_ready.mark(act.activation(st[:, 14:15], st[:, 13:14], ACT.Sqrt, bias=k.eps[0:P, :]))


def norm_stage(k, normalise=True):
    nc = k.nc
    st = k.arena[0:P, k.arena_words - 80:].rearrange("p (t s) -> p t s", t=T)
    f0, e0, d0, v0, rs0 = k.filled.n, k.emptied.n, k.dve_for_pe.n, k.var_ready.n, k.std_ready.n
    with nc.Block() as block:
        @block.sync
        def _(sp):
            k.feed(sp, 0)

        @block.vector
        def _(dve):
            if normalise:
                for t in range(T):
                    row_norm(k, dve, st[:, t, :], k.x[:, t, :])
                for t in range(T):
                    dve.wait_ge(k.std_ready.sem, rs0 + t + 1)
                    step(dve, k.dve_step, dve.reciprocal(st[:, t, 14:15], st[:, t, 14:15]))
                    k.dve_for_pe.mark(dve.tensor_scalar(k.xn[:, t, :], k.x[:, t, :], st[:, t, 12:13], st[:, t, 14:15],
                                                        ALU.subtract, ALU.mult))

        @block.tensor
        def _(pe):
            if normalise:
                pe.wait_ge(k.dve_for_pe.sem, d0 + T)
            for c in range(C):
                if c >= 4:
                    pe.wait_ge(k.emptied.sem, e0 + c - 3)
                for t in range(T):
                    last = pe.transpose(k.ps[:, c % 4, t * 128:t * 128 + P], k.xn[:, t, c * 128:(c + 1) * 128], k.ident[0:P, 0:P])
                k.filled.mark(last)

        @block.scalar
        def _(act):
            if normalise:
                for t in range(T):
                    deviation(k, act, st[:, t, :], v0 + t + 1)
            for c in range(C):
                act.wait_ge(k.filled.sem, f0 + c + 1)
                k.emptied.mark(act.activation(k.xT[:, c, :].rearrange("p (t n) -> p t n", t=T), tiles(k.ps[:, c % 4, :]), ACT.Copy))


def node_major(pe, out, lhs, w, chunks, cols=D, start=True, stop=True):
    for c in chunks:
        for b in range(2):
            last = pe.matmul(out[0:P, b * 512:b * 512 + cols // 2], lhs(c), w(c)[:, b * cols // 2:(b + 1) * cols // 2],
                             start=start and c == chunks[0], stop=stop and c == chunks[-1])
    return last


def feature_major(pe, out, parts, lhs, rhs, chunks):
    for c in chunks:
        for lo, hi in ((0, 512), (512, N)):
            last = pe.matmul(out[0:parts, lo:hi], lhs(c), rhs(c)[:, lo:hi], start=c == chunks[0], stop=c == chunks[-1])
    return last


def gat2_project_stage(k, heads, bs, bd, faug):
    nc, a = k.nc, k.a
    hw = D // heads
    bias = k.carve(P, 2, D)
    fd = k.carve(P, T, D)
    f0, e0, p0 = k.filled.n, k.emptied.n, k.params_in.n
    with nc.Block() as block:
        @block.sync
        def _(sp):
            for n, b in enumerate((bs, bd)):
                k.params_in.mark_dma(sp.dma_start(bias[:, n, :], a[b][0:P, :]))
            k.feed(sp, 2)
            fs_rows = k.fs_d.rearrange("(t p) (h f) -> t p h f", p=P, h=heads)
            fd_rows = k.fd_d.rearrange("(t p) d -> t p d", p=P)
            for t in range(T):
                sp.wait_ge(k.emptied.sem, e0 + t + 1)
                k.stored.mark_dma(sp.dma_start(fs_rows[t], faug[:, t, :, 0:hw]))
            for t in range(T):
                sp.wait_ge(k.emptied.sem, e0 + T + t + 1)
                k.stored.mark_dma(sp.dma_start(fd_rows[t], fd[:, t, :]))
            sp.wait_ge(k.stored.sem, k.stored.n)

        @block.tensor
        def _(pe):
            for n in range(2):
                w = k.slab(pe).rearrange("p (c d) -> p c d", c=C)
                for t in range(T):
                    j = n * T + t
                    wait(pe, k.emptied, e0 + j - 3 if j >= 4 else 0)
                    last = node_major(pe, k.ps[:, j % 4, :], lambda c: k.xT[:, c, t * P:(t + 1) * P], lambda c: w[:, c, :], range(C))
                    k.filled.mark(last)
                nop = k.filled.n
                pe.wait_ge(k.filled.sem, nop)
                pe.sem_inc(k.slab_free.sem, 1)
                k.slab_free.n += 1
                k.used += 1

        @block.vector
        def _(dve):
            k.dve_step.mark(dve.memset(faug[:, :, :, hw:hw + 1], 1.0))
            dve.wait_ge(k.params_in.sem, p0 + 32)
            for j in range(2 * T):
                dve.wait_ge(k.filled.sem, f0 + j + 1)
                src = halves(k.ps[0:P, j % 4, :])
                b = bias[:, j // T, :].rearrange("p (b f) -> p b f", b=2)
                if j < T:
                    out = faug[:, j, :, 0:hw]
                    if heads > 1:
                        src = src.rearrange("p b (h f) -> p b h f", f=hw)
                        b = b.rearrange("p b (h f) -> p b h f", f=hw)
                        out = out.rearrange("p (b h) f -> p b h f", b=2)
                    else:
                        out = faug[:, j, 0, 0:D].rearrange("p (b f) -> p b f", b=2)
                else:
                    out = fd[:, j - T, :].rearrange("p (b f) -> p b f", b=2)
                k.emptied.mark(dve.tensor_tensor(out, src, b, ALU.add))


def gat2_edge_stage(k, heads, attn):
    nc, a = k.nc, k.a
    SL, LAG = 4, 3
    ga = k.carve(P, SL, D)
    gb = k.carve(P, SL, D)
    attn_b = k.carve(P, D)
    logit = k.carve(P, ET, heads)
    p0, s0, a0, l0, sc0 = k.params_in.n, k.dve_ready.n, k.act_ready.n, k.logits_ready.n, k.scattered.n
    g0 = [g.n for g in k.gathered]
    with nc.Block() as block:
        @block.sync
        def _(sp):
            k.params_in.mark_dma(sp.dma_start(attn_b, a[attn][0:P, :]))
            k.feed(sp, 0)

        @block.gpsimd
        def _(pool):
            for t in range(ET + LAG):
                if t < ET:
                    if t >= SL:
                        pool.wait_ge(k.logits_ready.sem, l0 + t - SL + 1)
                    for buf, rows, idx in ((ga, k.fs_d, k.srci), (gb, k.fd_d, k.dsti)):
                        k.gathered[t % SL].mark_dma(pool.indirect_dma_start(
                            buf[:, t % SL, :], None, rows, bass.IndirectOffsetOnAxis(ap=idx[:, t:t + 1], axis=0)))
                s = t - LAG
                if s >= 0:
                    pool.wait_ge(k.logits_ready.sem, l0 + s + 1)
                    wait(pool, k.scattered, k.scattered.n)
                    k.scattered.mark_dma(pool.indirect_dma_start(
                        k.dense[heads], bass.IndirectOffsetOnAxis(ap=k.key[:, s:s + 1], axis=0), logit[:, s, :], None))
            pool.wait_ge(k.scattered.sem, k.scattered.n)

        @block.vector
        def _(dve):
            dve.wait_ge(k.params_in.sem, p0 + 16)
            for u in range(ET):
                    dve.wait_ge(k.gathered[u % SL].sem, g0[u % SL] + 32 * (u // SL + 1))
                    step(dve, k.dve_step, dve.tensor_tensor(ga[:, u % SL, :], ga[:, u % SL, :], gb[:, u % SL, :], ALU.add))
                    step(dve, k.dve_step, dve.scalar_tensor_tensor(ga[:, u % SL, :], ga[:, u % SL, :], SLOPE, ga[:, u % SL, :], ALU.mult, ALU.max))
                    step(dve, k.dve_step, dve.tensor_tensor(gb[:, u % SL, :], ga[:, u % SL, :], attn_b, ALU.mult))
                    k.logits_ready.mark(dve.tensor_reduce(logit[:, u, :], gb[:, u % SL, :].rearrange("p (h f) -> p h f", h=heads), AX, ALU.add))


def gat2_dense_stage(k, heads, faug, ln_w, ln_b, last_layer):
    nc, a = k.nc, k.a
    hw = D // heads
    L = k.carve(P, 2, N * heads)
    wt = k.carve(P, 3, T * P)
    m = k.carve(P, 2, heads)
    r = k.carve(P, D)
    e = k.carve(P, D)
    lnw = k.carve(P, D)
    lnb = k.carve(P, D)
    st = k.carve(P, 16)
    rden = k.carve(P, 8)
    p0 = k.params_in.n
    in0 = [s.n for s in k.dense_in]
    neg0, exp0, tr0, wt0, agg0, e0, el0 = (k.dve_ready.n, k.act_for_pe.n, k.filled.n, k.dve_for_pe.n,
                                           k.pe_step.n, k.emptied.n, k.act_ready.n)
    v0, rs0 = k.var_ready.n, k.std_ready.n
    with nc.Block() as block:
        @block.sync
        def _(sp):
            k.params_in.mark_dma(sp.dma_start(lnw, a[ln_w][0:P, :]))
            k.params_in.mark_dma(sp.dma_start(lnb, a[ln_b][0:P, :]))
            k.feed(sp, 0)
            table = k.dense[heads].rearrange("(j p s) h -> j p (s h)", p=P, j=T)
            for j in range(T):
                if j >= 2:
                    sp.wait_ge(k.filled.sem, tr0 + heads * (j - 1))
                k.dense_in[j % 2].mark_dma(sp.dma_start(L[:, j % 2, :], table[j]))

        @block.vector
        def _(dve):
            dve.wait_ge(k.params_in.sem, p0 + 32)

            def row_max(j):
                dve.wait_ge(k.dense_in[j % 2].sem, in0[j % 2] + 16 * (j // 2 + 1))
                if j >= 2:
                    dve.wait_ge(k.act_for_pe.sem, exp0 + heads * (j - 1))
                step(dve, k.dve_step, dve.tensor_reduce(m[:, j % 2, :], L[:, j % 2, :].rearrange("p (s h) -> p h s", h=heads), AX, ALU.max))
                k.dve_ready.mark(dve.tensor_scalar(m[:, j % 2, :], m[:, j % 2, :], -1.0, None, ALU.mult))

            row_max(0)
            for j in range(T):
                for h in range(heads):
                    n = j * heads + h
                    dve.wait_ge(k.filled.sem, tr0 + n + 1)
                    if n >= 3:
                        dve.wait_ge(k.pe_step.sem, agg0 + n - 2)
                    k.dve_for_pe.mark(dve.tensor_tensor(wt[:, n % 3, :].rearrange("p (i d) -> p i d", i=T), tiles(k.ps[0:P, n % 2, :]),
                                                        k.cT[:, :, j * P:(j + 1) * P], ALU.mult))
                    if h == 0 and j + 1 < T:
                        row_max(j + 1)
                dve.wait_ge(k.pe_step.sem, agg0 + (j + 1) * heads)
                out = k.ps[0:P, 2 + j % 2, :]
                if heads == 1:
                    num = wide(out[:, :])[:, :, :]
                    den = out[:, D:D + 1]
                    step(dve, k.dve_step, dve.tensor_scalar(rden[:, 0:1], den, 1e-30, None, ALU.max))
                    step(dve, k.dve_step, dve.reciprocal(rden[:, 0:1], rden[:, 0:1]))
                    step(dve, k.dve_step, dve.tensor_scalar(r, out[:, 0:D], rden[:, 0:1], None, ALU.mult))
                else:
                    v = wide(out)[:, :, 0:4 * (hw + 1)].rearrange("p b (h f) -> p b h f", f=hw + 1)
                    rd = rden[:, :].rearrange("p (b h o) -> p b h o", b=2, o=1)
                    step(dve, k.dve_step, dve.tensor_scalar(rd, v[:, :, :, hw:hw + 1], 1e-30, None, ALU.max))
                    step(dve, k.dve_step, dve.reciprocal(rden, rden))
                    step(dve, k.dve_step, dve.tensor_tensor(r.rearrange("p (b h f) -> p b h f", b=2, f=hw), v[:, :, :, 0:hw],
                                                            rd.broadcast_to([P, 2, 4, hw]), ALU.mult))
                k.emptied.mark(dve.tensor_scalar(e, r, 0.0, None, ALU.min))
                step(dve, k.dve_step, dve.tensor_scalar(r, r, 0.0, -1.0, ALU.max, ALU.add))
                dve.wait_ge(k.act_ready.sem, el0 + j + 1)
                step(dve, k.dve_step, dve.tensor_tensor(r, r, e, ALU.add))
                if not last_layer:
                    step(dve, k.dve_step, dve.tensor_tensor(r, r, k.xn[:, j, :], ALU.add))
                row_norm(k, dve, st, r)
                dve.wait_ge(k.std_ready.sem, rs0 + j + 1)
                step(dve, k.dve_step, dve.reciprocal(st[:, 14:15], st[:, 14:15]))
                step(dve, k.dve_step, dve.tensor_scalar(r, r, st[:, 12:13], st[:, 14:15], ALU.subtract, ALU.mult))
                step(dve, k.dve_step, dve.tensor_tensor(r, r, lnw, ALU.mult))
                if last_layer:
                    step(dve, k.dve_step, dve.tensor_tensor(r, r, lnb, ALU.add))
                    step(dve, k.dve_step, dve.tensor_tensor(k.x[:, j, :], k.x[:, j, :], r, ALU.add))
                else:
                    step(dve, k.dve_step, dve.tensor_tensor(k.xn[:, j, :], r, lnb, ALU.add))

        @block.scalar
        def _(act):
            def exps(j):
                act.wait_ge(k.dve_ready.sem, neg0 + j + 1)
                for h in range(heads):
                    v = L[:, j % 2, :].rearrange("p (s h) -> p h s", h=heads)[:, h, :]
                    k.act_for_pe.mark(act.activation(v, v, ACT.Exp, bias=m[:, j % 2, h:h + 1]))
            exps(0)
            for j in range(T):
                if j + 1 < T:
                    exps(j + 1)
                act.wait_ge(k.emptied.sem, e0 + j + 1)
                k.act_ready.mark(act.activation(e, e, ACT.Exp))
                deviation(k, act, st, v0 + j + 1)

        @block.tensor
        def _(pe):
            def aggregate(n):
                j, h = n // heads, n % heads
                pe.wait_ge(k.dve_for_pe.sem, wt0 + n + 1)
                if h == 0 and j >= 2:
                    pe.wait_ge(k.emptied.sem, e0 + j - 1)
                out = k.ps[0:P, 2 + j % 2, :]
                for i in range(T):
                    w = wt[:, n % 3, i * P:(i + 1) * P]
                    if heads == 1:
                        pe.matmul(out[:, 0:512], w, faug[:, i, 0, 0:512], start=i == 0, stop=i == T - 1)
                        last = pe.matmul(out[:, 512:D + 1], w, faug[:, i, 0, 512:D + 1], start=i == 0, stop=i == T - 1)
                    else:
                        at = h // 4 * 512 + (h % 4) * (hw + 1)
                        last = pe.matmul(out[:, at:at + hw + 1], w, faug[:, i, h, :], start=i == 0, stop=i == T - 1)
                k.pe_step.mark(last)
            for n in range(T * heads):
                j, h = n // heads, n % heads
                pe.wait_ge(k.act_for_pe.sem, exp0 + n + 1)
                if n >= 2:
                    pe.wait_ge(k.dve_for_pe.sem, wt0 + n - 1)
                v = L[:, j % 2, :].rearrange("p (s h) -> p h s", h=heads)
                for i in range(T):
                    last = pe.transpose(k.ps[0:P, n % 2, i * 128:i * 128 + P], v[:, h, i * P:(i + 1) * P], k.ident[0:P, 0:P])
                k.filled.mark(last)
                if n >= 1:
                    aggregate(n - 1)
            aggregate(T * heads - 1)
    for s, n in zip(k.dense_in, in0):
        pass


def gat2(k):
    for heads, bs, bd, attn, w, b, last in ((8, "L0_gnn_b1s", "L0_gnn_b1d", "L0_gnn_attn1", "L0_gnn_ln1_w", "L0_gnn_ln1_b", False),
                                            (1, "L0_gnn_bos", "L0_gnn_bod", "L0_gnn_attno", "L0_gnn_lno_w", "L0_gnn_lno_b", True)):
        norm_stage(k, normalise=not last)
        k.reset()
        faug = k.carve(P, T, heads, D // heads + 1)
        keep = k.at
        gat2_project_stage(k, heads, bs, bd, faug)
        k.reset(keep)
        gat2_edge_stage(k, heads, attn)
        k.reset(keep)
        gat2_dense_stage(k, heads, faug, w, b, last)


RMIN, RMAX, DEGREE = -4.0, 4.0, 3
STEP_H = (RMAX - RMIN) / (NCP - DEGREE)


def spline_stage(k):
    nc, a = k.nc, k.a
    k.reset()
    G = KG * N
    u = k.carve(128, C, N)
    bufs = k.carve(128, 2, 2, G)
    sq = k.carve(128, 2, G)
    zero = k.carve(128, D)
    z0 = k.pool_step.n
    groups = [(c, g) for c in range(C) for g in range(NCP // KG)]
    NG = len(groups)
    f0, s0, b0, ba0, act0, po0, e0 = k.filled.n, k.dve_ready.n, k.act_ready.n, k.dve_for_pe.n, k.act_step.n, k.pool_step.n, k.pe_step.n
    with nc.Block() as block:
        @block.sync
        def _(sp):
            k.feed(sp, 2)
            sp.wait_ge(k.pool_step.sem, z0 + 1)
            for c in range(0, EXPERTS * BLOCKS, BLOCKS):
                k.stored.mark_dma(sp.dma_start(k.y_d.rearrange("(c p) d -> p c d", p=128)[:, c:c + BLOCKS, :],
                                               zero.rearrange("p (o d) -> p o d", o=1).broadcast_to([128, BLOCKS, D])))
            sp.wait_ge(k.stored.sem, k.stored.n)

        @block.vector
        def _(dve):
            k.dve_ready.mark(dve.tensor_scalar(u, k.xT[:, :, :], 1.0 / STEP_H, -RMIN / STEP_H + DEGREE, ALU.mult, ALU.add))
            for n in range(NG):
                A, B = bufs[:, n % 2, 0, :], bufs[:, n % 2, 1, :]
                dve.wait_ge(k.act_ready.sem, b0 + 2 * n + 1)
                if n >= 2:
                    dve.wait_ge(k.pe_step.sem, e0 + n - 1)
                k.dve_ready.mark(dve.tensor_scalar(B, A, -1.0, 0.0, ALU.add, ALU.max))
                dve.wait_ge(k.act_ready.sem, b0 + 2 * n + 2)
                step(dve, k.dve_step, dve.scalar_tensor_tensor(B, sq[:, 1, :], -4.0, B, ALU.mult, ALU.mult))
                dve.wait_ge(k.pool_step.sem, po0 + n + 2)
                k.dve_for_pe.mark(dve.tensor_tensor(B, A, B, ALU.add))

        @block.scalar
        def _(act):
            act.wait_ge(k.dve_ready.sem, s0 + 1)
            for n, (c, g) in enumerate(groups):
                A, B = bufs[:, n % 2, 0, :], bufs[:, n % 2, 1, :]
                if n >= 2:
                    act.wait_ge(k.dve_for_pe.sem, ba0 + n - 1)
                for i in range(KG):
                    kk = g * KG + i
                    k.act_step.mark(act.activation(A[:, i * N:(i + 1) * N], u[:, c, :], ACT.Abs, bias=k.kcol[:, kk:kk + 1]))
                act.wait_ge(k.act_step.sem, k.act_step.n)
                k.act_ready.mark(act.activation(A, A, ACT.Relu, bias=k.two[:, :], scale=-1.0))
                if n >= 1:
                    act.wait_ge(k.pool_step.sem, po0 + n + 1)
                act.wait_ge(k.act_ready.sem, k.act_ready.n)
                k.act_step.mark(act.activation(sq[:, 0, :], A, ACT.Square))
                act.wait_ge(k.dve_ready.sem, s0 + 2 + n)
                if n >= 1:
                    act.wait_ge(k.dve_for_pe.sem, ba0 + n)
                k.act_ready.mark(act.activation(sq[:, 1, :], B, ACT.Square))

        @block.gpsimd
        def _(pool):
            step(pool, k.pool_step, pool.memset(zero, 0.0))
            for n in range(NG):
                A = bufs[:, n % 2, 0, :]
                pool.wait_ge(k.act_step.sem, act0 + (KG + 1) * (n + 1))
                pool.wait_ge(k.dve_ready.sem, s0 + 2 + n)
                k.pool_step.mark(pool.tensor_tensor(A, A, sq[:, 0, :], ALU.mult))

        @block.tensor
        def _(pe):
            for n, (c, g) in enumerate(groups):
                if n % 12 == 0:
                    w = k.slab(pe).rearrange("p (g k o) -> p g k o", k=KG, o=KH)
                pe.wait_ge(k.dve_for_pe.sem, ba0 + n + 1)
                B = bufs[:, n % 2, 1, :]
                for i in range(KG):
                    for lo, hi in ((0, 512), (512, N)):
                        last = pe.matmul(k.ps[0:KH, 0, lo:hi], w[:, n % 12, i, :], B[:, i * N + lo:i * N + hi],
                                         start=n == 0 and i == 0, stop=n == NG - 1 and i == KG - 1)
                k.pe_step.mark(last)
                if n % 12 == 11:
                    pe.wait_ge(k.pe_step.sem, k.pe_step.n)
                    pe.sem_inc(k.slab_free.sem, 1)
                    k.slab_free.n += 1
                    k.used += 1
            k.filled.n += 0
    k.reset()
    u2 = k.carve(128, N)
    A = k.carve(128, 8, N)
    B = k.carve(128, 8, N)
    S = k.carve(128, 8, N)
    f0, e0, ba0, a0 = k.filled.n, k.emptied.n, k.dve_for_pe.n, k.act_ready.n
    dr0 = k.dve_ready.n
    with nc.Block() as block:
        @block.sync
        def _(sp):
            k.feed(sp, 2)

        @block.scalar
        def _(act):
            act.wait_ge(k.dve_ready.sem, dr0 + 2)
            for i in range(8):
                k.act_step.mark(act.activation(A[:, i, :], u2, ACT.Abs, bias=k.kcol2[:, i:i + 1]))
            act.wait_ge(k.act_step.sem, k.act_step.n)
            k.act_ready.mark(act.activation(A, A, ACT.Relu, bias=k.two[:, :], scale=-1.0))
            act.wait_ge(k.act_ready.sem, k.act_ready.n)
            k.act_ready.mark(act.activation(S, A, ACT.Square))

        @block.vector
        def _(dve):
            for half in range(2):
                k.dve_ready.mark(dve.tensor_scalar(u2[half * 64:half * 64 + 64, :], k.ps[0:KH, 0, 0:N], 1.0 / (6.0 * STEP_H),
                                                   -RMIN / STEP_H + DEGREE, ALU.mult, ALU.add))
            dve.wait_ge(k.act_ready.sem, a0 + 1)
            step(dve, k.dve_step, dve.tensor_scalar(B, A, -1.0, 0.0, ALU.add, ALU.max))
            dve.wait_ge(k.act_ready.sem, a0 + 2)
            step(dve, k.dve_step, dve.tensor_tensor(A, S, A, ALU.mult))
            step(dve, k.dve_step, dve.tensor_tensor(S, B, B, ALU.mult))
            step(dve, k.dve_step, dve.scalar_tensor_tensor(B, S, -4.0, B, ALU.mult, ALU.mult))
            k.dve_for_pe.mark(dve.tensor_tensor(B, A, B, ALU.add))
            for t in range(T):
                dve.wait_ge(k.filled.sem, f0 + t + 1)
                xt = k.x[:, t, :].rearrange("p (b f) -> p b f", b=2)
                k.emptied.mark(dve.scalar_tensor_tensor(xt, halves(k.ps[0:P, t % 4, :]), 1.0 / 6.0, xt, ALU.mult, ALU.add))

        @block.tensor
        def _(pe):
            pe.wait_ge(k.dve_for_pe.sem, ba0 + 1)
            w = [k.slab(pe, s).rearrange("p (c d) -> p c d", c=C) for s in range(2)]
            for t in range(T):
                wait(pe, k.emptied, e0 + t - 3 if t >= 4 else 0)
                last = node_major(pe, k.ps[:, t % 4, :], lambda c: B[:, c, t * P:(t + 1) * P], lambda c: w[c // 4][:, c % 4, :], range(8))
                k.filled.mark(last)
            pe.wait_ge(k.filled.sem, k.filled.n)
            pe.sem_inc(k.slab_free.sem, 2)
            k.slab_free.n += 2
            k.used += 2


def pair_weights(k, as_col, ad_col, wt, tmp, loops):
    nc = k.nc
    diag, junk, cols = tmp["diag"], tmp["junk"], tmp["cols"]
    mx, pc, qc, as2 = cols[:, 0, :], cols[:, 1, :], cols[:, 2, :], cols[:, 3, :]
    ident = k.ident[0:P, 0:P].rearrange("p (o c) -> p o c", o=1).broadcast_to([P, T, P])
    d0, f0, a0, r0 = k.dve_for_pe.n, k.filled.n, k.act_ready.n, k.dve_ready.n
    used = []
    with nc.Block() as block:
        @block.sync
        def _(sp):
            k.feed(sp, 0)

        @block.vector
        def _(dve):
            def spread(n, col):
                c = col.rearrange("p (t o) -> p t o", o=1).broadcast_to([P, T, P])
                k.dve_for_pe.mark(dve.tensor_tensor(diag[:, n, :].rearrange("p (t c) -> p t c", t=T), ident, c, ALU.mult))
            spread(0, as_col)
            dve.wait_ge(k.filled.sem, f0 + 1)
            for j in range(T):
                step(dve, k.dve_step, dve.tensor_tensor(junk, tiles(k.ps[0:P, 0, :]), k.neg[:, j, :].rearrange("p (t s) -> p t s", t=T), ALU.add))
                step(dve, k.dve_step, dve.tensor_reduce(mx[:, j:j + 1], junk, mybir.AxisListType.XY, ALU.max))
            if loops:
                step(dve, k.dve_step, dve.tensor_tensor(mx, mx, as_col, ALU.max))
            step(dve, k.dve_step, dve.tensor_tensor(mx, mx, ad_col, ALU.add))
            step(dve, k.dve_step, dve.scalar_tensor_tensor(mx, mx, SLOPE, mx, ALU.mult, ALU.max))
            k.dve_step.mark(dve.tensor_tensor(pc, ad_col, mx, ALU.subtract))
            k.dve_step.mark(dve.tensor_scalar(as2, as_col, SLOPE, None, ALU.mult))
            step(dve, k.dve_step, dve.scalar_tensor_tensor(qc, ad_col, SLOPE, mx, ALU.mult, ALU.subtract))
            spread(1, pc)
            spread(2, qc)
            dve.wait_ge(k.filled.sem, f0 + 2)
            for i in range(T):
                dve.wait_ge(k.act_ready.sem, a0 + 2 * i + 1)
                v = tmp["t"][:, i % 2, :].rearrange("p (t c) -> p t c", t=T)
                k.dve_ready.mark(dve.scalar_tensor_tensor(v, tiles(k.ps[0:P, 1, :]), as_col[:, i:i + 1], v, ALU.add, ALU.max))
                if i >= 1:
                    dve.wait_ge(k.act_ready.sem, a0 + 2 * i)
                    used.append(k.dve_step.mark(dve.scalar_tensor_tensor(wt[:, i - 1, :], tmp["t"][:, (i - 1) % 2, :], 1.0,
                                                                         k.cT[:, i - 1, :], ALU.min, ALU.mult)))
            dve.wait_ge(k.act_ready.sem, a0 + 2 * T)
            k.dve_step.mark(dve.scalar_tensor_tensor(wt[:, T - 1, :], tmp["t"][:, (T - 1) % 2, :], 1.0, k.cT[:, T - 1, :], ALU.min, ALU.mult))

        @block.scalar
        def _(act):
            act.wait_ge(k.filled.sem, f0 + 2)
            for i in range(T):
                if i >= 2:
                    act.wait_ge(k.dve_step.sem, used[i - 2])
                v = tmp["t"][:, i % 2, :]
                k.act_ready.mark(act.activation(v.rearrange("p (t c) -> p t c", t=T), tiles(k.ps[0:P, 2, :]), ACT.Identity, bias=as2[:, i:i + 1]))
                act.wait_ge(k.dve_ready.sem, r0 + i + 1)
                k.act_ready.mark(act.activation(v, v, ACT.Exp))

        @block.tensor
        def _(pe):
            def rows(n, slot):
                for t in range(T):
                    last = pe.matmul(k.ps[:, slot, t * 128:t * 128 + P], k.ones[0:P, :], diag[:, n, t * P:(t + 1) * P], start=True, stop=True)
                return last
            pe.wait_ge(k.dve_for_pe.sem, d0 + 1)
            k.filled.mark(rows(0, 0))
            pe.wait_ge(k.dve_for_pe.sem, d0 + 3)
            rows(1, 1)
            k.filled.mark(rows(2, 2))


def pair_tmp(k):
    flat = k.xn[:, :, :].rearrange("p t d -> p (t d)")
    tmp = {"diag": flat[:, 0:3 * N].rearrange("p (n c) -> p n c", n=3),
           "junk": flat[:, 3 * N:4 * N].rearrange("p (t c) -> p t c", t=T),
           "t": flat[:, 4 * N:6 * N].rearrange("p (n c) -> p n c", n=2),
           "cols": flat[:, 6 * N:6 * N + 4 * T].rearrange("p (n c) -> p n c", n=4)}
    return tmp


def release_slabs(k, pe, count, n):
    pe.wait_ge(count.sem, count.n)
    pe.sem_inc(k.slab_free.sem, n)
    k.slab_free.n += n
    k.used += n


def gat1_head_stage(k, h, hh, cols, src, dst, width):
    nc, a = k.nc, k.a
    av = k.carve(P, 2, width)
    junk = k.carve(P, width)
    f0, e0, p0 = k.filled.n, k.emptied.n, k.params_in.n
    second = width == D
    chunks = 16 if second else C
    with nc.Block() as block:
        @block.sync
        def _(sp):
            for n, v in enumerate((src, dst)):
                rows = a[v][0:P, 0:D] if second else a[v][0:P, h * width:(h + 1) * width]
                k.params_in.mark_dma(sp.dma_start(av[:, n, :], rows))
            k.feed(sp, 3 if second else 1)

        @block.tensor
        def _(pe):
            if second:
                w = [k.slab(pe, s).rearrange("p (c d) -> p c d", c=C) for s in range(3)]
            else:
                w = k.slab(pe)[:, 0:C * HID1].rearrange("p (c d) -> p c d", c=C)
            for t in range(T):
                wait(pe, k.emptied, e0 + t - 3 if t >= 4 else 0)
                if second:
                    last = node_major(pe, k.ps[:, t % 4, :], lambda c: k.h2T[:, c, t * P:(t + 1) * P], lambda c: w[c // 6][:, c % 6, :], range(chunks))
                else:
                    for c in range(C):
                        last = pe.matmul(k.ps[0:P, t % 4, 0:HID1], k.xT[:, c, t * P:(t + 1) * P], w[:, c, :], start=c == 0, stop=c == C - 1)
                k.filled.mark(last)
            release_slabs(k, pe, k.filled, 3 if second else 1)

        @block.scalar
        def _(act):
            for t in range(T):
                act.wait_ge(k.filled.sem, f0 + t + 1)
                if second:
                    k.emptied.mark(act.activation(hh[:, t, 0:D].rearrange("p (b f) -> p b f", b=2), halves(k.ps[0:P, t % 4, :]), ACT.Copy))
                else:
                    k.emptied.mark(act.activation(hh[:, t, 0:HID1], k.ps[0:P, t % 4, 0:HID1], ACT.Copy))

        @block.vector
        def _(dve):
            k.dve_step.mark(dve.memset(hh[:, :, width:width + 1], 1.0))
            dve.wait_ge(k.params_in.sem, p0 + 32)
            for t in range(T):
                dve.wait_ge(k.emptied.sem, e0 + t + 1)
                for n in range(2):
                    dve.wait_ge(k.dve_step.sem, k.dve_step.n)
                    k.dve_step.mark(dve.tensor_tensor_reduce(junk, hh[:, t, 0:width], av[:, n, :], 1.0, 0.0, ALU.mult, ALU.add,
                                                             cols[:, n, t:t + 1]))


def gat1_gather_stage(k, h, hh, wt):
    nc, a = k.nc, k.a
    rden = k.carve(128, N)
    r = k.carve(128, 2, N)
    e = k.carve(128, 2, N)
    bcol = k.carve(128, 4)
    f0, e0, p0, r0, a0, s0 = k.filled.n, k.emptied.n, k.params_in.n, k.dve_ready.n, k.act_ready.n, k.dve_step.n
    FC = HID1 // 128
    with nc.Block() as block:
        @block.sync
        def _(sp):
            k.params_in.mark_dma(sp.dma_start(bcol, a["L1_gnn_b1"][:, h * FC:(h + 1) * FC]))
            k.feed(sp, 0)

        @block.tensor
        def _(pe):
            k.filled.mark(feature_major(pe, k.ps[:, 3, :], 128, lambda i: k.ones[0:P, :], lambda i: wt[:, i, :], range(T)))
            for f in range(FC):
                wait(pe, k.emptied, e0 + f - 2 if f >= 3 else 0)
                k.filled.mark(feature_major(pe, k.ps[:, f % 3, :], 128, lambda i: hh[:, i, f * 128:(f + 1) * 128], lambda i: wt[:, i, :], range(T)))

        @block.vector
        def _(dve):
            dve.wait_ge(k.filled.sem, f0 + 1)
            step(dve, k.dve_step, dve.tensor_scalar(rden, k.ps[:, 3, 0:N], 1e-16, None, ALU.add))
            step(dve, k.dve_step, dve.reciprocal(rden, rden))
            dve.wait_ge(k.params_in.sem, p0 + 16)
            for f in range(FC + 1):
                if f < FC:
                    R = r[:, f % 2, :]
                    dve.wait_ge(k.filled.sem, f0 + 2 + f)
                    k.emptied.mark(dve.tensor_tensor(R, k.ps[:, f % 3, 0:N], rden, ALU.mult))
                    dve.wait_ge(k.emptied.sem, k.emptied.n)
                    step(dve, k.dve_step, dve.tensor_scalar(R, R, bcol[:, f:f + 1], None, ALU.add))
                    k.dve_ready.mark(dve.tensor_scalar(e[:, f % 2, :], R, 0.0, None, ALU.min))
                    step(dve, k.dve_step, dve.tensor_scalar(R, R, 0.0, -1.0, ALU.max, ALU.add))
                if f >= 1:
                    dve.wait_ge(k.act_ready.sem, a0 + f)
                    step(dve, k.dve_step, dve.tensor_tensor(k.h2T[:, h * FC + f - 1, :], r[:, (f - 1) % 2, :], e[:, (f - 1) % 2, :], ALU.add))

        @block.scalar
        def _(act):
            for f in range(FC):
                act.wait_ge(k.dve_ready.sem, r0 + f + 1)
                k.act_ready.mark(act.activation(e[:, f % 2, :], e[:, f % 2, :], ACT.Exp))


def add_scaled_stage(k, lhs, rhs, slabs, finish, width=D):
    nc = k.nc
    f0, e0 = k.filled.n, k.emptied.n
    with nc.Block() as block:
        @block.sync
        def _(sp):
            k.feed(sp, slabs)

        @block.tensor
        def _(pe):
            for t in range(T):
                wait(pe, k.emptied, e0 + t - 3 if t >= 4 else 0)
                for i in range(T):
                    for lo, hi in ((0, min(512, width)), (512, width)):
                        if hi > lo:
                            last = pe.matmul(k.ps[0:P, t % 4, lo:hi], lhs(i, t), rhs(i)[:, lo:hi], start=i == 0, stop=i == T - 1)
                k.filled.mark(last)

        @block.vector
        def _(dve):
            for t in range(T):
                dve.wait_ge(k.filled.sem, f0 + t + 1)
                finish(dve, t, k.ps[0:P, t % 4, :])


def gat1(k):
    nc, a = k.nc, k.a
    norm_stage(k)
    k.reset()
    k.h2T = k.carve(128, 16, N)
    hh = k.carve(P, T, HID1 + 1)
    cols = k.carve(P, 2, T)
    keep = k.at
    loops_stage(k, 1.0)
    for h in range(H_L1):
        k.reset(keep)
        gat1_head_stage(k, h, hh, cols, "L1_gnn_a1_src", "L1_gnn_a1_dst", HID1)
        k.reset(keep)
        wt = k.carve(P, T, N)
        pair_weights(k, cols[:, 0, :], cols[:, 1, :], wt, pair_tmp(k), True)
        gat1_gather_stage(k, h, hh, wt)
    k.reset(16 * N)
    hh = k.carve(P, T, D + 1)
    cols = k.carve(P, 2, T)
    keep = k.at
    gat1_head_stage(k, 0, hh, cols, "L1_gnn_a2_src", "L1_gnn_a2_dst", D)
    k.reset(0)
    wt = k.carve(P, T, N)
    b2 = k.carve(P, D)
    r = k.carve(P, D)
    rden = k.carve(P, 1)
    pair_weights(k, cols[:, 0, :], cols[:, 1, :], wt, pair_tmp(k), True)
    load_stage(k, [(b2, a["L1_gnn_b2"][0:P, :])])

    def finish(dve, t, ps):
        step(dve, k.dve_step, dve.tensor_scalar(rden, ps[:, D:D + 1], 1e-16, None, ALU.add))
        step(dve, k.dve_step, dve.reciprocal(rden, rden))
        k.emptied.mark(dve.scalar_tensor_tensor(r, ps[:, 0:D], rden, b2, ALU.mult, ALU.add))
        dve.wait_ge(k.emptied.sem, k.emptied.n)
        step(dve, k.dve_step, dve.tensor_tensor(k.x[:, t, :], k.x[:, t, :], r, ALU.add))
    add_scaled_stage(k, lambda i, t: wt[:, i, t * P:(t + 1) * P], lambda i: hh[:, i, :], 0, finish, D + 1)


def load_stage(k, loads):
    with k.nc.Block() as block:
        @block.sync
        def _(sp):
            for dst, src in loads:
                k.params_in.mark_dma(sp.dma_start(dst, src))
            sp.wait_ge(k.params_in.sem, k.params_in.n)
            k.feed(sp, 0)


def loops_stage(k, sign):
    with k.nc.Block() as block:
        @block.vector
        def _(dve):
            for t in range(T):
                d = k.cT[:, t, t * P:(t + 1) * P]
                k.dve_step.mark(dve.scalar_tensor_tensor(d, k.ident[0:P, 0:P], sign, d, ALU.mult, ALU.add))
            k.dve_step.mark(dve.tensor_scalar(k.deg[:, :], k.deg[:, :], sign, None, ALU.add))


def route_stage(k, w_name, comb, bias_name, top, rank=None):
    nc, a = k.nc, k.a
    X8 = EXPERTS
    wr = k.carve(128, C, X8)
    sc = k.carve(P, T, X8)
    sel = k.carve(P, T, X8)
    big = k.carve(P, T, X8, X8)
    bi2 = k.carve(P, T, X8, X8)
    low = k.carve(P, X8, X8)
    mx = k.carve(P, T)
    bias = k.carve(P, X8)
    f0, p0, r0, a0 = k.filled.n, k.params_in.n, k.dve_ready.n, k.act_ready.n
    po0 = k.pool_step.n
    with nc.Block() as block:
        @block.sync
        def _(sp):
            k.params_in.mark_dma(sp.dma_start(wr, a[w_name].rearrange("p (c e) -> p c e", c=C)))
            if bias_name:
                k.params_in.mark_dma(sp.dma_start(bias, a[bias_name][0:P, :]))
            k.feed(sp, 0)

        @block.gpsimd
        def _(pool):
            step(pool, k.pool_step, pool.memset(low, 1.0))
            k.pool_step.mark(pool.affine_select(out=low, in_=low, compare_op=ALU.is_gt, fill=0.0, base=0,
                                                pattern=[[1, X8], [-1, X8]], channel_multiplier=0))

        @block.tensor
        def _(pe):
            pe.wait_ge(k.params_in.sem, p0 + 16 * (2 if bias_name else 1))
            for t in range(T):
                for c in range(C):
                    last = pe.matmul(k.ps[0:P, 0, t * X8:(t + 1) * X8], k.xT[:, c, t * P:(t + 1) * P], wr[:, c, :],
                                     start=c == 0, stop=c == C - 1, skip_group_check=True)
            k.filled.mark(last)

        @block.vector
        def _(dve):
            def cast(v):
                return v.rearrange("p (t o) -> p t o", o=1).broadcast_to([P, T, X8])
            dve.wait_ge(k.params_in.sem, p0 + 16 * (2 if bias_name else 1))
            dve.wait_ge(k.filled.sem, f0 + 1)
            lg = k.ps[0:P, 0, 0:T * X8].rearrange("p (t e) -> p t e", t=T)
            step(dve, k.dve_step, dve.tensor_reduce(mx, lg, AX, ALU.max))
            k.dve_ready.mark(dve.tensor_tensor(sc, lg, cast(mx), ALU.subtract))
            dve.wait_ge(k.act_ready.sem, a0 + 1)
            step(dve, k.dve_step, dve.tensor_reduce(mx, sc, AX, ALU.add))
            step(dve, k.dve_step, dve.reciprocal(mx, mx))
            step(dve, k.dve_step, dve.tensor_tensor(sc, sc, cast(mx), ALU.mult))
            if bias_name:
                step(dve, k.dve_step, dve.tensor_tensor(sel, sc, bias.rearrange("p (o e) -> p o e", o=1).broadcast_to([P, T, X8]), ALU.add))
            else:
                step(dve, k.dve_step, dve.tensor_copy(sel, sc))
            dve.wait_ge(k.pool_step.sem, po0 + 2)
            for t in range(T):
                me = sel[:, t, :].rearrange("p (e o) -> p e o", o=1).broadcast_to([P, X8, X8])
                other = sel[:, t, :].rearrange("p (o e) -> p o e", o=1).broadcast_to([P, X8, X8])
                k.dve_step.mark(dve.tensor_tensor(big[:, t], other, me, ALU.is_gt))
                step(dve, k.dve_step, dve.tensor_tensor(bi2[:, t], other, me, ALU.is_equal))
                step(dve, k.dve_step, dve.tensor_tensor(bi2[:, t], bi2[:, t], low, ALU.mult))
                step(dve, k.dve_step, dve.tensor_tensor(big[:, t], big[:, t], bi2[:, t], ALU.add))
                step(dve, k.dve_step, dve.tensor_reduce(sel[:, t, :], big[:, t], AX, ALU.add))
            if rank is not None:
                k.dve_step.mark(dve.tensor_copy(rank, sel))
            step(dve, k.dve_step, dve.tensor_scalar(sel, sel, float(top), None, ALU.is_lt))
            step(dve, k.dve_step, dve.tensor_tensor(comb, sel, sc, ALU.mult))
            if top > 1:
                step(dve, k.dve_step, dve.tensor_reduce(mx, comb, AX, ALU.add))
                step(dve, k.dve_step, dve.tensor_scalar(mx, mx, 1e-9, None, ALU.add))
                step(dve, k.dve_step, dve.reciprocal(mx, mx))
                step(dve, k.dve_step, dve.tensor_tensor(comb, comb, cast(mx), ALU.mult))

        @block.scalar
        def _(act):
            act.wait_ge(k.dve_ready.sem, r0 + 1)
            k.act_ready.mark(act.activation(sc, sc, ACT.Exp))


def dispatch_stage(k, rank, comb, slot, weight, idx, need):
    nc = k.nc
    X8 = EXPERTS
    mask = k.carve(P, T, X8)
    pos = k.carve(P, T, X8)
    pick = k.carve(P, 2, T * X8)
    base = k.carve(P, X8)
    tri = k.carve(P, P)
    node = k.carve(P, T)
    zero = k.carve(128, EXPERTS * BLOCKS)
    slotf = k.carve(P, 2, T)
    listed = k.carve(EXPERTS * BLOCKS, 128)
    r0, f0, po0, st0, sc0, p0, x0 = k.dve_for_pe.n, k.filled.n, k.pool_step.n, k.stored.n, k.scattered.n, k.params_in.n, k.dve_ready.n
    with nc.Block() as block:
        @block.sync
        def _(sp):
            k.stored.mark_dma(sp.dma_start(k.xn_d.rearrange("(t p) d -> p t d", p=P), k.xn[:, :, :]))
            sp.wait_ge(k.pool_step.sem, po0 + 1)
            k.stored.mark_dma(sp.dma_start(k.lists.rearrange("(p c) o -> p (c o)", p=128), zero))
            sp.wait_ge(k.stored.sem, k.stored.n)
            sp.wait_ge(k.scattered.sem, sc0 + 16 * 2 * T)
            k.params_in.mark_dma(sp.dma_start(listed, k.lists.rearrange("(c p) o -> c (p o)", p=128)))
            k.feed(sp, 0)

        @block.gpsimd
        def _(pool):
            step(pool, k.pool_step, pool.memset(zero, 0.0))
            step(pool, k.pool_step, pool.iota(node, [[P, T]], base=0, channel_multiplier=1, allow_small_or_imprecise_dtypes=True))
            step(pool, k.pool_step, pool.iota(base, [[LIST, X8]], base=0, channel_multiplier=0, allow_small_or_imprecise_dtypes=True))
            step(pool, k.pool_step, pool.memset(tri, 1.0))
            step(pool, k.pool_step, pool.affine_select(out=tri, in_=tri, compare_op=ALU.is_gt, fill=0.0, base=0,
                                                       pattern=[[1, P]], channel_multiplier=-1))
            pool.wait_ge(k.dve_ready.sem, x0 + 1)
            pool.wait_ge(k.stored.sem, st0 + 32)
            for c in range(2):
                for t in range(T):
                    k.scattered.mark_dma(pool.indirect_dma_start(
                        k.lists, bass.IndirectOffsetOnAxis(ap=slot[:, c, t:t + 1], axis=0), node[:, t:t + 1], None))
            pool.wait_ge(k.scattered.sem, k.scattered.n)

        @block.vector
        def _(dve):
            k.dve_for_pe.mark(dve.tensor_scalar(mask, rank, 2.0, None, ALU.is_lt))
            dve.wait_ge(k.filled.sem, f0 + 1)
            dve.wait_ge(k.pool_step.sem, po0 + 3)
            k.dve_step.mark(dve.tensor_copy(need[0:1, :], k.ps[0:1, 1, 0:X8]))
            step(dve, k.dve_step, dve.tensor_tensor(pos, k.ps[0:P, 0, 0:T * X8].rearrange("p (t e) -> p t e", t=T),
                                                    base.rearrange("p (o e) -> p o e", o=1).broadcast_to([P, T, X8]), ALU.add))
            for c in range(2):
                a, b = (pick[:, i, :].rearrange("p (t e) -> p t e", t=T) for i in range(2))
                step(dve, k.dve_step, dve.tensor_scalar(a, rank, float(c), None, ALU.is_equal))
                step(dve, k.dve_step, dve.tensor_tensor(b, a, pos, ALU.mult))
                step(dve, k.dve_step, dve.tensor_reduce(slotf[:, c, :], b, AX, ALU.add))
                step(dve, k.dve_step, dve.tensor_tensor(b, a, comb, ALU.mult))
                step(dve, k.dve_step, dve.tensor_reduce(weight[:, c, :], b, AX, ALU.add))
            k.dve_ready.mark(dve.tensor_copy(slot, slotf))
            dve.wait_ge(k.filled.sem, f0 + 2)
            k.dve_step.mark(dve.tensor_copy(idx, k.ps[:, 2, 0:EXPERTS * BLOCKS]))

        @block.tensor
        def _(pe):
            pe.wait_ge(k.dve_for_pe.sem, r0 + 1)
            pe.wait_ge(k.pool_step.sem, po0 + 5)
            for t in range(T):
                for i in range(t + 1):
                    pe.matmul(k.ps[0:P, 0, t * X8:(t + 1) * X8], k.ones[0:P, 0:P] if i < t else tri, mask[:, i, :],
                              start=i == 0, stop=i == t, skip_group_check=True)
            for i in range(T):
                last = pe.matmul(k.ps[0:1, 1, 0:X8], k.ones[0:P, 0:1], mask[:, i, :], start=i == 0, stop=i == T - 1)
            k.filled.mark(last)
            pe.wait_ge(k.params_in.sem, p0 + 16)
            k.filled.mark(pe.transpose(k.ps[:, 2, 0:EXPERTS * BLOCKS], listed, k.ident[0:EXPERTS * BLOCKS, 0:EXPERTS * BLOCKS]))


def either(eng, cond, counts, work):
    if cond is None:
        work()
        return
    before = [c.n for c in counts]
    with eng.If(cond):
        work()
    with eng.Else():
        for c, n in zip(counts, before):
            wait(eng, c, n)
            eng.sem_inc(c.sem, c.n - n)


def experts_stage(k, slot, weight, idx, need):
    nc = k.nc
    HS = FF // SIX
    XT = k.carve(128, 2, BLOCKS * C * 128)
    Y = k.carve(128, 2, BLOCKS * D)
    rows = k.carve(128, 2, D)
    sg = k.carve(128, 2, HS)
    hid = k.carve(128, 2, HS)
    hidT = k.carve(128, 2, HS)
    units = [(q, s, b) for q in range(EXPERTS + 1) for s in range(SIX) for b in range(BLOCKS)]
    NU = len(units)
    up, tr, down, silu, hidden, copied, added = (k.filled, k.pe_step, k.pe_down, k.act_ready, k.dve_for_pe, k.act_for_pe, k.emptied)
    up0, tr0, down0, silu0, hidden0, copied0, added0 = (c.n for c in (up, tr, down, silu, hidden, copied, added))
    turned, xt_ready = k.rows_turned, k.act_step
    turned0, xt0 = turned.n, xt_ready.n
    in0 = [g.n for g in k.gathered]
    take0 = k.dve_ready.n
    
    psum_up = [k.ps[:, 0, 0:512], k.ps[:, 0, 512:1024]]
    psum_tr = [k.ps[:, 1, 0:2 * 128], k.ps[:, 1, 512:512 + 2 * 128]]

    def parts(q):
        return P if q == 0 else 128

    def reach(eng):
        return [eng.value_load(need[0:1, e:e + 1]) for e in range(EXPERTS)]

    def cond(lengths, q, b):
        return None if q == 0 else lengths[q - 1] > 128 * b

    with nc.Block() as block:
        @block.sync
        def _(sp):
            k.feed(sp, SIX * (EXPERTS + 1), lambda i: (down, down0 + BLOCKS * (i + 1)))

        @block.gpsimd
        def _(pool):
            for q in range(EXPERTS):
                if True:
                    for b in range(BLOCKS):
                        g = q * BLOCKS + b

                        def gather():
                            if g >= 2:
                                pool.wait_ge(turned.sem, turned0 + g - 1)
                            k.gathered[g % 2].mark_dma(pool.indirect_dma_start(
                                rows[:, g % 2, :], None, k.xn_d, bass.IndirectOffsetOnAxis(ap=idx[:, g:g + 1], axis=0)))
                        gather()
            for b in range(BLOCKS):
                for e in range(2):
                    pool.wait_ge(k.y_out[e][b].sem, 16 * EXPERTS // 2)
            for n in range(2 * T):
                if n >= 2:
                    pool.wait_ge(k.dve_ready.sem, take0 + n - 1)
                k.gathered[n % 2].mark_dma(pool.indirect_dma_start(
                    rows[0:P, n % 2, :], None, k.y_d, bass.IndirectOffsetOnAxis(ap=slot[:, n // T, n % T:n % T + 1], axis=0)))

        @block.tensor
        def _(pe):
            n_list = reach(pe)
            slab = None
            for n in range(NU + 2):
                if n < NU:
                    q, s, b = units[n]
                    M = parts(q)
                    if b == 0:
                        slab = k.slab(pe, q * SIX + s)
                    w = slab[:, 0:C * 2 * HS].rearrange("p (c f) -> p c f", c=C)

                    def up_work():
                        if s == 0 and q > 0:
                            pe.wait_ge(xt_ready.sem, xt0 + (q - 1) * BLOCKS + b + 1)
                        if n >= 2:
                            pe.wait_ge(hidden.sem, hidden0 + n - 1)
                        for c in range(C):
                            x = k.xT[:, c, b * P:(b + 1) * P] if q == 0 else XT[:, q % 2, (b * C + c) * 128:(b * C + c + 1) * 128]
                            last = pe.matmul(psum_up[n % 2][0:M, :], x, w[:, c, :], start=c == 0, stop=c == C - 1)
                        up.mark(last)
                    either(pe, cond(n_list, q, b), [up], up_work)
                if 1 <= n <= NU:
                    m = n - 1
                    q, s, b = units[m]
                    M = parts(q)

                    def turn_work():
                        pe.wait_ge(hidden.sem, hidden0 + m + 1)
                        if m >= 2:
                            pe.wait_ge(copied.sem, copied0 + m - 1)
                        for i in range(2):
                            last = pe.transpose(psum_tr[m % 2][:, i * 128:i * 128 + M], hid[0:M, m % 2, i * 128:(i + 1) * 128], k.ident[0:M, 0:M])
                        tr.mark(last)
                    either(pe, cond(n_list, q, b), [tr], turn_work)
                if n >= 2:
                    m = n - 2
                    q, s, b = units[m]
                    M = parts(q)
                    wd = k.ring[:, (k.used + q * SIX + s) % RING, C * 2 * HS:].rearrange("p (i d) -> p i d", i=2)

                    def down_work():
                        pe.wait_ge(copied.sem, copied0 + m + 1)
                        if m >= 1:
                            pe.wait_ge(added.sem, added0 + m)
                        for i in range(2):
                            for h in range(2):
                                last = pe.matmul(k.ps[0:M, 2, h * 512:h * 512 + HALF], hidT[:, m % 2, i * 128:i * 128 + M], wd[:, i, h * HALF:(h + 1) * HALF],
                                                 start=i == 0, stop=i == 1)
                        down.mark(last)
                    either(pe, cond(n_list, q, b), [down], down_work)
                if n < NU:
                    q, s, b = units[n]
                    if b == BLOCKS - 1 and s < BLOCKS and q < EXPERTS:
                        g = q * BLOCKS + s
                        pe.wait_ge(k.gathered[g % 2].sem, in0[g % 2] + 16 * (g // 2 + 1))

                        def rows_work():
                            wait(pe, xt_ready, xt0 + g if g else 0)
                            for c in range(C):
                                last = pe.transpose(k.ps[:, 3, c * 128:(c + 1) * 128], rows[:, g % 2, c * 128:(c + 1) * 128], k.ident[:, :])
                            turned.mark(last)
                        either(pe, cond(n_list, q + 1, s), [turned], rows_work)
            pe.wait_ge(down.sem, down.n)
            pe.sem_inc(k.slab_free.sem, SIX * (EXPERTS + 1))
            k.slab_free.n += SIX * (EXPERTS + 1)
            k.used += SIX * (EXPERTS + 1)

        @block.scalar
        def _(act):
            n_list = reach(act)

            def write_rows(q):
                for b in range(BLOCKS):
                    def write():
                        act.wait_ge(added.sem, added0 + (q * SIX + SIX - 1) * BLOCKS + b + 1)
                        r = (q - 1) * LIST + b * 128
                        wait(act, k.y_out[q % 2][b], k.y_out[q % 2][b].n)
                        k.y_out[q % 2][b].mark_dma(act.dma_start(k.y_d[r:r + 128, :], Y[:, q % 2, b * D:(b + 1) * D]))
                    either(act, cond(n_list, q, b), [k.y_out[q % 2][b]], write)

            for n in range(NU + 1):
                if n % (SIX * BLOCKS) == BLOCKS and n > 2 * BLOCKS + SIX * BLOCKS:
                    write_rows(n // (SIX * BLOCKS) - 1)
                if n < NU:
                    q, s, b = units[n]
                    M = parts(q)

                    def silu_work():
                        act.wait_ge(up.sem, up0 + n + 1)
                        if n >= 2:
                            act.wait_ge(hidden.sem, hidden0 + n - 1)
                        silu.mark(act.activation(sg[0:M, n % 2, :], psum_up[n % 2][0:M, 0:HS], ACT.Silu))
                    either(act, cond(n_list, q, b), [silu], silu_work)
                if n >= 1:
                    m = n - 1
                    q, s, b = units[m]
                    M = parts(q)

                    def copy_work():
                        act.wait_ge(tr.sem, tr0 + m + 1)
                        if m >= 2:
                            act.wait_ge(down.sem, down0 + m - 1)
                        o = hidT[:, m % 2, :].rearrange("p (i t) -> p i t", i=2)[:, :, 0:M]
                        copied.mark(act.activation(o, psum_tr[m % 2].rearrange("p (i t) -> p i t", i=2)[:, :, 0:M], ACT.Copy))
                    either(act, cond(n_list, q, b), [copied], copy_work)
                if n < NU:
                    q, s, b = units[n]
                    if b == BLOCKS - 1 and s < BLOCKS and q < EXPERTS:
                        g = q * BLOCKS + s

                        def xt_work():
                            act.wait_ge(turned.sem, turned0 + g + 1)
                            xt_ready.mark(act.activation(XT[:, (q + 1) % 2, s * C * 128:(s + 1) * C * 128], k.ps[:, 3, 0:C * 128], ACT.Copy))
                        either(act, cond(n_list, q + 1, s), [xt_ready], xt_work)
            write_rows(EXPERTS)

        @block.vector
        def _(dve):
            n_list = reach(dve)
            for n in range(NU + 2):
                if n < NU:
                    q, s, b = units[n]
                    M = parts(q)

                    def hidden_work():
                        dve.wait_ge(silu.sem, silu0 + n + 1)
                        if n >= 2:
                            dve.wait_ge(tr.sem, tr0 + n - 1)
                        hidden.mark(dve.tensor_tensor(hid[0:M, n % 2, :], sg[0:M, n % 2, :], psum_up[n % 2][0:M, HS:2 * HS], ALU.mult))
                    either(dve, cond(n_list, q, b), [hidden], hidden_work)
                if n >= 2:
                    m = n - 2
                    q, s, b = units[m]
                    M = parts(q)

                    def add_work():
                        dve.wait_ge(down.sem, down0 + m + 1)
                        wait(dve, added, added0 + m if m else 0)
                        out = halves(k.ps[0:M, 2, :])
                        if q == 0:
                            y = k.x[:, b, :].rearrange("p (h f) -> p h f", h=2)
                        else:
                            y = Y[:, q % 2, b * D:(b + 1) * D].rearrange("p (h f) -> p h f", h=2)
                        if q > 0 and s == 0:
                            if q >= 3:
                                dve.wait_ge(k.y_out[q % 2][b].sem, 16 * ((q - 1) // 2))
                            added.mark(dve.tensor_copy(y, out))
                        else:
                            added.mark(dve.tensor_tensor(y, y, out, ALU.add))
                    either(dve, cond(n_list, q, b), [added], add_work)
            for n in range(2 * T):
                dve.wait_ge(k.gathered[n % 2].sem, in0[n % 2] + 16 * (EXPERTS * BLOCKS // 2) + 16 * (n // 2 + 1))
                c, t = n // T, n % T
                wait(dve, k.dve_ready, k.dve_ready.n)
                k.dve_ready.mark(dve.scalar_tensor_tensor(k.x[:, t, :], rows[0:P, n % 2, :], weight[:, c, t:t + 1], k.x[:, t, :], ALU.mult, ALU.add))


def gcn_project_stage(k, hs, dinv):
    nc = k.nc
    f0, e0, rs0 = k.filled.n, k.emptied.n, k.std_ready.n
    with nc.Block() as block:
        @block.sync
        def _(sp):
            k.feed(sp, 1)

        @block.tensor
        def _(pe):
            w = k.slab(pe).rearrange("p (c d) -> p c d", c=C)
            for t in range(T):
                wait(pe, k.emptied, e0 + t - 3 if t >= 4 else 0)
                k.filled.mark(node_major(pe, k.ps[:, t % 4, :], lambda c: k.xT[:, c, t * P:(t + 1) * P], lambda c: w[:, c, :], range(C)))
            release_slabs(k, pe, k.filled, 1)

        @block.scalar
        def _(act):
            k.std_ready.mark(act.activation(dinv, k.deg[:, :], ACT.Sqrt))

        @block.vector
        def _(dve):
            dve.wait_ge(k.std_ready.sem, rs0 + 1)
            step(dve, k.dve_step, dve.reciprocal(dinv, dinv))
            for t in range(T):
                dve.wait_ge(k.filled.sem, f0 + t + 1)
                k.emptied.mark(dve.tensor_scalar(hs[:, t, :].rearrange("p (b f) -> p b f", b=2), halves(k.ps[0:P, t % 4, :]),
                                                 dinv[:, t:t + 1], None, ALU.mult))


def gcn(k):
    a = k.a
    k.reset()
    hs = k.carve(P, T, D)
    dinv = k.carve(P, T)
    bias = k.carve(P, D)
    r = k.carve(P, D)
    for layer, b in ((0, "L2_gnn_b1"), (1, "L2_gnn_b2")):
        norm_stage(k, normalise=layer == 0)
        load_stage(k, [(bias, a[b][0:P, :])])
        gcn_project_stage(k, hs, dinv)

        def finish(dve, t, ps):
            k.emptied.mark(dve.scalar_tensor_tensor(r, ps[:, 0:D], dinv[:, t:t + 1], bias, ALU.mult, ALU.add))
            dve.wait_ge(k.emptied.sem, k.emptied.n)
            if layer == 0:
                step(dve, k.dve_step, dve.tensor_scalar(k.xn[:, t, :], r, 0.0, None, ALU.max))
            else:
                step(dve, k.dve_step, dve.tensor_tensor(k.x[:, t, :], k.x[:, t, :], r, ALU.add))
        add_scaled_stage(k, lambda i, t: k.cT[:, i, t * P:(t + 1) * P], lambda i: hs[:, i, :], 0, finish)


def sign_ffn(k):
    nc = k.nc
    norm_stage(k)
    f0, e0, a0 = k.filled.n, k.emptied.n, k.act_for_pe.n
    with nc.Block() as block:
        @block.sync
        def _(sp):
            k.feed(sp, 1)

        @block.scalar
        def _(act):
            w = k.slab(act)
            for c in range(C):
                k.act_for_pe.mark(act.activation(w[:, c * D:(c + 1) * D], w[:, c * D:(c + 1) * D], ACT.Sign))

        @block.tensor
        def _(pe):
            pe.wait_ge(k.act_for_pe.sem, a0 + C)
            w = k.slab(pe).rearrange("p (c d) -> p c d", c=C)
            for t in range(T):
                wait(pe, k.emptied, e0 + t - 3 if t >= 4 else 0)
                k.filled.mark(node_major(pe, k.ps[:, t % 4, :], lambda c: k.xT[:, c, t * P:(t + 1) * P], lambda c: w[:, c, :], range(C)))
            release_slabs(k, pe, k.filled, 1)

        @block.vector
        def _(dve):
            for t in range(T):
                dve.wait_ge(k.filled.sem, f0 + t + 1)
                xt = k.x[:, t, :].rearrange("p (b f) -> p b f", b=2)
                k.emptied.mark(dve.tensor_tensor(xt, halves(k.ps[0:P, t % 4, :]), xt, ALU.add))


def gat3(k):
    nc, a = k.nc, k.a
    norm_stage(k)
    k.reset()
    HD3 = 64
    ft = k.carve(P, T, H_L3, HD3 + 1)
    res = k.carve(P, T, D)
    asd = k.carve(P, 2, H_L3, T)
    keep = k.at
    bd = k.carve(128, 256)
    av = k.carve(P, 2, D)
    junk = k.carve(P, D)
    f0, e0, p0, s0 = k.filled.n, k.emptied.n, k.params_in.n, k.dve_ready.n
    with nc.Block() as block:
        @block.vector
        def _(dve):
            k.dve_ready.mark(dve.memset(bd, 0.0))
            k.dve_step.mark(dve.memset(ft[:, :, :, HD3:HD3 + 1], 1.0))
            dve.wait_ge(k.params_in.sem, p0 + 16 * 6)
            for t in range(T):
                for c2 in range(3):
                    n = t * 3 + c2
                    dve.wait_ge(k.filled.sem, f0 + n + 1)
                    ps = wide(k.ps[0:P, n % 4, :])[:, :, 0:256].rearrange("p b (w h f) -> p b w h f", w=2, h=2)
                    for b in range(2):
                        k.dve_step.mark(dve.tensor_copy(ft[:, t, 4 * c2 + 2 * b:4 * c2 + 2 * b + 2, 0:HD3], ps[:, b, 0]))
                    k.emptied.mark(dve.tensor_copy(res[:, t, c2 * 256:(c2 + 1) * 256].rearrange("p (b h f) -> p b h f", b=2, f=HD3), ps[:, :, 1]))
                for n in range(2):
                    dve.wait_ge(k.dve_step.sem, k.dve_step.n)
                    step(dve, k.dve_step, dve.tensor_tensor(junk.rearrange("p (h f) -> p h f", f=HD3), ft[:, t, :, 0:HD3],
                                                            av[:, n, :].rearrange("p (h f) -> p h f", f=HD3), ALU.mult))
                    step(dve, k.dve_step, dve.tensor_reduce(asd[:, n, :, t], junk.rearrange("p (h f) -> p h f", f=HD3), AX, ALU.add))

        @block.sync
        def _(sp):
            sp.wait_ge(k.dve_ready.sem, s0 + 1)
            for n, w in enumerate(("L3_gnn_W", "L3_gnn_W_res")):
                for q in range(2):
                    k.params_in.mark_dma(sp.dma_start(bd[64 * q:64 * q + 64, n * 128 + 64 * q:n * 128 + 64 * q + 64], a[w]))
            for n, v in enumerate(("L3_gnn_attn_l", "L3_gnn_attn_r")):
                k.params_in.mark_dma(sp.dma_start(av[:, n, :], a[v][0:P, :]))
            k.feed(sp, 0)

        @block.tensor
        def _(pe):
            pe.wait_ge(k.params_in.sem, p0 + 16 * 6)
            for t in range(T):
                for c2 in range(3):
                    n = t * 3 + c2
                    if n >= 4:
                        pe.wait_ge(k.emptied.sem, e0 + n - 3)
                    for b in range(2):
                        last = pe.matmul(k.ps[0:P, n % 4, b * 512:b * 512 + 256], k.xT[:, 2 * c2 + b, t * P:(t + 1) * P], bd, start=True, stop=True)
                    k.filled.mark(last)
    for h in range(H_L3):
        k.reset(keep)
        wt = k.carve(P, T, N)
        q = k.carve(P, T, HD3)
        rden = k.carve(P, T)
        pair_weights(k, asd[:, 0, h, :], asd[:, 1, h, :], wt, pair_tmp(k), False)
        f0 = k.filled.n
        with nc.Block() as block:
            @block.sync
            def _(sp):
                k.feed(sp, 0)

            @block.tensor
            def _(pe):
                for j in range(T):
                    for i in range(T):
                        last = pe.matmul(k.ps[0:P, 3, j * 65:(j + 1) * 65], wt[:, i, j * P:(j + 1) * P], ft[:, i, h, :], start=i == 0, stop=i == T - 1)
                k.filled.mark(last)

            @block.vector
            def _(dve):
                dve.wait_ge(k.filled.sem, f0 + 1)
                v = k.ps[0:P, 3, 0:T * 65].rearrange("p (t f) -> p t f", f=65)
                rd = rden.rearrange("p (t o) -> p t o", o=1)
                step(dve, k.dve_step, dve.tensor_scalar(rd, v[:, :, 64:65], 1e-16, None, ALU.max))
                step(dve, k.dve_step, dve.reciprocal(rden, rden))
                step(dve, k.dve_step, dve.tensor_tensor(q, v[:, :, 0:64], rd.broadcast_to([P, T, 64]), ALU.mult))
                step(dve, k.dve_step, dve.tensor_tensor(q, q, res[:, :, h * 64:(h + 1) * 64], ALU.add))
                xt = k.x[:, :, h * 64:(h + 1) * 64]
                k.dve_step.mark(dve.scalar_tensor_tensor(xt, q, 0.0, xt, ALU.max, ALU.add))


def ffn3(k, out):
    nc, a = k.nc, k.a
    norm_stage(k)
    k.reset()
    comb = k.carve(P, T, EXPERTS)
    keep = k.at
    route_stage(k, "L3_ffn_Wg", comb, None, 1)
    k.reset(keep)
    combT = k.carve(EXPERTS, N)
    diag = k.carve(P, 2, T * P)
    hid = k.carve(F3, EXPERTS, N)
    b1 = k.carve(F3, EXPERTS)
    b2 = k.carve(EXPERTS, D)
    f0, e0, p0, d0, a0, h0, r0, s0 = (k.filled.n, k.emptied.n, k.params_in.n, k.dve_for_pe.n, k.act_ready.n, k.pe_step.n,
                                      k.dve_ready.n, k.stored.n)
    ident = k.ident[0:P, 0:P].rearrange("p (o c) -> p o c", o=1).broadcast_to([P, T, P])
    with nc.Block() as block:
        @block.sync
        def _(sp):
            k.params_in.mark_dma(sp.dma_start(b1, a["L3_ffn_b1"]))
            k.params_in.mark_dma(sp.dma_start(b2, a["L3_ffn_b2"]))
            k.feed(sp, 3)
            rows = out.rearrange("(t p) d -> t p d", p=P)
            for t in range(T):
                sp.wait_ge(k.emptied.sem, e0 + t + 1)
                k.stored.mark_dma(sp.dma_start(rows[t], k.x[:, t, :]))
            sp.wait_ge(k.stored.sem, k.stored.n)

        marks_h = []

        @block.vector
        def _(dve):
            dve.wait_ge(k.filled.sem, f0 + 1)
            k.dve_step.mark(dve.tensor_copy(combT.rearrange("p (t c) -> p t c", t=T), tiles(k.ps[0:EXPERTS, 3, :])))
            for e in range(EXPERTS + 1):
                if e < EXPERTS:
                    if e >= 2:
                        dve.wait_ge(k.filled.sem, f0 + e)
                    k.dve_for_pe.mark(dve.tensor_tensor(diag[:, e % 2, :].rearrange("p (t c) -> p t c", t=T), ident,
                                                        comb[:, :, e:e + 1].broadcast_to([P, T, P]), ALU.mult))
                if e >= 1:
                    u = e - 1
                    dve.wait_ge(k.act_ready.sem, a0 + u + 1)
                    hv = hid[:, u, :].rearrange("p (t c) -> p t c", t=T)
                    marks_h.append(k.dve_step.mark(dve.tensor_tensor(hv, hv, tiles(k.ps[0:F3, 1, :]), ALU.mult)))
            for t in range(T):
                dve.wait_ge(k.filled.sem, f0 + 2 + EXPERTS + t)
                xt = k.x[:, t, :].rearrange("p (b f) -> p b f", b=2)
                k.emptied.mark(dve.tensor_tensor(xt, halves(k.ps[0:P, (2, 3, 0)[t % 3], :]), xt, ALU.add))
        @block.tensor
        def _(pe):
            for t in range(T):
                last = pe.transpose(k.ps[0:EXPERTS, 3, t * 128:t * 128 + P], comb[:, t, :], k.ident[0:P, 0:P])
            k.filled.mark(last)
            w1 = k.slab(pe).rearrange("p (c e f) -> p c e f", c=C, e=EXPERTS)
            for e in range(EXPERTS):
                if e >= 1:
                    pe.wait_ge(k.dve_step.sem, marks_h[e - 1])
                pe.wait_ge(k.dve_for_pe.sem, d0 + e + 1)
                for t in range(T):
                    pe.matmul(k.ps[0:F3, 1, t * 128:t * 128 + P], k.ones[0:P, 0:F3], diag[:, e % 2, t * P:(t + 1) * P], start=True, stop=True)
                k.filled.mark(feature_major(pe, k.ps[:, 0, :], F3, lambda c: w1[:, c, e, :], lambda c: k.xT[:, c, :], range(C)))
            w2 = [k.slab(pe, 1 + s).rearrange("p (c d) -> p c d", c=C) for s in range(2)]
            pe.wait_ge(k.dve_step.sem, marks_h[EXPERTS - 1])
            pe.wait_ge(k.params_in.sem, p0 + 32)
            for t in range(T):
                if t == 3:
                    pe.wait_ge(k.emptied.sem, e0 + 1)
                if t == 4:
                    pe.wait_ge(k.emptied.sem, e0 + 2)
                slot = (2, 3, 0)[t % 3]
                node_major(pe, k.ps[:, slot, :], lambda c: hid[:, c, t * P:(t + 1) * P], lambda c: w2[c // 4][0:F3, c % 4, :], range(EXPERTS), stop=False)
                k.filled.mark(node_major(pe, k.ps[:, slot, :], lambda c: combT[:, t * P:(t + 1) * P], lambda c: b2, range(1), start=False))
            release_slabs(k, pe, k.filled, 3)

        @block.scalar
        def _(act):
            act.wait_ge(k.params_in.sem, p0 + 32)
            for e in range(EXPERTS):
                act.wait_ge(k.filled.sem, f0 + 2 + e)
                k.act_ready.mark(act.activation(hid[:, e, :], k.ps[0:F3, 0, 0:N], ACT.Silu, bias=b1[:, e:e + 1]))



def network(nc, a, out, upto=99):
    with ExitStack() as ctx:
        k = Kit(nc, ctx, a)
        plan_slabs(k)
        graph_stage(k)
        done = [lambda: gat2(k), lambda: (norm_stage(k), spline_stage(k)), lambda: gat1(k), lambda: moe(k),
                lambda: gcn(k), lambda: (loops_stage(k, -1.0), sign_ffn(k)), lambda: gat3(k)]
        for n, f in enumerate(done):
            if n < upto:
                f()
        if upto >= 8:
            ffn3(k, out)
        else:
            with nc.Block() as block:
                @block.sync
                def _(sp):
                    k.stored.mark_dma(sp.dma_start(out.rearrange("(t p) d -> p t d", p=P), k.x[:, :, :]))
                    sp.wait_ge(k.stored.sem, k.stored.n)
                    for s in k.slab_in:
                        pass
                    for i in range(max(0, k.issued - RING), k.issued):
                        sp.wait_ge(k.slab_in[i % RING].sem, 16 * (i // RING + 1))


def moe(k):
    norm_stage(k)
    k.reset()
    comb = k.carve(P, T, EXPERTS)
    rank = k.carve(P, T, EXPERTS)
    keep = k.at
    route_stage(k, "L1_ffn_w_router", comb, "L1_ffn_expert_bias", 2, rank)
    k.reset(keep)
    dispatch_stage(k, rank, comb, k.slot[:, :, :], k.weight[:, :, :], k.idx[:, :], k.need[:, :])
    k.reset()
    experts_stage(k, k.slot[:, :, :], k.weight[:, :, :], k.idx[:, :], k.need[:, :])


def layouts(np, x):
    def chunked(w):
        i, o = w.shape
        return np.ascontiguousarray(w.reshape(i // 128, 128, o).transpose(1, 0, 2).reshape(128, -1))

    def rows(v):
        return np.ascontiguousarray(np.broadcast_to(v.reshape(1, -1), (128, v.size)))

    def cols(v):
        return np.ascontiguousarray(v.reshape(-1, 128).T)

    def halved(w):
        h = w.shape[1] // 2
        return np.concatenate([chunked(w[:, :h]), chunked(w[:, h:])], axis=1)

    o = {"x": x["x"], "src": x["src"], "dst": x["dst"]}
    for n in ("L0_gnn_W1s", "L0_gnn_W1d", "L0_gnn_Wos", "L0_gnn_Wod", "L1_gnn_W2", "L2_gnn_W1", "L2_gnn_W2"):
        o[n] = chunked(x[n])
    for n in ("L0_gnn_b1s", "L0_gnn_b1d", "L0_gnn_attn1", "L0_gnn_ln1_w", "L0_gnn_ln1_b", "L0_gnn_bos", "L0_gnn_bod", "L0_gnn_attno",
              "L0_gnn_lno_w", "L0_gnn_lno_b", "L1_gnn_a1_src", "L1_gnn_a1_dst", "L1_gnn_a2_src", "L1_gnn_a2_dst", "L1_gnn_b2",
              "L1_ffn_expert_bias", "L2_gnn_b1", "L2_gnn_b2", "L3_gnn_attn_l", "L3_gnn_attn_r"):
        o[n] = rows(x[n])
    o["L1_gnn_b1"] = cols(x["L1_gnn_b1"])
    o["L0_ffn_w1"] = np.ascontiguousarray(x["L0_ffn_w1"].reshape(64, 6, 128, 16).transpose(2, 1, 3, 0).reshape(128, -1))
    o["L0_ffn_w2"] = np.ascontiguousarray(x["L0_ffn_w2"].reshape(768, 64, 8, 2).transpose(3, 1, 2, 0).reshape(128, -1))
    o["L1_gnn_W1"] = np.concatenate([chunked(x["L1_gnn_W1"][:, h * 512:(h + 1) * 512]) for h in range(4)], axis=1)
    def sixths(g, u, d):
        def half(w):
            return w.reshape(6, 256, 6, 128).transpose(0, 3, 2, 1)
        gu = np.concatenate([half(g), half(u)], axis=3).reshape(6, 128, -1)
        return np.concatenate([gu, d.T.reshape(6, 2, 128, 768).transpose(0, 2, 1, 3).reshape(6, 128, -1)], axis=2)

    o["L1_ffn_experts"] = np.stack([sixths(g, u, d) for g, u, d in zip(x["L1_ffn_Wg"], x["L1_ffn_Wu"], x["L1_ffn_Wd"])])
    o["L1_ffn_shared"] = sixths(x["L1_ffn_sg"], x["L1_ffn_su"], x["L1_ffn_sd"])
    o["L1_ffn_w_router"] = chunked(x["L1_ffn_w_router"].T)
    o["L2_ffn_weight"] = chunked(x["L2_ffn_weight"].T)
    o["L3_gnn_W"], o["L3_gnn_W_res"] = np.ascontiguousarray(x["L3_gnn_W"].T), np.ascontiguousarray(x["L3_gnn_W_res"].T)
    o["L3_ffn_Wg"] = chunked(x["L3_ffn_Wg"])
    o["L3_ffn_W1"] = chunked(x["L3_ffn_W1"].transpose(1, 0, 2).reshape(768, 768))
    o["L3_ffn_b1"] = np.ascontiguousarray(x["L3_ffn_b1"].T)
    o["L3_ffn_W2"] = np.ascontiguousarray(x["L3_ffn_W2"].transpose(1, 0, 2).reshape(96, -1))
    o["L3_ffn_b2"] = x["L3_ffn_b2"]
    return o


UPTO = 99


def kernel(**inputs):
    import numpy as _np
    import concourse.bacc as _bacc
    from concourse import mybir as _mybir
    from concourse.bass_utils import run_bass_kernel_spmd as _run

    nc = _bacc.Bacc("TRN2", target_bir_lowering=False, num_devices=1)
    arrays, aps = {}, {}
    for name, v in layouts(_np, {n: _np.asarray(v) for n, v in inputs.items()}).items():
        v = _np.ascontiguousarray(v)
        arrays[f"in_{name}"] = v
        aps[name] = nc.dram_tensor(f"in_{name}", v.shape, _mybir.dt.from_np(v.dtype), kind="ExternalInput").ap()
    out = nc.dram_tensor("out_0", (N, D), _mybir.dt.float32, kind="ExternalOutput").ap()
    network(nc, aps, out, UPTO)
    r = _run(nc, [arrays], core_ids=[0])
    return r.results[0]["out_0"]
```

```python
from contextlib import ExitStack

import concourse.bass as bass
from concourse import mybir

ALU = mybir.AluOpType
ACT = mybir.ActivationFunctionType
AX = mybir.AxisListType.X
F32 = mybir.dt.float32
BF16 = mybir.dt.bfloat16
I32 = mybir.dt.int32
I16 = mybir.dt.int16

N = 625
P = 125
T = N // P
D = 768
C = D // 128
HALF = D // 2
E = 10000
ET = E // P
RING = 3
SLAB = C * D
NEG = -1.0e30
EPS = 1e-5
SLOPE = 0.2
NCP = 16
KH = 64
KG = 2
H_L0, H_L1, H_L3 = 8, 4, 12
HID1 = 512
FF, EXPERTS = 1536, 8
SIX = 6
BLOCKS = 5
LIST = 128 * BLOCKS
F3 = 96
DW = D + 8


class Count:

    def __init__(self, sem):
        self.sem, self.n = sem, 0

    def mark(self, ins):
        ins.then_inc(self.sem, 1)
        self.n += 1
        return self.n

    def mark_dma(self, ins):
        ins.then_inc(self.sem, 16)
        self.n += 16
        return self.n


def wait(eng, count, value):
    if value > 0:
        eng.wait_ge(count.sem, value)


def step(eng, count, ins):
    eng.wait_ge(count.sem, count.mark(ins))


class Kit:

    def __init__(self, nc, ctx, a):
        self.nc, self.a = nc, a

        def sb(name, shape, dt=F32):
            return ctx.enter_context(nc.sbuf_tensor(name, shape, dt))

        def count(name):
            return Count(ctx.enter_context(nc.semaphore(name)))

        self.x = sb("x", [P, T, D])
        self.xn = sb("xn", [P, T, D])
        self.xT = sb("xT", [128, C, N])
        self.ring = sb("ring", [128, RING, SLAB])
        self.cT = sb("cT", [P, T, N])
        self.neg = sb("neg", [P, T, N])
        self.deg = sb("deg", [P, T])
        self.key = sb("key", [P, ET], I32)
        self.srci = sb("srci", [P, ET], I32)
        self.dsti = sb("dsti", [P, ET], I32)
        self.ident = sb("ident", [128, 128])
        self.ones = sb("ones", [128, 128])
        self.kcol = sb("kcol", [128, NCP])
        self.kcol2 = sb("kcol2", [128, NCP // 2])
        self.two = sb("two", [128, 1])
        self.eps = sb("eps", [128, 1])
        self.arena_words = 20600
        self.arena = sb("arena", [128, self.arena_words])
        self.ps = ctx.enter_context(nc.psum_tensor("ps", [128, 4, 1024], F32))

        self.filled = count("psum_filled")
        self.emptied = count("psum_emptied")
        self.var_ready = count("var_ready")
        self.std_ready = count("std_ready")
        self.dve_step = count("dve_step")
        self.act_step = count("act_step")
        self.pool_step = count("pool_step")
        self.pe_step = count("pe_step")
        self.act_ready = count("act_ready")
        self.dve_ready = count("dve_ready")
        self.dve_for_pe = count("dve_for_pe")
        self.act_for_pe = count("act_for_pe")
        self.params_in = count("params_in")
        self.tables_filled = count("tables_filled")
        self.edge_sum = count("edge_sum")
        self.edge_relu = count("edge_relu")
        self.hot_ready = count("hot_ready")
        self.hot_used = count("hot_used")
        self.stored = count("stored")
        self.slab_in = [count(f"slab_in{i}") for i in range(RING)]
        self.slab_free = count("slab_free")
        self.gathered = [count(f"gathered{i}") for i in range(5)]
        self.scattered = count("scattered")
        self.logits_ready = count("logits_ready")
        self.dense_in = [count(f"dense_in{i}") for i in range(T)]

        self.pe_down = count("expert_outputs")
        self.rows_turned = count("rows_turned")
        self.y_out = [[count(f"y_out{e}_{b}") for b in range(BLOCKS)] for e in range(2)]
        self.xn_d = nc.dram_tensor("xn_rows", (N, D), F32, kind="Internal").ap()
        self.y_d = nc.dram_tensor("expert_rows", (EXPERTS * LIST, D), F32, kind="Internal").ap()
        self.lists = nc.dram_tensor("expert_lists", (EXPERTS * LIST, 1), F32, kind="Internal").ap()
        self.slot = sb("slot", [P, 2, T], I32)
        self.weight = sb("weight", [P, 2, T])
        self.idx = sb("idx", [128, EXPERTS * BLOCKS], I32)
        self.need = sb("need", [1, EXPERTS], I32)
        self.slabs, self.issued, self.used = [], 0, 0
        self.fs_d = nc.dram_tensor("fs_rows", (N, DW), F32, kind="Internal").ap()
        self.fd_d = nc.dram_tensor("fd_rows", (N, DW), F32, kind="Internal").ap()
        self.dense = {8: nc.dram_tensor("dense_logits8", (N * N, 8), F32, kind="Internal").ap(),
                      1: nc.dram_tensor("dense_logits1", (N * N, 1), F32, kind="Internal").ap()}

    def reset(self, keep=0):
        self.at = keep

    def carve(self, parts, *shape):
        n = 1
        for s in shape:
            n *= s
        v = self.arena[0:parts, self.at:self.at + n]
        self.at += n
        assert self.at <= self.arena_words, self.at
        if len(shape) == 2:
            v = v.rearrange("p (a b) -> p a b", a=shape[0])
        elif len(shape) == 3:
            v = v.rearrange("p (a b c) -> p a b c", a=shape[0], b=shape[1])
        return v

    def feed(self, sp, uses, freed=None):
        first = self.used_before
        self.will_use = self.used_before + uses
        while self.issued < min(len(self.slabs), self.will_use + RING - 1):
            i = self.issued
            src, parts, words = self.slabs[i]
            if i >= RING and freed and i - RING >= first:
                count, value = freed(i - RING - first)
                sp.wait_ge(count.sem, value)
            elif i >= RING:
                sp.wait_ge(self.slab_free.sem, i - RING + 1)
            dst = self.ring[0:parts, i % RING, 0:words]
            self.slab_in[i % RING].mark_dma(sp.dma_start(dst, src))
            self.issued += 1
        self.used_before += uses

    def slab(self, eng, n=0):
        i = self.used + n
        eng.wait_ge(self.slab_in[i % RING].sem, 16 * (i // RING + 1))
        return self.ring[:, i % RING, :]

    def release(self, ins):
        self.slab_free.mark(ins)
        self.used += 1


def plan_slabs(k):
    a = k.a

    def add(ap, parts=128):
        k.slabs.append((ap, parts, ap.shape[1]))

    for w in ("L0_gnn_W1s", "L0_gnn_W1d", "L0_gnn_Wos", "L0_gnn_Wod"):
        add(a[w])
    for h in range(2):
        add(a["L0_ffn_w1"][:, h * 48 * KH:(h + 1) * 48 * KH])
    for h in range(2):
        add(a["L0_ffn_w2"][:, h * 4 * D:(h + 1) * 4 * D])
    for h in range(H_L1):
        add(a["L1_gnn_W1"][:, h * C * HID1:(h + 1) * C * HID1])
    for c0, c1 in ((0, 6), (6, 12), (12, 16)):
        add(a["L1_gnn_W2"][:, c0 * D:c1 * D])
    for q in range(EXPERTS + 1):
        for n in range(SIX):
            add(a["L1_ffn_shared"][n] if q == 0 else a["L1_ffn_experts"][q - 1, n])
    for w in ("L2_gnn_W1", "L2_gnn_W2", "L2_ffn_weight", "L3_ffn_W1"):
        add(a[w])
    for h in range(2):
        add(a["L3_ffn_W2"][:, h * 4 * D:(h + 1) * 4 * D], F3)
    k.used_before = 0


def halves(ap):
    return ap.rearrange("p (b f) -> p b f", b=2)[:, :, 0:HALF]


def wide(ap):
    return ap.rearrange("p (b f) -> p b f", b=2)


def tiles(ap):
    return ap.rearrange("p (t c) -> p t c", c=128)[:, 0:T, 0:P]


def setup_stage(k):
    nc, a = k.nc, k.a
    k.reset()
    srcf = k.carve(P, ET)
    dstf = k.carve(P, ET)
    keyf = k.carve(P, ET)
    no_edge = k.neg[:, :, :].rearrange("p t n -> p (t n)")
    dve0 = k.dve_ready.n
    with nc.Block() as block:
        @block.sync
        def _(sp):
            k.params_in.mark_dma(sp.dma_start(k.x[:, :, :], a["x"].rearrange("(t p) d -> p t d", p=P)))
            k.params_in.mark_dma(sp.dma_start(k.srci[:, :], a["src"].rearrange("(p t) -> p t", t=ET)))
            k.params_in.mark_dma(sp.dma_start(k.dsti[:, :], a["dst"].rearrange("(p t) -> p t", t=ET)))
            k.feed(sp, 0)
            sp.wait_ge(k.dve_ready.sem, dve0 + 1)
            table = k.dense[8].rearrange("(k p c) h -> k p (c h)", p=P, k=25)
            for i in range(25):
                k.tables_filled.mark_dma(sp.dma_start(table[i], no_edge[:, 0:1000]))
            k.tables_filled.mark_dma(sp.dma_start(k.dense[1].rearrange("(p c) h -> p (c h)", p=P), no_edge))
            sp.wait_ge(k.params_in.sem, k.params_in.n)

        @block.gpsimd
        def _(pool):
            step(pool, k.pool_step, pool.memset(k.ident[:, :], 0.0))
            step(pool, k.pool_step, pool.affine_select(out=k.ident[:, :], in_=k.ident[:, :], compare_op=ALU.not_equal,
                                                       fill=1.0, base=0, pattern=[[-1, 128]], channel_multiplier=1))
            step(pool, k.pool_step, pool.memset(k.ones[:, :], 1.0))
            step(pool, k.pool_step, pool.iota(k.kcol[:, :], [[-1, NCP]], base=-2, channel_multiplier=0,
                                              allow_small_or_imprecise_dtypes=True))
            for half in range(2):
                step(pool, k.pool_step, pool.iota(k.kcol2[64 * half:64 * half + 64, :], [[-2, NCP // 2]], base=-2 - half,
                                                  channel_multiplier=0, allow_small_or_imprecise_dtypes=True))

        @block.vector
        def _(dve):
            k.dve_ready.mark(dve.memset(no_edge, NEG))
            k.dve_step.mark(dve.memset(k.two[:, :], 2.0))
            k.dve_step.mark(dve.memset(k.eps[:, :], EPS))
            dve.wait_ge(k.params_in.sem, 48)
            k.dve_step.mark(dve.tensor_copy(srcf, k.srci[:, :]))
            step(dve, k.dve_step, dve.tensor_copy(dstf, k.dsti[:, :]))
            step(dve, k.dve_step, dve.scalar_tensor_tensor(keyf, dstf, float(N), srcf, ALU.mult, ALU.add))
            k.dve_step.mark(dve.tensor_copy(k.key[:, :], keyf))


def row_norm(k, dve, st, src, j=0):
    k.dve_step.mark(dve.bn_stats(st[:, 0:6], src[:, 0:HALF]))
    step(dve, k.dve_step, dve.bn_stats(st[:, 6:12], src[:, HALF:D]))
    k.var_ready.mark(dve.bn_aggr(st[:, 12:14], st[:, 0:12]))


def deviation(k, act, st, nth):
    act.wait_ge(k.var_ready.sem, nth)
    k.std_ready.mark(act.activation(st[:, 14:15], st[:, 13:14], ACT.Sqrt, bias=k.eps[0:P, :]))


def norm_stage(k, normalise=True):
    nc = k.nc
    st = k.arena[0:P, k.arena_words - 80:].rearrange("p (t s) -> p t s", t=T)
    f0, e0, d0, v0, rs0 = k.filled.n, k.emptied.n, k.dve_for_pe.n, k.var_ready.n, k.std_ready.n
    with nc.Block() as block:
        @block.sync
        def _(sp):
            k.feed(sp, 0)

        @block.vector
        def _(dve):
            if normalise:
                for t in range(T + 1):
                    if t < T:
                        row_norm(k, dve, st[:, t, :], k.x[:, t, :])
                    if t >= 1:
                        m = t - 1
                        dve.wait_ge(k.std_ready.sem, rs0 + m + 1)
                        step(dve, k.dve_step, dve.reciprocal(st[:, m, 14:15], st[:, m, 14:15]))
                        k.dve_for_pe.mark(dve.tensor_scalar(k.xn[:, m, :], k.x[:, m, :], st[:, m, 12:13], st[:, m, 14:15],
                                                            ALU.subtract, ALU.mult))

        @block.tensor
        def _(pe):
            for t in range(T):
                if normalise:
                    pe.wait_ge(k.dve_for_pe.sem, d0 + t + 1)
                if t >= 4:
                    pe.wait_ge(k.emptied.sem, e0 + t - 3)
                for c in range(C):
                    last = pe.transpose(k.ps[:, t % 4, c * 128:c * 128 + P], k.xn[:, t, c * 128:(c + 1) * 128], k.ident[0:P, 0:P])
                k.filled.mark(last)

        @block.scalar
        def _(act):
            for t in range(T + 2):
                if normalise and t < T:
                    deviation(k, act, st[:, t, :], v0 + t + 1)
                if t >= 2:
                    m = t - 2
                    act.wait_ge(k.filled.sem, f0 + m + 1)
                    k.emptied.mark(act.activation(k.xT[:, :, m * P:(m + 1) * P],
                                                  k.ps[:, m % 4, 0:C * 128].rearrange("p (c n) -> p c n", c=C)[:, :, 0:P], ACT.Copy))


def node_major(pe, out, lhs, w, chunks, cols=D, start=True, stop=True):
    for c in chunks:
        for b in range(2):
            last = pe.matmul(out[0:P, b * 512:b * 512 + cols // 2], lhs(c), w(c)[:, b * cols // 2:(b + 1) * cols // 2],
                             start=start and c == chunks[0], stop=stop and c == chunks[-1])
    return last


def feature_major(pe, out, parts, lhs, rhs, chunks):
    for c in chunks:
        for lo, hi in ((0, 512), (512, N)):
            last = pe.matmul(out[0:parts, lo:hi], lhs(c), rhs(c)[:, lo:hi], start=c == chunks[0], stop=c == chunks[-1])
    return last


def gat2_project_stage(k, heads, bs, bd, attn, faug):
    nc, a = k.nc, k.a
    hw = D // heads
    bias = k.carve(P, 2, D)
    fd = k.carve(P, T, D)
    attn_b = k.carve(P, D)
    prod = k.carve(P, D)
    lin = k.carve(P, 2 * T, DW - D)
    f0, e0, p0, dr0 = k.filled.n, k.emptied.n, k.params_in.n, k.dve_ready.n
    with nc.Block() as block:
        @block.sync
        def _(sp):
            for n, b in enumerate((bs, bd)):
                k.params_in.mark_dma(sp.dma_start(bias[:, n, :], a[b][0:P, :]))
            k.params_in.mark_dma(sp.dma_start(attn_b, a[attn][0:P, :]))
            k.feed(sp, 2)
            fs_rows = k.fs_d.rearrange("(t p) d -> t p d", p=P)
            fd_rows = k.fd_d.rearrange("(t p) d -> t p d", p=P)
            for n in range(2 * T):
                t = n % T
                sp.wait_ge(k.dve_ready.sem, dr0 + n + 1)
                if n < T:
                    k.stored.mark_dma(sp.dma_start(fs_rows[t][:, 0:D].rearrange("p (h f) -> p h f", h=heads), faug[:, t, :, 0:hw]))
                else:
                    k.stored.mark_dma(sp.dma_start(fd_rows[t][:, 0:D], fd[:, t, :]))
                k.stored.mark_dma(sp.dma_start((fs_rows, fd_rows)[n // T][t][:, D:DW], lin[:, n, :]))
            sp.wait_ge(k.stored.sem, k.stored.n)

        @block.tensor
        def _(pe):
            for n in range(2):
                w = k.slab(pe).rearrange("p (c d) -> p c d", c=C)
                for t in range(T):
                    j = n * T + t
                    wait(pe, k.emptied, e0 + j - 3 if j >= 4 else 0)
                    last = node_major(pe, k.ps[:, j % 4, :], lambda c: k.xT[:, c, t * P:(t + 1) * P], lambda c: w[:, c, :], range(C))
                    k.filled.mark(last)
                release_slabs(k, pe, k.filled, 1)

        @block.vector
        def _(dve):
            k.dve_step.mark(dve.memset(faug[:, :, :, hw:hw + 1], 1.0))
            step(dve, k.dve_step, dve.memset(lin, 0.0))
            dve.wait_ge(k.params_in.sem, p0 + 48)
            pv = prod.rearrange("p (h f) -> p h f", h=heads)
            av = attn_b.rearrange("p (h f) -> p h f", h=heads)
            for j in range(2 * T):
                dve.wait_ge(k.filled.sem, f0 + j + 1)
                src = halves(k.ps[0:P, j % 4, :])
                b = bias[:, j // T, :].rearrange("p (b f) -> p b f", b=2)
                if j < T:
                    out = faug[:, j, :, 0:hw]
                    if heads > 1:
                        src = src.rearrange("p b (h f) -> p b h f", f=hw)
                        b = b.rearrange("p b (h f) -> p b h f", f=hw)
                        out = out.rearrange("p (b h) f -> p b h f", b=2)
                    else:
                        out = faug[:, j, 0, 0:D].rearrange("p (b f) -> p b f", b=2)
                else:
                    out = fd[:, j - T, :].rearrange("p (b f) -> p b f", b=2)
                k.emptied.mark(dve.tensor_tensor(out, src, b, ALU.add))
                dve.wait_ge(k.emptied.sem, k.emptied.n)
                row = faug[:, j, :, 0:hw] if j < T else fd[:, j - T, :].rearrange("p (h f) -> p h f", h=heads)
                step(dve, k.dve_step, dve.scalar_tensor_tensor(pv, row, SLOPE, av, ALU.mult, ALU.mult))
                k.dve_ready.mark(dve.tensor_reduce(lin[:, j, 0:heads], pv, AX, ALU.add))
                dve.wait_ge(k.dve_ready.sem, k.dve_ready.n)


def gat2_edge_stage(k, heads, attn, count):
    nc, a = k.nc, k.a
    SL, LAG, HOTS = 5, 4, 3
    ga = k.carve(P, SL, DW)
    gb = k.carve(P, SL, DW)
    attn_b = k.carve(P, D)
    logit = k.carve(P, ET, heads)
    red = k.carve(P, 2, heads)
    if count:
        srcf = k.carve(P, ET)
        dstf = k.carve(P, ET)
        iota = k.carve(P, (N + 1) // 2 + 1).bitcast(I16)[:, 0:N]
        hot = k.carve(P, HOTS * 2 * (N + 1) // 2).bitcast(BF16).rearrange("p (s w n) -> p s w n", s=HOTS, w=2)[:, :, :, 0:N]
    p0, l0, sc0, po0 = k.params_in.n, k.logits_ready.n, k.scattered.n, k.pool_step.n
    sum0, relu0, hot0, used0, f0, e0 = k.edge_sum.n, k.edge_relu.n, k.hot_ready.n, k.hot_used.n, k.filled.n, k.emptied.n
    g0 = [g.n for g in k.gathered]
    counts_in = []

    def bank(i):
        b = T + i // 3
        return (k.ps[0:P, i // 2, (i % 2) * 512:(i % 2) * 512 + 500],
                k.ps[0:P, b // 2, (b % 2) * 512 + (i % 3) * P:(b % 2) * 512 + (i % 3 + 1) * P])

    with nc.Block() as block:
        @block.sync
        def _(sp):
            k.params_in.mark_dma(sp.dma_start(attn_b, a[attn][0:P, :]))
            k.feed(sp, 0)

        @block.gpsimd
        def _(pool):
            if count:
                step(pool, k.pool_step, pool.iota(iota, [[1, N]], base=0, channel_multiplier=0, allow_small_or_imprecise_dtypes=True))
            for t in range(ET + LAG):
                if t < ET:
                    if t >= SL:
                        pool.wait_ge(k.logits_ready.sem, l0 + t - SL + 1)
                    for buf, rows, idx in ((ga, k.fs_d, k.srci), (gb, k.fd_d, k.dsti)):
                        k.gathered[t % SL].mark_dma(pool.indirect_dma_start(
                            buf[:, t % SL, :], None, rows[:, :], bass.IndirectOffsetOnAxis(ap=idx[:, t:t + 1], axis=0)))
                s = t - LAG
                if s >= 0:
                    if s == 0:
                        pool.wait_ge(k.tables_filled.sem, k.tables_filled.n)
                    pool.wait_ge(k.logits_ready.sem, l0 + s + 1)
                    wait(pool, k.scattered, k.scattered.n)
                    k.scattered.mark_dma(pool.indirect_dma_start(
                        k.dense[heads], bass.IndirectOffsetOnAxis(ap=k.key[:, s:s + 1], axis=0), logit[:, s, :], None))
            pool.wait_ge(k.scattered.sem, k.scattered.n)

        @block.scalar
        def _(act):
            for t in range(ET):
                act.wait_ge(k.edge_sum.sem, sum0 + t + 1)
                k.edge_relu.mark(act.activation(gb[:, t % SL, 0:D], ga[:, t % SL, 0:D], ACT.Relu, scale=1.0 - SLOPE))

        @block.vector
        def _(dve):
            if count:
                k.dve_step.mark(dve.tensor_copy(srcf, k.srci[:, :]))
                step(dve, k.dve_step, dve.tensor_copy(dstf, k.dsti[:, :]))
                dve.wait_ge(k.pool_step.sem, po0 + 1)
            dve.wait_ge(k.params_in.sem, p0 + 16)
            for t in range(ET + 1):
                if t < ET:
                    dve.wait_ge(k.gathered[t % SL].sem, g0[t % SL] + 32 * (t // SL + 1))
                    k.edge_sum.mark(dve.tensor_tensor(ga[:, t % SL, :], ga[:, t % SL, :], gb[:, t % SL, :], ALU.add))
                    if count:
                        if t >= HOTS:
                            dve.wait_ge(k.hot_used.sem, used0 + t - HOTS + 1)
                        k.hot_ready.mark(dve.tensor_scalar(hot[:, t % HOTS, 0, :], iota, srcf[:, t:t + 1], None, ALU.is_equal))
                        k.hot_ready.mark(dve.tensor_scalar(hot[:, t % HOTS, 1, :], iota, dstf[:, t:t + 1], None, ALU.is_equal))
                if t >= 1:
                    u = t - 1
                    A, B = ga[:, u % SL, :], gb[:, u % SL, 0:D]
                    dve.wait_ge(k.edge_relu.sem, relu0 + u + 1)
                    if heads == 1:
                        step(dve, k.dve_step, dve.tensor_tensor_reduce(B, B, attn_b, 1.0, 0.0, ALU.mult, ALU.add, red[:, u % 2, :]))
                    else:
                        step(dve, k.dve_step, dve.tensor_tensor(B, B, attn_b, ALU.mult))
                        step(dve, k.dve_step, dve.tensor_reduce(red[:, u % 2, :], B.rearrange("p (h f) -> p h f", h=heads), AX, ALU.add))
                    k.logits_ready.mark(dve.tensor_tensor(logit[:, u, :], red[:, u % 2, :], A[:, D:D + heads], ALU.add))
            if count:
                dve.wait_ge(k.filled.sem, f0 + 1)
                for i in range(T):
                    head, tail = bank(i)
                    k.dve_step.mark(dve.tensor_copy(k.cT[:, i, 0:500], head))
                    k.dve_step.mark(dve.tensor_copy(k.cT[:, i, 500:625], tail))
                counts_in.append(k.dve_step.n)
                dve.wait_ge(k.tables_filled.sem, k.tables_filled.n)
                for j in range(T):
                    dve.wait_ge(k.filled.sem, f0 + 2 + j)
                    k.dve_step.mark(dve.tensor_scalar(k.neg[:, j, :].rearrange("p (i s) -> p i s", i=T), tiles(k.ps[0:P, j % 4, :]),
                                                      0.0, NEG, ALU.is_equal, ALU.mult))
                    k.emptied.mark(dve.tensor_reduce(k.deg[:, j:j + 1], tiles(k.ps[0:P, j % 4, :]), mybir.AxisListType.XY, ALU.add))

        @block.tensor
        def _(pe):
            if count:
                for t in range(ET):
                    pe.wait_ge(k.hot_ready.sem, hot0 + 2 * t + 2)
                    for i in range(T):
                        w = hot[:, t % HOTS, 0, i * P:(i + 1) * P]
                        head, tail = bank(i)
                        pe.matmul(head, w, hot[:, t % HOTS, 1, 0:500], start=t == 0, stop=t == ET - 1, skip_group_check=True)
                        last = pe.matmul(tail, w, hot[:, t % HOTS, 1, 500:625], start=t == 0 and i % 3 == 0, stop=t == ET - 1,
                                         skip_group_check=True)
                    if t < ET - 1:
                        k.hot_used.mark(last)
                    else:
                        k.filled.mark(last)
                pe.wait_ge(k.dve_step.sem, counts_in[0])
                for j in range(T):
                    if j >= 4:
                        pe.wait_ge(k.emptied.sem, e0 + j - 3)
                    for i in range(T):
                        last = pe.transpose(k.ps[0:P, j % 4, i * 128:i * 128 + P], k.cT[:, i, j * P:(j + 1) * P], k.ident[0:P, 0:P])
                    k.filled.mark(last)


def gat2_dense_stage(k, heads, faug, ln_w, ln_b, last_layer):
    nc, a = k.nc, k.a
    hw = D // heads
    LB, AHEAD = (2, 1) if heads > 1 else (T, T)
    arrived = k.dense_in
    L = k.carve(P, LB, N * heads)
    wt = k.carve(P, 3, T * P)
    m = k.carve(P, LB, heads)
    r = k.carve(P, D)
    e = k.carve(P, D)
    lnw = k.carve(P, D)
    lnb = k.carve(P, D)
    st = k.carve(P, 16)
    rden = k.carve(P, 8)
    p0 = k.params_in.n
    in0 = [s.n for s in arrived]
    neg0, exp0, tr0, wt0, agg0, e0, el0 = (k.dve_ready.n, k.act_for_pe.n, k.filled.n, k.dve_for_pe.n,
                                           k.pe_step.n, k.emptied.n, k.act_ready.n)
    v0, rs0 = k.var_ready.n, k.std_ready.n
    with nc.Block() as block:
        @block.sync
        def _(sp):
            k.params_in.mark_dma(sp.dma_start(lnw, a[ln_w][0:P, :]))
            k.params_in.mark_dma(sp.dma_start(lnb, a[ln_b][0:P, :]))
            k.feed(sp, 0)
            table = k.dense[heads].rearrange("(j p s) h -> j p (s h)", p=P, j=T)
            for j in range(T):
                if j >= LB:
                    sp.wait_ge(k.filled.sem, tr0 + heads * (j - LB + 1))
                arrived[j % LB].mark_dma(sp.dma_start(L[:, j % LB, :], table[j]))

        @block.vector
        def _(dve):
            dve.wait_ge(k.params_in.sem, p0 + 32)

            def row_max(j):
                dve.wait_ge(arrived[j % LB].sem, in0[j % LB] + 16 * (j // LB + 1))
                if j >= LB:
                    dve.wait_ge(k.act_for_pe.sem, exp0 + heads * (j - LB + 1))
                step(dve, k.dve_step, dve.tensor_reduce(m[:, j % LB, :], L[:, j % LB, :].rearrange("p (s h) -> p h s", h=heads), AX, ALU.max))
                k.dve_ready.mark(dve.tensor_scalar(m[:, j % LB, :], m[:, j % LB, :], -1.0, None, ALU.mult))

            def finish(j):
                dve.wait_ge(k.pe_step.sem, agg0 + (j + 1) * heads)
                out = k.ps[0:P, 2 + j % 2, :]
                if heads == 1:
                    den = out[:, D:D + 1]
                    step(dve, k.dve_step, dve.tensor_scalar(rden[:, 0:1], den, 1e-30, None, ALU.max))
                    step(dve, k.dve_step, dve.reciprocal(rden[:, 0:1], rden[:, 0:1]))
                    step(dve, k.dve_step, dve.tensor_scalar(r, out[:, 0:D], rden[:, 0:1], None, ALU.mult))
                else:
                    v = wide(out)[:, :, 0:4 * (hw + 1)].rearrange("p b (h f) -> p b h f", f=hw + 1)
                    rd = rden[:, :].rearrange("p (b h o) -> p b h o", b=2, o=1)
                    step(dve, k.dve_step, dve.tensor_scalar(rd, v[:, :, :, hw:hw + 1], 1e-30, None, ALU.max))
                    step(dve, k.dve_step, dve.reciprocal(rden, rden))
                    step(dve, k.dve_step, dve.tensor_tensor(r.rearrange("p (b h f) -> p b h f", b=2, f=hw), v[:, :, :, 0:hw],
                                                            rd.broadcast_to([P, 2, 4, hw]), ALU.mult))
                k.emptied.mark(dve.tensor_scalar(e, r, 0.0, None, ALU.min))
                step(dve, k.dve_step, dve.tensor_scalar(r, r, 0.0, -1.0, ALU.max, ALU.add))
                dve.wait_ge(k.act_ready.sem, el0 + j + 1)
                step(dve, k.dve_step, dve.tensor_tensor(r, r, e, ALU.add))
                if not last_layer:
                    step(dve, k.dve_step, dve.tensor_tensor(r, r, k.xn[:, j, :], ALU.add))
                row_norm(k, dve, st, r)
                dve.wait_ge(k.std_ready.sem, rs0 + j + 1)
                step(dve, k.dve_step, dve.reciprocal(st[:, 14:15], st[:, 14:15]))
                step(dve, k.dve_step, dve.tensor_scalar(r, r, st[:, 12:13], st[:, 14:15], ALU.subtract, ALU.mult))
                step(dve, k.dve_step, dve.tensor_tensor(r, r, lnw, ALU.mult))
                if last_layer:
                    step(dve, k.dve_step, dve.tensor_tensor(r, r, lnb, ALU.add))
                    step(dve, k.dve_step, dve.tensor_tensor(k.x[:, j, :], k.x[:, j, :], r, ALU.add))
                else:
                    step(dve, k.dve_step, dve.tensor_tensor(k.xn[:, j, :], r, lnb, ALU.add))

            max_at, finish_at = (5, 2) if heads > 1 else (0, 0)
            for j in range(AHEAD):
                row_max(j)
            for j in range(T):
                for h in range(heads):
                    n = j * heads + h
                    dve.wait_ge(k.filled.sem, tr0 + n + 1)
                    if n >= 3:
                        dve.wait_ge(k.pe_step.sem, agg0 + n - 2)
                    k.dve_for_pe.mark(dve.tensor_tensor(wt[:, n % 3, :].rearrange("p (i d) -> p i d", i=T), tiles(k.ps[0:P, n % 2, :]),
                                                        k.cT[:, :, j * P:(j + 1) * P], ALU.mult))
                    if h == max_at and j + AHEAD < T:
                        row_max(j + AHEAD)
                    if h == finish_at and j >= 1:
                        finish(j - 1)
            finish(T - 1)

        @block.scalar
        def _(act):
            def exps(j):
                act.wait_ge(k.dve_ready.sem, neg0 + j + 1)
                for h in range(heads):
                    v = L[:, j % LB, :].rearrange("p (s h) -> p h s", h=heads)[:, h, :]
                    k.act_for_pe.mark(act.activation(v, v, ACT.Exp, bias=m[:, j % LB, h:h + 1]))
            for j in range(AHEAD):
                exps(j)
            for j in range(T):
                if j + AHEAD < T:
                    exps(j + AHEAD)
                act.wait_ge(k.emptied.sem, e0 + j + 1)
                k.act_ready.mark(act.activation(e, e, ACT.Exp))
                deviation(k, act, st, v0 + j + 1)

        @block.tensor
        def _(pe):
            def aggregate(n):
                j, h = n // heads, n % heads
                pe.wait_ge(k.dve_for_pe.sem, wt0 + n + 1)
                if h == 0 and j >= 2:
                    pe.wait_ge(k.emptied.sem, e0 + j - 1)
                out = k.ps[0:P, 2 + j % 2, :]
                for i in range(T):
                    w = wt[:, n % 3, i * P:(i + 1) * P]
                    if heads == 1:
                        pe.matmul(out[:, 0:512], w, faug[:, i, 0, 0:512], start=i == 0, stop=i == T - 1)
                        last = pe.matmul(out[:, 512:D + 1], w, faug[:, i, 0, 512:D + 1], start=i == 0, stop=i == T - 1)
                    else:
                        at = h // 4 * 512 + (h % 4) * (hw + 1)
                        last = pe.matmul(out[:, at:at + hw + 1], w, faug[:, i, h, :], start=i == 0, stop=i == T - 1)
                k.pe_step.mark(last)
            for n in range(T * heads):
                j, h = n // heads, n % heads
                pe.wait_ge(k.act_for_pe.sem, exp0 + n + 1)
                if n >= 2:
                    pe.wait_ge(k.dve_for_pe.sem, wt0 + n - 1)
                v = L[:, j % LB, :].rearrange("p (s h) -> p h s", h=heads)
                for i in range(T):
                    last = pe.transpose(k.ps[0:P, n % 2, i * 128:i * 128 + P], v[:, h, i * P:(i + 1) * P], k.ident[0:P, 0:P])
                k.filled.mark(last)
                if n >= 1:
                    aggregate(n - 1)
            aggregate(T * heads - 1)


def gat2(k):
    for heads, bs, bd, attn, w, b, last in ((8, "L0_gnn_b1s", "L0_gnn_b1d", "L0_gnn_attn1", "L0_gnn_ln1_w", "L0_gnn_ln1_b", False),
                                            (1, "L0_gnn_bos", "L0_gnn_bod", "L0_gnn_attno", "L0_gnn_lno_w", "L0_gnn_lno_b", True)):
        norm_stage(k, normalise=not last)
        k.reset()
        faug = k.carve(P, T, heads, D // heads + 1)
        keep = k.at
        gat2_project_stage(k, heads, bs, bd, attn, faug)
        k.reset(keep)
        gat2_edge_stage(k, heads, attn, not last)
        k.reset(keep)
        gat2_dense_stage(k, heads, faug, w, b, last)


RMIN, RMAX, DEGREE = -4.0, 4.0, 3
STEP_H = (RMAX - RMIN) / (NCP - DEGREE)


def spline_stage(k):
    nc = k.nc
    k.reset()
    G = KG * N
    NA, NS = 4, 3
    u = k.xT
    abuf = k.carve(128, NA, G)
    bbuf = k.carve(128, NA, G)
    asq = k.carve(128, NS, G)
    bsq = k.carve(128, NS, G)
    zero = k.carve(128, D)
    groups = [(c, g) for c in range(C) for g in range(NCP // KG)]
    NG = len(groups)
    PER_SLAB = NG // 2
    u_ready, s_ready, ab_ready, asq_ready, bsq_ready = k.dve_ready, k.act_ready, k.dve_ready, k.act_step, k.act_for_pe
    cubed, bases, used = k.pool_step, k.dve_for_pe, k.pe_step
    u0, s0, asq0, bsq0, cu0, ba0, us0 = u_ready.n, s_ready.n, asq_ready.n, bsq_ready.n, cubed.n + 1, bases.n, used.n
    ab0 = u0 + 1
    with nc.Block() as block:
        @block.sync
        def _(sp):
            k.feed(sp, 2)
            sp.wait_ge(cubed.sem, cu0)
            for c in range(0, EXPERTS * BLOCKS, BLOCKS):
                k.stored.mark_dma(sp.dma_start(k.y_d.rearrange("(c p) d -> p c d", p=128)[:, c:c + BLOCKS, :],
                                               zero.rearrange("p (o d) -> p o d", o=1).broadcast_to([128, BLOCKS, D])))
            sp.wait_ge(k.stored.sem, k.stored.n)

        @block.vector
        def _(dve):
            u_ready.mark(dve.tensor_scalar(u[:, :, :], u[:, :, :], 1.0 / STEP_H, -RMIN / STEP_H + DEGREE, ALU.mult, ALU.add))
            for n in range(NG + 2):
                if n < NG:
                    dve.wait_ge(s_ready.sem, s0 + KG * (n + 1))
                    if n >= NA:
                        dve.wait_ge(used.sem, us0 + n - NA + 1)
                    A = abuf[:, n % NA, :]
                    ab_ready.mark(dve.tensor_scalar(bbuf[:, n % NA, :], A, -1.0, 0.0, ALU.add, ALU.min))
                    dve.wait_ge(ab_ready.sem, ab_ready.n)
                    ab_ready.mark(dve.tensor_scalar(A, A, -2.0, 0.0, ALU.add, ALU.min))
                if n >= 2:
                    m = n - 2
                    B = bbuf[:, m % NA, :]
                    dve.wait_ge(bsq_ready.sem, bsq0 + m + 1)
                    step(dve, k.dve_step, dve.scalar_tensor_tensor(B, bsq[:, m % NS, :], -4.0, B, ALU.mult, ALU.mult))
                    dve.wait_ge(cubed.sem, cu0 + m + 1)
                    bases.mark(dve.tensor_tensor(B, abuf[:, m % NA, :], B, ALU.add))

        @block.scalar
        def _(act):
            act.wait_ge(u_ready.sem, u0 + 1)
            for n in range(NG + 1):
                if n < NG:
                    c, g = groups[n]
                    A = abuf[:, n % NA, :]
                    if n >= NA:
                        act.wait_ge(bases.sem, ba0 + n - NA + 1)
                    for i in range(KG):
                        kk = g * KG + i
                        s_ready.mark(act.activation(A[:, i * N:(i + 1) * N], u[:, c, :], ACT.Abs, bias=k.kcol[:, kk:kk + 1]))
                if n >= 1:
                    m = n - 1
                    act.wait_ge(ab_ready.sem, ab0 + 2 * m + 1)
                    if m >= NS:
                        act.wait_ge(bases.sem, ba0 + m - NS + 1)
                    bsq_ready.mark(act.activation(bsq[:, m % NS, :], bbuf[:, m % NA, :], ACT.Square))
                    act.wait_ge(ab_ready.sem, ab0 + 2 * m + 2)
                    if m >= NS:
                        act.wait_ge(cubed.sem, cu0 + m - NS + 1)
                    asq_ready.mark(act.activation(asq[:, m % NS, :], abuf[:, m % NA, :], ACT.Square))

        @block.gpsimd
        def _(pool):
            step(pool, cubed, pool.memset(zero, 0.0))
            for n in range(NG):
                pool.wait_ge(asq_ready.sem, asq0 + n + 1)
                A = abuf[:, n % NA, :]
                cubed.mark(pool.tensor_tensor(A, A, asq[:, n % NS, :], ALU.mult))

        @block.tensor
        def _(pe):
            for n in range(NG):
                if n % PER_SLAB == 0:
                    w = k.slab(pe).rearrange("p (g k o) -> p g k o", k=KG, o=KH)
                pe.wait_ge(bases.sem, ba0 + n + 1)
                for i in range(KG):
                    for lo, hi in ((0, 512), (512, N)):
                        last = pe.matmul(k.ps[0:KH, 0, lo:hi], w[:, n % PER_SLAB, i, :], bbuf[:, n % NA, i * N + lo:i * N + hi],
                                         start=n == 0 and i == 0, stop=n == NG - 1 and i == KG - 1)
                used.mark(last)
                if n % PER_SLAB == PER_SLAB - 1:
                    release_slabs(k, pe, used, 1)
    spline_out_stage(k)


def spline_out_stage(k):
    nc = k.nc
    PAIRS = NCP // 2
    k.reset()
    u2 = k.carve(128, N)
    A = k.carve(128, PAIRS, N)
    B = k.carve(128, PAIRS, N)
    asq = k.carve(128, 2, PAIRS, P)
    bsq = k.carve(128, 2, PAIRS, P)
    s_ready, ab_ready, squared, bases, product = k.act_step, k.dve_ready, k.act_ready, k.dve_for_pe, k.filled
    u0, sq0, ba0, f0, e0 = ab_ready.n, squared.n, bases.n, product.n, k.emptied.n
    ab0 = u0 + 2
    s0 = s_ready.n

    def tile(v, t):
        return v[:, :, t * P:(t + 1) * P]

    with nc.Block() as block:
        @block.sync
        def _(sp):
            k.feed(sp, 2)

        @block.scalar
        def _(act):
            act.wait_ge(ab_ready.sem, u0 + 2)
            for i in range(PAIRS):
                s_ready.mark(act.activation(A[:, i, :], u2, ACT.Abs, bias=k.kcol2[:, i:i + 1]))
            for t in range(T):
                act.wait_ge(ab_ready.sem, ab0 + 2 * t + 2)
                if t >= 2:
                    act.wait_ge(bases.sem, ba0 + t - 1)
                squared.mark(act.activation(bsq[:, t % 2], tile(B, t), ACT.Square))
                squared.mark(act.activation(asq[:, t % 2], tile(A, t), ACT.Square))

        @block.vector
        def _(dve):
            for half in range(2):
                ab_ready.mark(dve.tensor_scalar(u2[half * 64:half * 64 + 64, :], k.ps[0:KH, 0, 0:N], -1.0 / (6.0 * STEP_H),
                                                -RMIN / STEP_H + DEGREE, ALU.mult, ALU.add))
            dve.wait_ge(s_ready.sem, s0 + PAIRS)
            for t in range(T + 1):
                if t < T:
                    ab_ready.mark(dve.tensor_scalar(tile(B, t), tile(A, t), -1.0, 0.0, ALU.add, ALU.min))
                    dve.wait_ge(ab_ready.sem, ab_ready.n)
                    ab_ready.mark(dve.tensor_scalar(tile(A, t), tile(A, t), -2.0, 0.0, ALU.add, ALU.min))
                if t >= 1:
                    m = t - 1
                    dve.wait_ge(squared.sem, sq0 + 2 * m + 2)
                    k.dve_step.mark(dve.scalar_tensor_tensor(tile(B, m), bsq[:, m % 2], -4.0, tile(B, m), ALU.mult, ALU.mult))
                    step(dve, k.dve_step, dve.tensor_tensor(tile(A, m), asq[:, m % 2], tile(A, m), ALU.mult))
                    bases.mark(dve.tensor_tensor(tile(B, m), tile(A, m), tile(B, m), ALU.add))
            for t in range(T):
                dve.wait_ge(product.sem, f0 + t + 1)
                xt = k.x[:, t, :].rearrange("p (b f) -> p b f", b=2)
                k.emptied.mark(dve.scalar_tensor_tensor(xt, halves(k.ps[0:P, t % 4, :]), -1.0 / 6.0, xt, ALU.mult, ALU.add))

        @block.tensor
        def _(pe):
            w = [k.slab(pe, s).rearrange("p (c d) -> p c d", c=C) for s in range(2)]
            for t in range(T):
                pe.wait_ge(bases.sem, ba0 + t + 1)
                wait(pe, k.emptied, e0 + t - 3 if t >= 4 else 0)
                product.mark(node_major(pe, k.ps[:, t % 4, :], lambda c: B[:, c, t * P:(t + 1) * P], lambda c: w[c // 4][:, c % 4, :], range(PAIRS)))
            release_slabs(k, pe, product, 2)


class NextHead:

    def __init__(self, k, h, hh, cols):
        self.k, self.h, self.hh, self.cols = k, h, hh, cols
        self.av = k.carve(P, 2, HID1)
        self.junk = k.carve(P, HID1)
        self.f0, self.e0, self.p0 = k.pe_step.n, k.emptied.n, k.params_in.n

    def bank(self, t):
        return self.k.ps[0:P, 3, t % 2 * 512:t % 2 * 512 + HID1]

    def load(self, sp):
        k, h = self.k, self.h
        for n, v in enumerate(("L1_gnn_a1_src", "L1_gnn_a1_dst")):
            k.params_in.mark_dma(sp.dma_start(self.av[:, n, :], k.a[v][0:P, h * HID1:(h + 1) * HID1]))

    def multiply(self, pe, t):
        k = self.k
        if t == 0:
            self.w = k.slab(pe)[:, 0:C * HID1].rearrange("p (c d) -> p c d", c=C)
        if t >= 2:
            pe.wait_ge(k.emptied.sem, self.e0 + t - 1)
        for c in range(C):
            last = pe.matmul(self.bank(t), k.xT[:, c, t * P:(t + 1) * P], self.w[:, c, :], start=c == 0, stop=c == C - 1)
        k.pe_step.mark(last)
        if t == T - 1:
            release_slabs(k, pe, k.pe_step, 1)

    def copy(self, act, t):
        k = self.k
        act.wait_ge(k.pe_step.sem, self.f0 + t + 1)
        k.emptied.mark(act.activation(self.hh[:, t, 0:HID1], self.bank(t), ACT.Copy))

    def project(self, dve, t):
        k = self.k
        if t == 0:
            dve.wait_ge(k.params_in.sem, self.p0 + 32)
        dve.wait_ge(k.emptied.sem, self.e0 + t + 1)
        for n in range(2):
            dve.wait_ge(k.dve_step.sem, k.dve_step.n)
            k.dve_step.mark(dve.tensor_tensor_reduce(self.junk, self.hh[:, t, 0:HID1], self.av[:, n, :], 1.0, 0.0, ALU.mult, ALU.add,
                                                     self.cols[:, n, t:t + 1]))


def pair_weights(k, as_col, ad_col, wt, tmp, beside=None):
    nc = k.nc
    diag, junk, tt, cols = tmp["diag"], tmp["junk"], tmp["t"], tmp["cols"]
    mx, pc, qc, as2 = cols[:, 0, :], cols[:, 1, :], cols[:, 2, :], cols[:, 3, :]
    ident = k.ident[0:P, 0:P].rearrange("p (o c) -> p o c", o=1).broadcast_to([P, T, P])
    spread_done, rows, linear, top, expd = k.dve_for_pe, k.filled, k.act_for_pe, k.dve_ready, k.act_ready
    d0, f0, lin0, top0, exp0 = spread_done.n, rows.n, linear.n, top.n, expd.n
    made = []
    with nc.Block() as block:
        @block.sync
        def _(sp):
            if beside:
                beside.load(sp)
            k.feed(sp, 1 if beside else 0)

        @block.vector
        def _(dve):
            def spread(n, col):
                c = col.rearrange("p (t o) -> p t o", o=1).broadcast_to([P, T, P])
                spread_done.mark(dve.tensor_tensor(diag[:, n, :].rearrange("p (t c) -> p t c", t=T), ident, c, ALU.mult))
            spread(0, as_col)
            k.dve_step.mark(dve.tensor_scalar(as2, as_col, SLOPE, None, ALU.mult))
            dve.wait_ge(rows.sem, f0 + 1)
            for j in range(T):
                step(dve, k.dve_step, dve.tensor_tensor_reduce(junk, tiles(k.ps[0:P, 0, :]), k.neg[:, j, :].rearrange("p (t s) -> p t s", t=T),
                                                               1.0, 3 * NEG, ALU.add, ALU.max, mx[:, j:j + 1]))
            step(dve, k.dve_step, dve.tensor_tensor(mx, mx, as_col, ALU.max))
            step(dve, k.dve_step, dve.tensor_tensor(mx, mx, ad_col, ALU.add))
            step(dve, k.dve_step, dve.scalar_tensor_tensor(mx, mx, SLOPE, mx, ALU.mult, ALU.max))
            k.dve_step.mark(dve.tensor_tensor(pc, ad_col, mx, ALU.subtract))
            step(dve, k.dve_step, dve.scalar_tensor_tensor(qc, ad_col, SLOPE, mx, ALU.mult, ALU.subtract))
            spread(1, pc)
            spread(2, qc)
            dve.wait_ge(rows.sem, f0 + 2)
            for i in range(T + 1):
                if i < T:
                    dve.wait_ge(linear.sem, lin0 + i + 1)
                    v = tt[:, i % 3, :].rearrange("p (t c) -> p t c", t=T)
                    top.mark(dve.scalar_tensor_tensor(v, tiles(k.ps[0:P, 1, :]), as_col[:, i:i + 1], v, ALU.add, ALU.max))
                if i >= 1:
                    m = i - 1
                    dve.wait_ge(expd.sem, exp0 + m + 1)
                    k.dve_step.mark(dve.scalar_tensor_tensor(wt[:, m, :], tt[:, m % 3, :], 1.0, k.cT[:, m, :], ALU.min, ALU.mult))
                    made.append(k.dve_step.n)
            if beside:
                for t in range(T):
                    beside.project(dve, t)

        @block.scalar
        def _(act):
            if beside:
                beside.copy(act, 0)
                beside.copy(act, 1)
            act.wait_ge(rows.sem, f0 + 2)
            for i in range(T + 1):
                if i < T:
                    if i >= 3:
                        act.wait_ge(k.dve_step.sem, made[i - 3])
                    v = tt[:, i % 3, :]
                    linear.mark(act.activation(v.rearrange("p (t c) -> p t c", t=T), tiles(k.ps[0:P, 2, :]), ACT.Identity, bias=as2[:, i:i + 1]))
                if i >= 1:
                    m = i - 1
                    act.wait_ge(top.sem, top0 + m + 1)
                    expd.mark(act.activation(tt[:, m % 3, :], tt[:, m % 3, :], ACT.Exp))
                if beside and i >= T - 1:
                    beside.copy(act, i - 2)
            if beside:
                beside.copy(act, T - 1)

        @block.tensor
        def _(pe):
            def spread_rows(n, slot):
                for t in range(T):
                    last = pe.matmul(k.ps[:, slot, t * 128:t * 128 + P], k.ones[0:P, :], diag[:, n, t * P:(t + 1) * P], start=True, stop=True)
                return last
            pe.wait_ge(spread_done.sem, d0 + 1)
            rows.mark(spread_rows(0, 0))
            if beside:
                beside.multiply(pe, 0)
                beside.multiply(pe, 1)
            pe.wait_ge(spread_done.sem, d0 + 3)
            spread_rows(1, 1)
            rows.mark(spread_rows(2, 2))
            if beside:
                for t in range(2, T):
                    beside.multiply(pe, t)


def pair_tmp(k):
    flat = k.xn[:, :, :].rearrange("p t d -> p (t d)")
    tmp = {"diag": flat[:, 0:3 * N].rearrange("p (n c) -> p n c", n=3),
           "junk": flat[:, 3 * N:4 * N].rearrange("p (t c) -> p t c", t=T),
           "t": flat[:, 3 * N:6 * N].rearrange("p (n c) -> p n c", n=3),
           "cols": flat[:, 6 * N:6 * N + 4 * T].rearrange("p (n c) -> p n c", n=4)}
    return tmp


def release_slabs(k, pe, count, n):
    pe.wait_ge(count.sem, count.n)
    pe.sem_inc(k.slab_free.sem, n)
    k.slab_free.n += n
    k.used += n


def gat1_head_stage(k, h, hh, cols, src, dst, width):
    nc, a = k.nc, k.a
    av = k.carve(P, 2, width)
    junk = k.carve(P, width)
    f0, e0, p0 = k.filled.n, k.emptied.n, k.params_in.n
    second = width == D
    chunks = 16 if second else C
    with nc.Block() as block:
        @block.sync
        def _(sp):
            for n, v in enumerate((src, dst)):
                rows = a[v][0:P, 0:D] if second else a[v][0:P, h * width:(h + 1) * width]
                k.params_in.mark_dma(sp.dma_start(av[:, n, :], rows))
            k.feed(sp, 3 if second else 1)

        @block.tensor
        def _(pe):
            if second:
                w = [k.slab(pe, s).rearrange("p (c d) -> p c d", c=C) for s in range(3)]
            else:
                w = k.slab(pe)[:, 0:C * HID1].rearrange("p (c d) -> p c d", c=C)
            for t in range(T):
                wait(pe, k.emptied, e0 + t - 3 if t >= 4 else 0)
                if second:
                    last = node_major(pe, k.ps[:, t % 4, :], lambda c: k.h2T[:, c, t * P:(t + 1) * P], lambda c: w[c // 6][:, c % 6, :], range(chunks))
                else:
                    for c in range(C):
                        last = pe.matmul(k.ps[0:P, t % 4, 0:HID1], k.xT[:, c, t * P:(t + 1) * P], w[:, c, :], start=c == 0, stop=c == C - 1)
                k.filled.mark(last)
            release_slabs(k, pe, k.filled, 3 if second else 1)

        @block.scalar
        def _(act):
            for t in range(T):
                act.wait_ge(k.filled.sem, f0 + t + 1)
                if second:
                    k.emptied.mark(act.activation(hh[:, t, 0:D].rearrange("p (b f) -> p b f", b=2), halves(k.ps[0:P, t % 4, :]), ACT.Copy))
                else:
                    k.emptied.mark(act.activation(hh[:, t, 0:HID1], k.ps[0:P, t % 4, 0:HID1], ACT.Copy))

        @block.vector
        def _(dve):
            k.dve_step.mark(dve.memset(hh[:, :, width:width + 1], 1.0))
            dve.wait_ge(k.params_in.sem, p0 + 32)
            for t in range(T):
                dve.wait_ge(k.emptied.sem, e0 + t + 1)
                for n in range(2):
                    dve.wait_ge(k.dve_step.sem, k.dve_step.n)
                    k.dve_step.mark(dve.tensor_tensor_reduce(junk, hh[:, t, 0:width], av[:, n, :], 1.0, 0.0, ALU.mult, ALU.add,
                                                             cols[:, n, t:t + 1]))


def gat1_gather_stage(k, h, hh, wt):
    nc, a = k.nc, k.a
    rden = k.carve(128, N)
    e = k.carve(128, 2, N)
    bcol = k.carve(128, 4)
    f0, e0, p0, r0, a0, s0 = k.filled.n, k.emptied.n, k.params_in.n, k.dve_ready.n, k.act_ready.n, k.dve_step.n
    FC = HID1 // 128
    with nc.Block() as block:
        @block.sync
        def _(sp):
            k.params_in.mark_dma(sp.dma_start(bcol, a["L1_gnn_b1"][:, h * FC:(h + 1) * FC]))
            k.feed(sp, 0)

        @block.tensor
        def _(pe):
            k.filled.mark(feature_major(pe, k.ps[:, 3, :], 128, lambda i: k.ones[0:P, :], lambda i: wt[:, i, :], range(T)))
            for f in range(FC):
                wait(pe, k.emptied, e0 + f - 2 if f >= 3 else 0)
                k.filled.mark(feature_major(pe, k.ps[:, f % 3, :], 128, lambda i: hh[:, i, f * 128:(f + 1) * 128], lambda i: wt[:, i, :], range(T)))

        @block.vector
        def _(dve):
            dve.wait_ge(k.filled.sem, f0 + 1)
            step(dve, k.dve_step, dve.tensor_scalar(rden, k.ps[:, 3, 0:N], 1e-16, None, ALU.add))
            step(dve, k.dve_step, dve.reciprocal(rden, rden))
            dve.wait_ge(k.params_in.sem, p0 + 16)
            for f in range(FC + 1):
                if f < FC:
                    R = k.h2T[:, h * FC + f, :]
                    dve.wait_ge(k.filled.sem, f0 + 2 + f)
                    k.emptied.mark(dve.tensor_tensor(R, k.ps[:, f % 3, 0:N], rden, ALU.mult))
                    dve.wait_ge(k.emptied.sem, k.emptied.n)
                    step(dve, k.dve_step, dve.tensor_scalar(R, R, bcol[:, f:f + 1], None, ALU.add))
                    k.dve_ready.mark(dve.tensor_scalar(e[:, f % 2, :], R, 0.0, None, ALU.min))
                    step(dve, k.dve_step, dve.tensor_scalar(R, R, 0.0, -1.0, ALU.max, ALU.add))
                if f >= 1:
                    dve.wait_ge(k.act_ready.sem, a0 + f)
                    R = k.h2T[:, h * FC + f - 1, :]
                    step(dve, k.dve_step, dve.tensor_tensor(R, R, e[:, (f - 1) % 2, :], ALU.add))

        @block.scalar
        def _(act):
            for f in range(FC):
                act.wait_ge(k.dve_ready.sem, r0 + f + 1)
                k.act_ready.mark(act.activation(e[:, f % 2, :], e[:, f % 2, :], ACT.Exp))


def add_scaled_stage(k, lhs, rhs, slabs, finish, width=D):
    nc = k.nc
    f0, e0 = k.filled.n, k.emptied.n
    with nc.Block() as block:
        @block.sync
        def _(sp):
            k.feed(sp, slabs)

        @block.tensor
        def _(pe):
            for t in range(T):
                wait(pe, k.emptied, e0 + t - 3 if t >= 4 else 0)
                for i in range(T):
                    for lo, hi in ((0, min(512, width)), (512, width)):
                        if hi > lo:
                            last = pe.matmul(k.ps[0:P, t % 4, lo:hi], lhs(i, t), rhs(i)[:, lo:hi], start=i == 0, stop=i == T - 1)
                k.filled.mark(last)

        @block.vector
        def _(dve):
            for t in range(T):
                dve.wait_ge(k.filled.sem, f0 + t + 1)
                finish(dve, t, k.ps[0:P, t % 4, :])


def gat1(k):
    a = k.a
    norm_stage(k)
    k.reset()
    k.h2T = k.carve(128, 16, N)
    hh = [k.carve(P, T, HID1 + 1) for _ in range(2)]
    cols = [k.carve(P, 2, T) for _ in range(2)]
    wt = k.carve(P, T, N)
    keep = k.at
    loops_stage(k, 1.0, ones=[b[:, :, HID1:HID1 + 1] for b in hh])
    gat1_head_stage(k, 0, hh[0], cols[0], "L1_gnn_a1_src", "L1_gnn_a1_dst", HID1)
    for h in range(H_L1):
        k.reset(keep)
        beside = NextHead(k, h + 1, hh[(h + 1) % 2], cols[(h + 1) % 2]) if h + 1 < H_L1 else None
        pair_weights(k, cols[h % 2][:, 0, :], cols[h % 2][:, 1, :], wt, pair_tmp(k), beside)
        k.reset(keep)
        gat1_gather_stage(k, h, hh[h % 2], wt)
    k.reset(16 * N)
    hh = k.carve(P, T, D + 1)
    cols = k.carve(P, 2, T)
    keep = k.at
    gat1_head_stage(k, 0, hh, cols, "L1_gnn_a2_src", "L1_gnn_a2_dst", D)
    k.reset(0)
    wt = k.carve(P, T, N)
    b2 = k.carve(P, D)
    r = k.carve(P, D)
    rden = k.carve(P, 1)
    pair_weights(k, cols[:, 0, :], cols[:, 1, :], wt, pair_tmp(k))
    load_stage(k, [(b2, a["L1_gnn_b2"][0:P, :])])

    def finish(dve, t, ps):
        step(dve, k.dve_step, dve.tensor_scalar(rden, ps[:, D:D + 1], 1e-16, None, ALU.add))
        step(dve, k.dve_step, dve.reciprocal(rden, rden))
        k.emptied.mark(dve.scalar_tensor_tensor(r, ps[:, 0:D], rden, b2, ALU.mult, ALU.add))
        dve.wait_ge(k.emptied.sem, k.emptied.n)
        step(dve, k.dve_step, dve.tensor_tensor(k.x[:, t, :], k.x[:, t, :], r, ALU.add))
    add_scaled_stage(k, lambda i, t: wt[:, i, t * P:(t + 1) * P], lambda i: hh[:, i, :], 0, finish, D + 1)


def load_stage(k, loads):
    with k.nc.Block() as block:
        @block.sync
        def _(sp):
            for dst, src in loads:
                k.params_in.mark_dma(sp.dma_start(dst, src))
            sp.wait_ge(k.params_in.sem, k.params_in.n)
            k.feed(sp, 0)


def loops_stage(k, sign, ones=()):
    with k.nc.Block() as block:
        @block.vector
        def _(dve):
            for t in range(T):
                d = k.cT[:, t, t * P:(t + 1) * P]
                k.dve_step.mark(dve.scalar_tensor_tensor(d, k.ident[0:P, 0:P], sign, d, ALU.mult, ALU.add))
            k.dve_step.mark(dve.tensor_scalar(k.deg[:, :], k.deg[:, :], sign, None, ALU.add))
            for columns in ones:
                k.dve_step.mark(dve.memset(columns, 1.0))


def route_stage(k, w_name, comb, bias_name, top, rank=None):
    nc, a = k.nc, k.a
    X8 = EXPERTS
    wr = k.carve(128, C, X8)
    sc = k.carve(P, T, X8)
    sel = k.carve(P, T, X8)
    big = k.carve(P, T, X8, X8)
    bi2 = k.carve(P, T, X8, X8)
    low = k.carve(P, X8, X8)
    mx = k.carve(P, T)
    bias = k.carve(P, X8)
    f0, p0, r0, a0 = k.filled.n, k.params_in.n, k.dve_ready.n, k.act_ready.n
    po0 = k.pool_step.n
    with nc.Block() as block:
        @block.sync
        def _(sp):
            k.params_in.mark_dma(sp.dma_start(wr, a[w_name].rearrange("p (c e) -> p c e", c=C)))
            if bias_name:
                k.params_in.mark_dma(sp.dma_start(bias, a[bias_name][0:P, :]))
            k.feed(sp, 0)

        @block.gpsimd
        def _(pool):
            step(pool, k.pool_step, pool.memset(low, 1.0))
            k.pool_step.mark(pool.affine_select(out=low, in_=low, compare_op=ALU.is_gt, fill=0.0, base=0,
                                                pattern=[[1, X8], [-1, X8]], channel_multiplier=0))

        @block.tensor
        def _(pe):
            pe.wait_ge(k.params_in.sem, p0 + 16 * (2 if bias_name else 1))
            for t in range(T):
                for c in range(C):
                    last = pe.matmul(k.ps[0:P, 0, t * X8:(t + 1) * X8], k.xT[:, c, t * P:(t + 1) * P], wr[:, c, :],
                                     start=c == 0, stop=c == C - 1, skip_group_check=True)
            k.filled.mark(last)

        @block.vector
        def _(dve):
            def cast(v):
                return v.rearrange("p (t o) -> p t o", o=1).broadcast_to([P, T, X8])
            dve.wait_ge(k.params_in.sem, p0 + 16 * (2 if bias_name else 1))
            dve.wait_ge(k.filled.sem, f0 + 1)
            lg = k.ps[0:P, 0, 0:T * X8].rearrange("p (t e) -> p t e", t=T)
            step(dve, k.dve_step, dve.tensor_reduce(mx, lg, AX, ALU.max))
            k.dve_ready.mark(dve.tensor_tensor(sc, lg, cast(mx), ALU.subtract))
            dve.wait_ge(k.act_ready.sem, a0 + 1)
            step(dve, k.dve_step, dve.tensor_reduce(mx, sc, AX, ALU.add))
            step(dve, k.dve_step, dve.reciprocal(mx, mx))
            step(dve, k.dve_step, dve.tensor_tensor(sc, sc, cast(mx), ALU.mult))
            if bias_name:
                step(dve, k.dve_step, dve.tensor_tensor(sel, sc, bias.rearrange("p (o e) -> p o e", o=1).broadcast_to([P, T, X8]), ALU.add))
            else:
                step(dve, k.dve_step, dve.tensor_copy(sel, sc))
            dve.wait_ge(k.pool_step.sem, po0 + 2)
            for t in range(T):
                me = sel[:, t, :].rearrange("p (e o) -> p e o", o=1).broadcast_to([P, X8, X8])
                other = sel[:, t, :].rearrange("p (o e) -> p o e", o=1).broadcast_to([P, X8, X8])
                k.dve_step.mark(dve.tensor_tensor(big[:, t], other, me, ALU.is_gt))
                step(dve, k.dve_step, dve.tensor_tensor(bi2[:, t], other, me, ALU.is_equal))
                step(dve, k.dve_step, dve.tensor_tensor(bi2[:, t], bi2[:, t], low, ALU.mult))
                step(dve, k.dve_step, dve.tensor_tensor(big[:, t], big[:, t], bi2[:, t], ALU.add))
                step(dve, k.dve_step, dve.tensor_reduce(sel[:, t, :], big[:, t], AX, ALU.add))
            if rank is not None:
                k.dve_step.mark(dve.tensor_copy(rank, sel))
            step(dve, k.dve_step, dve.tensor_scalar(sel, sel, float(top), None, ALU.is_lt))
            step(dve, k.dve_step, dve.tensor_tensor(comb, sel, sc, ALU.mult))
            if top > 1:
                step(dve, k.dve_step, dve.tensor_reduce(mx, comb, AX, ALU.add))
                step(dve, k.dve_step, dve.tensor_scalar(mx, mx, 1e-9, None, ALU.add))
                step(dve, k.dve_step, dve.reciprocal(mx, mx))
                step(dve, k.dve_step, dve.tensor_tensor(comb, comb, cast(mx), ALU.mult))

        @block.scalar
        def _(act):
            act.wait_ge(k.dve_ready.sem, r0 + 1)
            k.act_ready.mark(act.activation(sc, sc, ACT.Exp))


def dispatch_stage(k, rank, comb, slot, weight, idx, need):
    nc = k.nc
    X8 = EXPERTS
    mask = k.carve(P, T, X8)
    pos = k.carve(P, T, X8)
    pick = k.carve(P, 2, T * X8)
    base = k.carve(P, X8)
    tri = k.carve(P, P)
    node = k.carve(P, T)
    zero = k.carve(128, EXPERTS * BLOCKS)
    slotf = k.carve(P, 2, T)
    listed = k.carve(EXPERTS * BLOCKS, 128)
    r0, f0, po0, st0, sc0, p0, x0 = k.dve_for_pe.n, k.filled.n, k.pool_step.n, k.stored.n, k.scattered.n, k.params_in.n, k.dve_ready.n
    with nc.Block() as block:
        @block.sync
        def _(sp):
            k.stored.mark_dma(sp.dma_start(k.xn_d.rearrange("(t p) d -> p t d", p=P), k.xn[:, :, :]))
            sp.wait_ge(k.pool_step.sem, po0 + 1)
            k.stored.mark_dma(sp.dma_start(k.lists.rearrange("(p c) o -> p (c o)", p=128), zero))
            sp.wait_ge(k.stored.sem, k.stored.n)
            sp.wait_ge(k.scattered.sem, sc0 + 16 * 2 * T)
            k.params_in.mark_dma(sp.dma_start(listed, k.lists.rearrange("(c p) o -> c (p o)", p=128)))
            k.feed(sp, 0)

        @block.gpsimd
        def _(pool):
            step(pool, k.pool_step, pool.memset(zero, 0.0))
            step(pool, k.pool_step, pool.iota(node, [[P, T]], base=0, channel_multiplier=1, allow_small_or_imprecise_dtypes=True))
            step(pool, k.pool_step, pool.iota(base, [[LIST, X8]], base=0, channel_multiplier=0, allow_small_or_imprecise_dtypes=True))
            step(pool, k.pool_step, pool.memset(tri, 1.0))
            step(pool, k.pool_step, pool.affine_select(out=tri, in_=tri, compare_op=ALU.is_gt, fill=0.0, base=0,
                                                       pattern=[[1, P]], channel_multiplier=-1))
            pool.wait_ge(k.dve_ready.sem, x0 + 1)
            pool.wait_ge(k.stored.sem, st0 + 32)
            for c in range(2):
                for t in range(T):
                    k.scattered.mark_dma(pool.indirect_dma_start(
                        k.lists, bass.IndirectOffsetOnAxis(ap=slot[:, c, t:t + 1], axis=0), node[:, t:t + 1], None))
            pool.wait_ge(k.scattered.sem, k.scattered.n)

        @block.vector
        def _(dve):
            k.dve_for_pe.mark(dve.tensor_scalar(mask, rank, 2.0, None, ALU.is_lt))
            dve.wait_ge(k.filled.sem, f0 + 1)
            dve.wait_ge(k.pool_step.sem, po0 + 3)
            k.dve_step.mark(dve.tensor_copy(need[0:1, :], k.ps[0:1, 1, 0:X8]))
            step(dve, k.dve_step, dve.tensor_tensor(pos, k.ps[0:P, 0, 0:T * X8].rearrange("p (t e) -> p t e", t=T),
                                                    base.rearrange("p (o e) -> p o e", o=1).broadcast_to([P, T, X8]), ALU.add))
            for c in range(2):
                a, b = (pick[:, i, :].rearrange("p (t e) -> p t e", t=T) for i in range(2))
                step(dve, k.dve_step, dve.tensor_scalar(a, rank, float(c), None, ALU.is_equal))
                step(dve, k.dve_step, dve.tensor_tensor(b, a, pos, ALU.mult))
                step(dve, k.dve_step, dve.tensor_reduce(slotf[:, c, :], b, AX, ALU.add))
                step(dve, k.dve_step, dve.tensor_tensor(b, a, comb, ALU.mult))
                step(dve, k.dve_step, dve.tensor_reduce(weight[:, c, :], b, AX, ALU.add))
            k.dve_ready.mark(dve.tensor_copy(slot, slotf))
            dve.wait_ge(k.filled.sem, f0 + 2)
            k.dve_step.mark(dve.tensor_copy(idx, k.ps[:, 2, 0:EXPERTS * BLOCKS]))

        @block.tensor
        def _(pe):
            pe.wait_ge(k.dve_for_pe.sem, r0 + 1)
            pe.wait_ge(k.pool_step.sem, po0 + 5)
            for t in range(T):
                for i in range(t + 1):
                    pe.matmul(k.ps[0:P, 0, t * X8:(t + 1) * X8], k.ones[0:P, 0:P] if i < t else tri, mask[:, i, :],
                              start=i == 0, stop=i == t, skip_group_check=True)
            for i in range(T):
                last = pe.matmul(k.ps[0:1, 1, 0:X8], k.ones[0:P, 0:1], mask[:, i, :], start=i == 0, stop=i == T - 1)
            k.filled.mark(last)
            pe.wait_ge(k.params_in.sem, p0 + 16)
            k.filled.mark(pe.transpose(k.ps[:, 2, 0:EXPERTS * BLOCKS], listed, k.ident[0:EXPERTS * BLOCKS, 0:EXPERTS * BLOCKS]))


def either(eng, cond, counts, work):
    if cond is None:
        work()
        return
    before = [c.n for c in counts]
    with eng.If(cond):
        work()
    with eng.Else():
        for c, n in zip(counts, before):
            wait(eng, c, n)
            eng.sem_inc(c.sem, c.n - n)


def experts_stage(k, slot, weight, idx, need):
    nc = k.nc
    HS = FF // SIX
    XT = k.carve(128, 2, BLOCKS * C * 128)
    Y = k.carve(128, 2, BLOCKS * D)
    rows = k.carve(128, 2, D)
    sg = k.carve(128, 2, HS)
    hid = k.carve(128, 2, HS)
    hidT = k.carve(128, 2, HS)
    units = [(q, s, b) for q in range(EXPERTS + 1) for s in range(SIX) for b in range(BLOCKS)]
    NU = len(units)
    up, tr, down, silu, hidden, copied, added = (k.filled, k.pe_step, k.pe_down, k.act_ready, k.dve_for_pe, k.act_for_pe, k.emptied)
    up0, tr0, down0, silu0, hidden0, copied0, added0 = (c.n for c in (up, tr, down, silu, hidden, copied, added))
    turned, xt_ready = k.rows_turned, k.act_step
    turned0, xt0 = turned.n, xt_ready.n
    in0 = [g.n for g in k.gathered]
    take0 = k.dve_ready.n
    taken = XT.rearrange("p h w -> p (h w)")[:, 0:T * D].rearrange("p (t d) -> p t d", t=T)
    psum_up = [k.ps[:, 0, 0:512], k.ps[:, 0, 512:1024]]
    psum_tr = [k.ps[:, 1, 0:2 * 128], k.ps[:, 1, 512:512 + 2 * 128]]

    def parts(q):
        return P if q == 0 else 128

    def reach(eng):
        return [eng.value_load(need[0:1, e:e + 1]) for e in range(EXPERTS)]

    def cond(lengths, q, b):
        return None if q == 0 else lengths[q - 1] > 128 * b

    with nc.Block() as block:
        @block.sync
        def _(sp):
            k.feed(sp, SIX * (EXPERTS + 1), lambda i: (down, down0 + BLOCKS * (i + 1)))

        @block.gpsimd
        def _(pool):
            for q in range(EXPERTS):
                for b in range(BLOCKS):
                    g = q * BLOCKS + b
                    if g >= 2:
                        pool.wait_ge(turned.sem, turned0 + g - 1)
                    k.gathered[g % 2].mark_dma(pool.indirect_dma_start(
                        rows[:, g % 2, :], None, k.xn_d, bass.IndirectOffsetOnAxis(ap=idx[:, g:g + 1], axis=0)))
            for b in range(BLOCKS):
                for e in range(2):
                    pool.wait_ge(k.y_out[e][b].sem, 16 * EXPERTS // 2)
            for n in range(2 * T):
                if n >= T:
                    pool.wait_ge(k.dve_ready.sem, take0 + n - T + 1)
                k.gathered[n % T].mark_dma(pool.indirect_dma_start(
                    taken[0:P, n % T, :], None, k.y_d, bass.IndirectOffsetOnAxis(ap=slot[:, n // T, n % T:n % T + 1], axis=0)))

        @block.tensor
        def _(pe):
            n_list = reach(pe)
            slab = None
            for n in range(NU + 2):
                if n < NU:
                    q, s, b = units[n]
                    M = parts(q)
                    if b == 0:
                        slab = k.slab(pe, q * SIX + s)
                    w = slab[:, 0:C * 2 * HS].rearrange("p (c f) -> p c f", c=C)

                    def up_work():
                        if s == 0 and q > 0:
                            pe.wait_ge(xt_ready.sem, xt0 + (q - 1) * BLOCKS + b + 1)
                        if n >= 2:
                            pe.wait_ge(hidden.sem, hidden0 + n - 1)
                        for c in range(C):
                            x = k.xT[:, c, b * P:(b + 1) * P] if q == 0 else XT[:, q % 2, (b * C + c) * 128:(b * C + c + 1) * 128]
                            last = pe.matmul(psum_up[n % 2][0:M, :], x, w[:, c, :], start=c == 0, stop=c == C - 1)
                        up.mark(last)
                    either(pe, cond(n_list, q, b), [up], up_work)
                if 1 <= n <= NU:
                    m = n - 1
                    q, s, b = units[m]
                    M = parts(q)

                    def turn_work():
                        pe.wait_ge(hidden.sem, hidden0 + m + 1)
                        if m >= 2:
                            pe.wait_ge(copied.sem, copied0 + m - 1)
                        for i in range(2):
                            last = pe.transpose(psum_tr[m % 2][:, i * 128:i * 128 + M], hid[0:M, m % 2, i * 128:(i + 1) * 128], k.ident[0:M, 0:M])
                        tr.mark(last)
                    either(pe, cond(n_list, q, b), [tr], turn_work)
                if n >= 2:
                    m = n - 2
                    q, s, b = units[m]
                    M = parts(q)
                    wd = k.ring[:, (k.used + q * SIX + s) % RING, C * 2 * HS:].rearrange("p (i d) -> p i d", i=2)

                    def down_work():
                        pe.wait_ge(copied.sem, copied0 + m + 1)
                        if m >= 1:
                            pe.wait_ge(added.sem, added0 + m)
                        for i in range(2):
                            for h in range(2):
                                last = pe.matmul(k.ps[0:M, 2, h * 512:h * 512 + HALF], hidT[:, m % 2, i * 128:i * 128 + M], wd[:, i, h * HALF:(h + 1) * HALF],
                                                 start=i == 0, stop=i == 1)
                        down.mark(last)
                    either(pe, cond(n_list, q, b), [down], down_work)
                if n < NU:
                    q, s, b = units[n]
                    if b == BLOCKS - 1 and s < BLOCKS and q < EXPERTS:
                        g = q * BLOCKS + s
                        pe.wait_ge(k.gathered[g % 2].sem, in0[g % 2] + 16 * (g // 2 + 1))

                        def rows_work():
                            wait(pe, xt_ready, xt0 + g if g else 0)
                            for c in range(C):
                                last = pe.transpose(k.ps[:, 3, c * 128:(c + 1) * 128], rows[:, g % 2, c * 128:(c + 1) * 128], k.ident[:, :])
                            turned.mark(last)
                        either(pe, cond(n_list, q + 1, s), [turned], rows_work)
            pe.wait_ge(down.sem, down.n)
            pe.sem_inc(k.slab_free.sem, SIX * (EXPERTS + 1))
            k.slab_free.n += SIX * (EXPERTS + 1)
            k.used += SIX * (EXPERTS + 1)

        @block.scalar
        def _(act):
            n_list = reach(act)

            def write_rows(q):
                for b in range(BLOCKS):
                    def write():
                        act.wait_ge(added.sem, added0 + (q * SIX + SIX - 1) * BLOCKS + b + 1)
                        r = (q - 1) * LIST + b * 128
                        wait(act, k.y_out[q % 2][b], k.y_out[q % 2][b].n)
                        k.y_out[q % 2][b].mark_dma(act.dma_start(k.y_d[r:r + 128, :], Y[:, q % 2, b * D:(b + 1) * D]))
                    either(act, cond(n_list, q, b), [k.y_out[q % 2][b]], write)

            for n in range(NU + 1):
                if n % (SIX * BLOCKS) == BLOCKS and n > 2 * BLOCKS + SIX * BLOCKS:
                    write_rows(n // (SIX * BLOCKS) - 1)
                if n < NU:
                    q, s, b = units[n]
                    M = parts(q)

                    def silu_work():
                        act.wait_ge(up.sem, up0 + n + 1)
                        if n >= 2:
                            act.wait_ge(hidden.sem, hidden0 + n - 1)
                        silu.mark(act.activation(sg[0:M, n % 2, :], psum_up[n % 2][0:M, 0:HS], ACT.Silu))
                    either(act, cond(n_list, q, b), [silu], silu_work)
                if n >= 1:
                    m = n - 1
                    q, s, b = units[m]
                    M = parts(q)

                    def copy_work():
                        act.wait_ge(tr.sem, tr0 + m + 1)
                        if m >= 2:
                            act.wait_ge(down.sem, down0 + m - 1)
                        o = hidT[:, m % 2, :].rearrange("p (i t) -> p i t", i=2)[:, :, 0:M]
                        copied.mark(act.activation(o, psum_tr[m % 2].rearrange("p (i t) -> p i t", i=2)[:, :, 0:M], ACT.Copy))
                    either(act, cond(n_list, q, b), [copied], copy_work)
                if n < NU:
                    q, s, b = units[n]
                    if b == BLOCKS - 1 and s < BLOCKS and q < EXPERTS:
                        g = q * BLOCKS + s

                        def xt_work():
                            act.wait_ge(turned.sem, turned0 + g + 1)
                            xt_ready.mark(act.activation(XT[:, (q + 1) % 2, s * C * 128:(s + 1) * C * 128], k.ps[:, 3, 0:C * 128], ACT.Copy))
                        either(act, cond(n_list, q + 1, s), [xt_ready], xt_work)
            write_rows(EXPERTS)

        @block.vector
        def _(dve):
            n_list = reach(dve)
            for n in range(NU + 2):
                if n < NU:
                    q, s, b = units[n]
                    M = parts(q)

                    def hidden_work():
                        dve.wait_ge(silu.sem, silu0 + n + 1)
                        if n >= 2:
                            dve.wait_ge(tr.sem, tr0 + n - 1)
                        hidden.mark(dve.tensor_tensor(hid[0:M, n % 2, :], sg[0:M, n % 2, :], psum_up[n % 2][0:M, HS:2 * HS], ALU.mult))
                    either(dve, cond(n_list, q, b), [hidden], hidden_work)
                if n >= 2:
                    m = n - 2
                    q, s, b = units[m]
                    M = parts(q)

                    def add_work():
                        dve.wait_ge(down.sem, down0 + m + 1)
                        wait(dve, added, added0 + m if m else 0)
                        out = halves(k.ps[0:M, 2, :])
                        if q == 0:
                            y = k.x[:, b, :].rearrange("p (h f) -> p h f", h=2)
                        else:
                            y = Y[:, q % 2, b * D:(b + 1) * D].rearrange("p (h f) -> p h f", h=2)
                        if q > 0 and s == 0:
                            if q >= 3:
                                dve.wait_ge(k.y_out[q % 2][b].sem, 16 * ((q - 1) // 2))
                            added.mark(dve.tensor_copy(y, out))
                        else:
                            added.mark(dve.tensor_tensor(y, y, out, ALU.add))
                    either(dve, cond(n_list, q, b), [added], add_work)
            for n in range(2 * T):
                c, t = n // T, n % T
                tokens = 16 * (EXPERTS * BLOCKS // 2) if t < 2 else 0
                dve.wait_ge(k.gathered[t].sem, in0[t] + tokens + 16 * (c + 1))
                wait(dve, k.dve_ready, k.dve_ready.n)
                k.dve_ready.mark(dve.scalar_tensor_tensor(k.x[:, t, :], taken[0:P, t, :], weight[:, c, t:t + 1], k.x[:, t, :], ALU.mult, ALU.add))


def gcn_project_stage(k, hs, dinv, bias):
    nc = k.nc
    f0, e0, rs0 = k.filled.n, k.emptied.n, k.std_ready.n
    with nc.Block() as block:
        @block.sync
        def _(sp):
            k.params_in.mark_dma(sp.dma_start(*bias))
            k.feed(sp, 1)
            sp.wait_ge(k.params_in.sem, k.params_in.n)

        @block.tensor
        def _(pe):
            w = k.slab(pe).rearrange("p (c d) -> p c d", c=C)
            for t in range(T):
                wait(pe, k.emptied, e0 + t - 3 if t >= 4 else 0)
                k.filled.mark(node_major(pe, k.ps[:, t % 4, :], lambda c: k.xT[:, c, t * P:(t + 1) * P], lambda c: w[:, c, :], range(C)))
            release_slabs(k, pe, k.filled, 1)

        @block.scalar
        def _(act):
            k.std_ready.mark(act.activation(dinv, k.deg[:, :], ACT.Sqrt))

        @block.vector
        def _(dve):
            dve.wait_ge(k.std_ready.sem, rs0 + 1)
            step(dve, k.dve_step, dve.reciprocal(dinv, dinv))
            for t in range(T):
                dve.wait_ge(k.filled.sem, f0 + t + 1)
                k.emptied.mark(dve.tensor_scalar(hs[:, t, :].rearrange("p (b f) -> p b f", b=2), halves(k.ps[0:P, t % 4, :]),
                                                 dinv[:, t:t + 1], None, ALU.mult))


def gcn(k):
    a = k.a
    k.reset()
    hs = k.carve(P, T, D)
    dinv = k.carve(P, T)
    bias = k.carve(P, D)
    r = k.carve(P, D)
    for layer, b in ((0, "L2_gnn_b1"), (1, "L2_gnn_b2")):
        norm_stage(k, normalise=layer == 0)
        gcn_project_stage(k, hs, dinv, (bias, a[b][0:P, :]))

        def finish(dve, t, ps):
            k.emptied.mark(dve.scalar_tensor_tensor(r, ps[:, 0:D], dinv[:, t:t + 1], bias, ALU.mult, ALU.add))
            dve.wait_ge(k.emptied.sem, k.emptied.n)
            if layer == 0:
                step(dve, k.dve_step, dve.tensor_scalar(k.xn[:, t, :], r, 0.0, None, ALU.max))
            else:
                step(dve, k.dve_step, dve.tensor_tensor(k.x[:, t, :], k.x[:, t, :], r, ALU.add))
        add_scaled_stage(k, lambda i, t: k.cT[:, i, t * P:(t + 1) * P], lambda i: hs[:, i, :], 0, finish)


def sign_ffn(k):
    nc = k.nc
    norm_stage(k)
    f0, e0, a0 = k.filled.n, k.emptied.n, k.act_for_pe.n
    with nc.Block() as block:
        @block.sync
        def _(sp):
            k.feed(sp, 1)

        @block.scalar
        def _(act):
            w = k.slab(act)
            for c in range(C):
                k.act_for_pe.mark(act.activation(w[:, c * D:(c + 1) * D], w[:, c * D:(c + 1) * D], ACT.Sign))

        @block.tensor
        def _(pe):
            pe.wait_ge(k.act_for_pe.sem, a0 + C)
            w = k.slab(pe).rearrange("p (c d) -> p c d", c=C)
            for t in range(T):
                wait(pe, k.emptied, e0 + t - 3 if t >= 4 else 0)
                k.filled.mark(node_major(pe, k.ps[:, t % 4, :], lambda c: k.xT[:, c, t * P:(t + 1) * P], lambda c: w[:, c, :], range(C)))
            release_slabs(k, pe, k.filled, 1)

        @block.vector
        def _(dve):
            for t in range(T):
                dve.wait_ge(k.filled.sem, f0 + t + 1)
                xt = k.x[:, t, :].rearrange("p (b f) -> p b f", b=2)
                k.emptied.mark(dve.tensor_tensor(xt, halves(k.ps[0:P, t % 4, :]), xt, ALU.add))


def gat3(k):
    nc, a = k.nc, k.a
    norm_stage(k)
    k.reset()
    HD3 = 64
    ft = k.carve(P, T, H_L3, HD3 + 1)
    res = k.carve(P, T, D)
    asd = k.carve(P, 2, H_L3, T)
    keep = k.at
    bd = k.carve(128, 256)
    av = k.carve(P, 2, D)
    junk = k.carve(P, D)
    f0, e0, p0, s0 = k.filled.n, k.emptied.n, k.params_in.n, k.dve_ready.n
    with nc.Block() as block:
        @block.vector
        def _(dve):
            k.dve_ready.mark(dve.memset(bd, 0.0))
            k.dve_step.mark(dve.memset(ft[:, :, :, HD3:HD3 + 1], 1.0))
            dve.wait_ge(k.params_in.sem, p0 + 16 * 6)
            for t in range(T):
                for c2 in range(3):
                    n = t * 3 + c2
                    dve.wait_ge(k.filled.sem, f0 + n + 1)
                    ps = wide(k.ps[0:P, n % 4, :])[:, :, 0:256].rearrange("p b (w h f) -> p b w h f", w=2, h=2)
                    for b in range(2):
                        k.dve_step.mark(dve.tensor_copy(ft[:, t, 4 * c2 + 2 * b:4 * c2 + 2 * b + 2, 0:HD3], ps[:, b, 0]))
                    k.emptied.mark(dve.tensor_copy(res[:, t, c2 * 256:(c2 + 1) * 256].rearrange("p (b h f) -> p b h f", b=2, f=HD3), ps[:, :, 1]))
                for n in range(2):
                    dve.wait_ge(k.dve_step.sem, k.dve_step.n)
                    step(dve, k.dve_step, dve.tensor_tensor(junk.rearrange("p (h f) -> p h f", f=HD3), ft[:, t, :, 0:HD3],
                                                            av[:, n, :].rearrange("p (h f) -> p h f", f=HD3), ALU.mult))
                    step(dve, k.dve_step, dve.tensor_reduce(asd[:, n, :, t], junk.rearrange("p (h f) -> p h f", f=HD3), AX, ALU.add))

        @block.sync
        def _(sp):
            sp.wait_ge(k.dve_ready.sem, s0 + 1)
            for n, w in enumerate(("L3_gnn_W", "L3_gnn_W_res")):
                for q in range(2):
                    k.params_in.mark_dma(sp.dma_start(bd[64 * q:64 * q + 64, n * 128 + 64 * q:n * 128 + 64 * q + 64], a[w]))
            for n, v in enumerate(("L3_gnn_attn_l", "L3_gnn_attn_r")):
                k.params_in.mark_dma(sp.dma_start(av[:, n, :], a[v][0:P, :]))
            k.feed(sp, 0)

        @block.tensor
        def _(pe):
            pe.wait_ge(k.params_in.sem, p0 + 16 * 6)
            for t in range(T):
                for c2 in range(3):
                    n = t * 3 + c2
                    if n >= 4:
                        pe.wait_ge(k.emptied.sem, e0 + n - 3)
                    for b in range(2):
                        last = pe.matmul(k.ps[0:P, n % 4, b * 512:b * 512 + 256], k.xT[:, 2 * c2 + b, t * P:(t + 1) * P], bd, start=True, stop=True)
                    k.filled.mark(last)
    k.reset(keep)
    gat3_heads_stage(k, ft, res, asd)


def gat3_heads_stage(k, ft, res, asd):
    nc = k.nc
    H, HD3 = H_L3, 64
    flat = k.xn[:, :, :].rearrange("p t d -> p (t d)")
    da = flat[:, 0:2 * N].rearrange("p (n c) -> p n c", n=2)
    junk = flat[:, 2 * N:3 * N].rearrange("p (t c) -> p t c", t=T)
    q = flat[:, 3 * N:3 * N + T * HD3].rearrange("p (t f) -> p t f", t=T)
    rden = flat[:, 3 * N + T * HD3:3 * N + T * HD3 + T]
    wt = k.carve(P, 2, T, N)
    dpq = k.carve(P, 4, N)
    tt = k.carve(P, 3, N)
    cols = k.carve(P, 4, H, T)
    mx, pc, qc, as2 = (cols[:, i] for i in range(4))
    as_col, ad_col = asd[:, 0], asd[:, 1]
    ident = k.ident[0:P, 0:P].rearrange("p (o c) -> p o c", o=1).broadcast_to([P, T, P])
    diag, rows, agg, maxed = k.pool_step, k.filled, k.pe_step, k.logits_ready
    cols_ready, linear, top, expd, made, added = k.dve_ready, k.act_for_pe, k.emptied, k.act_ready, k.dve_for_pe, k.dve_step
    diag0, rows0, agg0, max0, cr0, lin0, top0, exp0, made0 = (c.n for c in (diag, rows, agg, maxed, cols_ready, linear, top, expd, made))
    NT = H * T
    head_done = []

    def score_slot(h, w):
        return k.ps[0:P, 2 * (h % 2) + w, :]

    def out_cols(h):
        return k.ps[0:P, 2 * (h % 2), 640:640 + T * (HD3 + 1)]

    with nc.Block() as block:
        @block.sync
        def _(sp):
            k.feed(sp, 0)

        @block.gpsimd
        def _(pool):
            def spread(dst, col):
                c = col.rearrange("p (t o) -> p t o", o=1).broadcast_to([P, T, P])
                diag.mark(pool.tensor_tensor(dst.rearrange("p (t c) -> p t c", t=T), ident, c, ALU.mult))
            for h in range(H):
                if h >= 2:
                    pool.wait_ge(rows.sem, rows0 + h - 1)
                spread(da[:, h % 2, :], as_col[:, h, :])
            pool.wait_ge(cols_ready.sem, cr0 + 1)
            for h in range(H):
                if h >= 2:
                    pool.wait_ge(rows.sem, rows0 + H + h - 1)
                spread(dpq[:, 2 * (h % 2), :], pc[:, h, :])
                spread(dpq[:, 2 * (h % 2) + 1, :], qc[:, h, :])

        @block.vector
        def _(dve):
            for h in range(H):
                dve.wait_ge(rows.sem, rows0 + h + 1)
                for j in range(T):
                    if h + j:
                        dve.wait_ge(added.sem, added.n)
                    ins = dve.tensor_tensor_reduce(junk, tiles(k.ps[0:P, h % 4, :]), k.neg[:, j, :].rearrange("p (t s) -> p t s", t=T),
                                                   1.0, 3 * NEG, ALU.add, ALU.max, mx[:, h, j:j + 1])
                    added.mark(ins)
                dve.wait_ge(added.sem, added.n)
                k.logits_ready.mark(dve.tensor_scalar(as2[:, h, :], as_col[:, h, :], SLOPE, None, ALU.mult))
            step(dve, added, dve.tensor_tensor(mx, mx, ad_col, ALU.add))
            step(dve, added, dve.scalar_tensor_tensor(mx, mx, SLOPE, mx, ALU.mult, ALU.max))
            added.mark(dve.tensor_tensor(pc, ad_col, mx, ALU.subtract))
            step(dve, added, dve.scalar_tensor_tensor(qc, ad_col, SLOPE, mx, ALU.mult, ALU.subtract))
            cols_ready.mark(dve.memset(junk[:, 0, 0:1], 0.0))

            def finish(h):
                dve.wait_ge(agg.sem, agg0 + h + 1)
                v = out_cols(h).rearrange("p (t f) -> p t f", f=HD3 + 1)
                rd = rden.rearrange("p (t o) -> p t o", o=1)
                step(dve, added, dve.tensor_scalar(rd, v[:, :, HD3:HD3 + 1], 1e-16, None, ALU.max))
                step(dve, added, dve.reciprocal(rden, rden))
                step(dve, added, dve.tensor_tensor(q, v[:, :, 0:HD3], rd.broadcast_to([P, T, HD3]), ALU.mult))
                head_done.append(added.n)
                step(dve, added, dve.tensor_tensor(q, q, res[:, :, h * HD3:(h + 1) * HD3], ALU.add))
                xt = k.x[:, :, h * HD3:(h + 1) * HD3]
                step(dve, added, dve.scalar_tensor_tensor(xt, q, 0.0, xt, ALU.max, ALU.add))
            for n in range(NT + 1):
                if n < NT:
                    h, i = n // T, n % T
                    dve.wait_ge(linear.sem, lin0 + n + 1)
                    v = tt[:, n % 3, :].rearrange("p (t c) -> p t c", t=T)
                    top.mark(dve.scalar_tensor_tensor(v, tiles(score_slot(h, 0)), as_col[:, h, i:i + 1], v, ALU.add, ALU.max))
                if n >= 1:
                    m = n - 1
                    h, i = m // T, m % T
                    dve.wait_ge(expd.sem, exp0 + m + 1)
                    if h >= 2 and i == 0:
                        dve.wait_ge(agg.sem, agg0 + h - 1)
                    made.mark(dve.scalar_tensor_tensor(wt[:, h % 2, i, :], tt[:, m % 3, :], 1.0, k.cT[:, i, :], ALU.min, ALU.mult))
                    if i == 1 and h >= 1:
                        finish(h - 1)
            finish(H - 1)

        @block.scalar
        def _(act):
            act.wait_ge(maxed.sem, max0 + H)
            for n in range(NT + 1):
                if n < NT:
                    h, i = n // T, n % T
                    if i == 0:
                        act.wait_ge(rows.sem, rows0 + H + h + 1)
                    if n >= 3:
                        act.wait_ge(made.sem, made0 + n - 2)
                    v = tt[:, n % 3, :].rearrange("p (t c) -> p t c", t=T)
                    linear.mark(act.activation(v, tiles(score_slot(h, 1)), ACT.Identity, bias=as2[:, h, i:i + 1]))
                if n >= 1:
                    m = n - 1
                    act.wait_ge(top.sem, top0 + m + 1)
                    expd.mark(act.activation(tt[:, m % 3, :], tt[:, m % 3, :], ACT.Exp))

        @block.tensor
        def _(pe):
            def spread_rows(out, d):
                for t in range(T):
                    last = pe.matmul(out[:, t * 128:t * 128 + P], k.ones[0:P, 0:P], d[:, t * P:(t + 1) * P], start=True, stop=True)
                return last

            def aggregate(h):
                pe.wait_ge(made.sem, made0 + (h + 1) * T)
                for j in range(T):
                    for i in range(T):
                        last = pe.matmul(out_cols(h)[:, j * (HD3 + 1):(j + 1) * (HD3 + 1)], wt[:, h % 2, i, j * P:(j + 1) * P], ft[:, i, h, :],
                                         start=i == 0, stop=i == T - 1)
                agg.mark(last)
            for h in range(H):
                pe.wait_ge(diag.sem, diag0 + h + 1)
                if h >= 4:
                    pe.wait_ge(maxed.sem, max0 + h - 3)
                rows.mark(spread_rows(k.ps[0:P, h % 4, :], da[:, h % 2, :]))
            pe.wait_ge(maxed.sem, max0 + H)
            for h in range(H):
                pe.wait_ge(diag.sem, diag0 + H + 2 * h + 2)
                if h >= 2:
                    pe.wait_ge(added.sem, head_done[h - 2])
                spread_rows(score_slot(h, 0), dpq[:, 2 * (h % 2), :])
                rows.mark(spread_rows(score_slot(h, 1), dpq[:, 2 * (h % 2) + 1, :]))
                if h >= 1:
                    aggregate(h - 1)
            aggregate(H - 1)


def ffn3(k, out):
    nc, a = k.nc, k.a
    norm_stage(k)
    k.reset()
    comb = k.carve(P, T, EXPERTS)
    keep = k.at
    route_stage(k, "L3_ffn_Wg", comb, None, 1)
    k.reset(keep)
    combT = k.carve(EXPERTS, N)
    diag = k.carve(P, 2, T * P)
    hid = k.carve(F3, EXPERTS, N)
    b1 = k.carve(F3, EXPERTS)
    b2 = k.carve(EXPERTS, D)
    f0, e0, p0, d0, a0, h0, r0, s0 = (k.filled.n, k.emptied.n, k.params_in.n, k.dve_for_pe.n, k.act_ready.n, k.pe_step.n,
                                      k.dve_ready.n, k.stored.n)
    ident = k.ident[0:P, 0:P].rearrange("p (o c) -> p o c", o=1).broadcast_to([P, T, P])
    with nc.Block() as block:
        @block.sync
        def _(sp):
            k.params_in.mark_dma(sp.dma_start(b1, a["L3_ffn_b1"]))
            k.params_in.mark_dma(sp.dma_start(b2, a["L3_ffn_b2"]))
            k.feed(sp, 3)
            rows = out.rearrange("(t p) d -> t p d", p=P)
            for t in range(T):
                sp.wait_ge(k.emptied.sem, e0 + t + 1)
                k.stored.mark_dma(sp.dma_start(rows[t], k.x[:, t, :]))
            sp.wait_ge(k.stored.sem, k.stored.n)

        marks_h = []

        @block.vector
        def _(dve):
            dve.wait_ge(k.filled.sem, f0 + 1)
            k.dve_step.mark(dve.tensor_copy(combT.rearrange("p (t c) -> p t c", t=T), tiles(k.ps[0:EXPERTS, 3, :])))
            for e in range(EXPERTS + 1):
                if e < EXPERTS:
                    if e >= 2:
                        dve.wait_ge(k.filled.sem, f0 + e)
                    k.dve_for_pe.mark(dve.tensor_tensor(diag[:, e % 2, :].rearrange("p (t c) -> p t c", t=T), ident,
                                                        comb[:, :, e:e + 1].broadcast_to([P, T, P]), ALU.mult))
                if e >= 1:
                    u = e - 1
                    dve.wait_ge(k.act_ready.sem, a0 + u + 1)
                    hv = hid[:, u, :].rearrange("p (t c) -> p t c", t=T)
                    marks_h.append(k.dve_step.mark(dve.tensor_tensor(hv, hv, tiles(k.ps[0:F3, 1, :]), ALU.mult)))
            for t in range(T):
                dve.wait_ge(k.filled.sem, f0 + 2 + EXPERTS + t)
                xt = k.x[:, t, :].rearrange("p (b f) -> p b f", b=2)
                k.emptied.mark(dve.tensor_tensor(xt, halves(k.ps[0:P, (2, 3, 0)[t % 3], :]), xt, ALU.add))
        @block.tensor
        def _(pe):
            for t in range(T):
                last = pe.transpose(k.ps[0:EXPERTS, 3, t * 128:t * 128 + P], comb[:, t, :], k.ident[0:P, 0:P])
            k.filled.mark(last)
            w1 = k.slab(pe).rearrange("p (c e f) -> p c e f", c=C, e=EXPERTS)
            for e in range(EXPERTS):
                if e >= 1:
                    pe.wait_ge(k.dve_step.sem, marks_h[e - 1])
                pe.wait_ge(k.dve_for_pe.sem, d0 + e + 1)
                for t in range(T):
                    pe.matmul(k.ps[0:F3, 1, t * 128:t * 128 + P], k.ones[0:P, 0:F3], diag[:, e % 2, t * P:(t + 1) * P], start=True, stop=True)
                k.filled.mark(feature_major(pe, k.ps[:, 0, :], F3, lambda c: w1[:, c, e, :], lambda c: k.xT[:, c, :], range(C)))
            w2 = [k.slab(pe, 1 + s).rearrange("p (c d) -> p c d", c=C) for s in range(2)]
            pe.wait_ge(k.dve_step.sem, marks_h[EXPERTS - 1])
            pe.wait_ge(k.params_in.sem, p0 + 32)
            for t in range(T):
                if t == 3:
                    pe.wait_ge(k.emptied.sem, e0 + 1)
                if t == 4:
                    pe.wait_ge(k.emptied.sem, e0 + 2)
                slot = (2, 3, 0)[t % 3]
                node_major(pe, k.ps[:, slot, :], lambda c: hid[:, c, t * P:(t + 1) * P], lambda c: w2[c // 4][0:F3, c % 4, :], range(EXPERTS), stop=False)
                k.filled.mark(node_major(pe, k.ps[:, slot, :], lambda c: combT[:, t * P:(t + 1) * P], lambda c: b2, range(1), start=False))
            release_slabs(k, pe, k.filled, 3)

        @block.scalar
        def _(act):
            act.wait_ge(k.params_in.sem, p0 + 32)
            for e in range(EXPERTS):
                act.wait_ge(k.filled.sem, f0 + 2 + e)
                k.act_ready.mark(act.activation(hid[:, e, :], k.ps[0:F3, 0, 0:N], ACT.Silu, bias=b1[:, e:e + 1]))



def network(nc, a, out):
    with ExitStack() as ctx:
        k = Kit(nc, ctx, a)
        plan_slabs(k)
        setup_stage(k)
        gat2(k)
        norm_stage(k)
        spline_stage(k)
        gat1(k)
        moe(k)
        gcn(k)
        loops_stage(k, -1.0)
        sign_ffn(k)
        gat3(k)
        ffn3(k, out)


def moe(k):
    norm_stage(k)
    k.reset()
    comb = k.carve(P, T, EXPERTS)
    rank = k.carve(P, T, EXPERTS)
    keep = k.at
    route_stage(k, "L1_ffn_w_router", comb, "L1_ffn_expert_bias", 2, rank)
    k.reset(keep)
    dispatch_stage(k, rank, comb, k.slot[:, :, :], k.weight[:, :, :], k.idx[:, :], k.need[:, :])
    k.reset()
    experts_stage(k, k.slot[:, :, :], k.weight[:, :, :], k.idx[:, :], k.need[:, :])


def layouts(np, x):
    def chunked(w):
        i, o = w.shape
        return np.ascontiguousarray(w.reshape(i // 128, 128, o).transpose(1, 0, 2).reshape(128, -1))

    def rows(v):
        return np.ascontiguousarray(np.broadcast_to(v.reshape(1, -1), (128, v.size)))

    def cols(v):
        return np.ascontiguousarray(v.reshape(-1, 128).T)

    def halved(w):
        h = w.shape[1] // 2
        return np.concatenate([chunked(w[:, :h]), chunked(w[:, h:])], axis=1)

    o = {"x": x["x"], "src": x["src"], "dst": x["dst"]}
    for n in ("L0_gnn_W1s", "L0_gnn_W1d", "L0_gnn_Wos", "L0_gnn_Wod", "L1_gnn_W2", "L2_gnn_W1", "L2_gnn_W2"):
        o[n] = chunked(x[n])
    for n in ("L0_gnn_b1s", "L0_gnn_b1d", "L0_gnn_attn1", "L0_gnn_ln1_w", "L0_gnn_ln1_b", "L0_gnn_bos", "L0_gnn_bod", "L0_gnn_attno",
              "L0_gnn_lno_w", "L0_gnn_lno_b", "L1_gnn_a1_src", "L1_gnn_a1_dst", "L1_gnn_a2_src", "L1_gnn_a2_dst", "L1_gnn_b2",
              "L1_ffn_expert_bias", "L2_gnn_b1", "L2_gnn_b2", "L3_gnn_attn_l", "L3_gnn_attn_r"):
        o[n] = rows(x[n])
    o["L1_gnn_b1"] = cols(x["L1_gnn_b1"])
    o["L0_ffn_w1"] = np.ascontiguousarray(x["L0_ffn_w1"].reshape(64, 6, 128, 16).transpose(2, 1, 3, 0).reshape(128, -1))
    o["L0_ffn_w2"] = np.ascontiguousarray(x["L0_ffn_w2"].reshape(768, 64, 8, 2).transpose(3, 1, 2, 0).reshape(128, -1))
    o["L1_gnn_W1"] = np.concatenate([chunked(x["L1_gnn_W1"][:, h * 512:(h + 1) * 512]) for h in range(4)], axis=1)

    def sixths(g, u, d):
        def half(w):
            return w.reshape(6, 256, 6, 128).transpose(0, 3, 2, 1)
        gu = np.concatenate([half(g), half(u)], axis=3).reshape(6, 128, -1)
        return np.concatenate([gu, d.T.reshape(6, 2, 128, 768).transpose(0, 2, 1, 3).reshape(6, 128, -1)], axis=2)

    o["L1_ffn_experts"] = np.stack([sixths(g, u, d) for g, u, d in zip(x["L1_ffn_Wg"], x["L1_ffn_Wu"], x["L1_ffn_Wd"])])
    o["L1_ffn_shared"] = sixths(x["L1_ffn_sg"], x["L1_ffn_su"], x["L1_ffn_sd"])
    o["L1_ffn_w_router"] = chunked(x["L1_ffn_w_router"].T)
    o["L2_ffn_weight"] = chunked(x["L2_ffn_weight"].T)
    o["L3_gnn_W"], o["L3_gnn_W_res"] = np.ascontiguousarray(x["L3_gnn_W"].T), np.ascontiguousarray(x["L3_gnn_W_res"].T)
    o["L3_ffn_Wg"] = chunked(x["L3_ffn_Wg"])
    o["L3_ffn_W1"] = chunked(x["L3_ffn_W1"].transpose(1, 0, 2).reshape(768, 768))
    o["L3_ffn_b1"] = np.ascontiguousarray(x["L3_ffn_b1"].T)
    o["L3_ffn_W2"] = np.ascontiguousarray(x["L3_ffn_W2"].transpose(1, 0, 2).reshape(96, -1))
    o["L3_ffn_b2"] = x["L3_ffn_b2"]
    return o




def kernel(**inputs):
    import numpy as _np
    import concourse.bacc as _bacc
    from concourse import mybir as _mybir
    from concourse.bass_utils import run_bass_kernel_spmd as _run

    nc = _bacc.Bacc("TRN2", target_bir_lowering=False, num_devices=1)
    arrays, aps = {}, {}
    for name, v in layouts(_np, {n: _np.asarray(v) for n, v in inputs.items()}).items():
        v = _np.ascontiguousarray(v)
        arrays[f"in_{name}"] = v
        aps[name] = nc.dram_tensor(f"in_{name}", v.shape, _mybir.dt.from_np(v.dtype), kind="ExternalInput").ap()
    out = nc.dram_tensor("out_0", (N, D), _mybir.dt.float32, kind="ExternalOutput").ap()
    network(nc, aps, out)
    r = _run(nc, [arrays], core_ids=[0])
    return r.results[0]["out_0"]
```
